# Optimizing a Trainium2 kernel written in Bass

```python
import numpy as np
import jax
import jax.numpy as jnp

def _softmax(x, axis=-1):
    return jax.nn.softmax(x, axis=axis)

def _gelu(x):
    return jax.nn.gelu(x, approximate=True)

def _silu(x):
    return jax.nn.silu(x)

def _sigmoid(x):
    return jax.nn.sigmoid(x)

def _layernorm(x, axis=-1, eps=1e-05):
    m = jnp.mean(x, axis=axis, keepdims=True)
    v = jnp.var(x, axis=axis, keepdims=True)
    return (x - m) / jnp.sqrt(v + eps)

def _scatter_add(tgt, idx, src, axis=0):
    return tgt.at[idx].add(src)

def _segment_sum(src, seg, n):
    return jax.ops.segment_sum(src, seg, n)
kernel_name = 'mk_gnn_ffn_d4_gnn_r8_cfb5a0'

def setup_inputs(seed: int=0):
    np.random.seed(seed)
    _w = jnp.asarray

    def _rec_inputs():
        import jax
        import jax.numpy as jnp
        _gk = jax.random.key(seed)
        x = -7.329e-05 + 0.9999 * jax.random.normal(jax.random.fold_in(_gk, 1), (1250, 512), jnp.float32)
        src = jax.random.randint(jax.random.fold_in(_gk, 2), (20000,), 0, 1250, jnp.int32)
        dst = jax.random.randint(jax.random.fold_in(_gk, 3), (20000,), 0, 1250, jnp.int32)
        _o = jnp.argsort(dst, stable=True)
        src = src[_o]
        dst = dst[_o]
        edge_attr_8 = 0.0012443 + 1.0001 * jax.random.normal(jax.random.fold_in(_gk, 12), (20000, 8), jnp.float32)
        return (x, src, dst, edge_attr_8)
    x, src, dst, edge_attr_8 = _rec_inputs()

    def _L0_gnn_setup():
        import jax, jax.numpy as jnp
        import numpy as np
        N = 12500
        IN_C = 512
        HID = 128
        OUT_C = 512
        E = 400000

        def _gcn_conv(x, W, b, src, dst, n):
            h = x @ W
            loop = jnp.arange(n, dtype=src.dtype)
            src2 = jnp.concatenate([src, loop])
            dst2 = jnp.concatenate([dst, loop])
            deg = jax.ops.segment_sum(jnp.ones_like(dst2, dtype=h.dtype), dst2, num_segments=n)
            dinv = jnp.where(deg > 0, jax.lax.rsqrt(deg), 0.0)
            norm = dinv[src2] * dinv[dst2]
            msgs = h[src2] * norm[:, None]
            out = jax.ops.segment_sum(msgs, dst2, num_segments=n)
            return out + b
        key = jax.random.key(seed)
        k1, k2, k3, k4 = jax.random.split(key, 4)
        z = jax.random.normal(k1, (N, IN_C), dtype=jnp.float32)
        edge_index = jax.random.randint(k2, (2, E), 0, N, dtype=jnp.int64)
        W1 = jax.random.normal(k3, (IN_C, HID), dtype=jnp.float32) * (1.0 / np.sqrt(IN_C))
        b1 = jnp.zeros((HID,), dtype=jnp.float32)
        W2 = jax.random.normal(k4, (HID, OUT_C), dtype=jnp.float32) * (1.0 / np.sqrt(HID))
        b2 = jnp.zeros((OUT_C,), dtype=jnp.float32)
        return {'z': z, 'edge_index': edge_index, 'W1': W1, 'b1': b1, 'W2': W2, 'b2': b2}
    _L0_gnn_all = _L0_gnn_setup()
    _L0_gnn_in = {k: v for k, v in _L0_gnn_all.items() if k in ('W1', 'b1', 'W2', 'b2')}
    del _L0_gnn_all

    def _L0_ffn_setup():
        import jax, jax.numpy as jnp
        import numpy as np
        D_MODEL = 512
        D_FF = 256
        N_EXPERTS = 8
        TOP_K = 2
        key = jax.random.key(seed)
        ks = jax.random.split(key, 6)
        x = jax.random.normal(ks[0], (4, 1024, D_MODEL), dtype=jnp.float32)
        router_w = jax.random.normal(ks[1], (N_EXPERTS, D_MODEL), dtype=jnp.float32) * 0.02
        lim1 = float(np.sqrt(6.0 / (D_FF + D_MODEL)))
        w1 = jax.random.uniform(ks[2], (N_EXPERTS, D_FF, D_MODEL), minval=-lim1, maxval=lim1, dtype=jnp.float32)
        b1 = jnp.zeros((N_EXPERTS, D_FF), dtype=jnp.float32)
        lim2 = float(np.sqrt(6.0 / (D_MODEL + D_FF)))
        w2 = jax.random.uniform(ks[3], (N_EXPERTS, D_MODEL, D_FF), minval=-lim2, maxval=lim2, dtype=jnp.float32)
        b2 = jnp.zeros((N_EXPERTS, D_MODEL), dtype=jnp.float32)
        return {'x': x, 'router_w': router_w, 'w1': w1, 'b1': b1, 'w2': w2, 'b2': b2}
    _L0_ffn_all = _L0_ffn_setup()
    _L0_ffn_in = {k: v for k, v in _L0_ffn_all.items() if k in ('router_w', 'w1', 'b1', 'w2', 'b2')}
    del _L0_ffn_all

    def _L1_gnn_setup():
        import jax, jax.numpy as jnp
        import numpy as np
        N = 2500
        E = 40000
        D = 512
        H = 8
        DK = D // H
        key = jax.random.key(seed)
        ks = jax.random.split(key, 12)
        x = jax.random.normal(ks[0], (N, D), jnp.float32)
        rows = jnp.sort(jax.random.randint(ks[1], (E,), 0, N))
        cols = jax.random.randint(ks[2], (E,), 0, N)
        edge_index = jnp.stack([rows, cols]).astype(jnp.int32)
        att_bias = jax.random.normal(ks[3], (E, H), jnp.float32)
        s = float(1.0 / np.sqrt(D))
        Wq = jax.random.normal(ks[4], (D, D), jnp.float32) * s
        Wk = jax.random.normal(ks[5], (D, D), jnp.float32) * s
        Wv = jax.random.normal(ks[6], (D, D), jnp.float32) * s
        Wo = jax.random.normal(ks[7], (D, D), jnp.float32) * s
        bq = jnp.zeros((D,), jnp.float32)
        bk = jnp.zeros((D,), jnp.float32)
        bv = jnp.zeros((D,), jnp.float32)
        bo = jnp.zeros((D,), jnp.float32)
        return dict(x=x, edge_index=edge_index, att_bias=att_bias, Wq=Wq, bq=bq, Wk=Wk, bk=bk, Wv=Wv, bv=bv, Wo=Wo, bo=bo)
    _L1_gnn_all = _L1_gnn_setup()
    _L1_gnn_in = {k: v for k, v in _L1_gnn_all.items() if k in ('Wq', 'bq', 'Wk', 'bk', 'Wv', 'bv', 'Wo', 'bo')}
    del _L1_gnn_all

    def _L1_ffn_setup():
        import jax, jax.numpy as jnp
        import numpy as np
        D, NH, HID, E = (512, 8, 256, 8)
        EPS = 1e-05

        def _layernorm(x, g, b):
            mu = jnp.mean(x, axis=-1, keepdims=True)
            var = jnp.mean(jnp.square(x - mu), axis=-1, keepdims=True)
            return (x - mu) * jax.lax.rsqrt(var + EPS) * g + b
        key = jax.random.key(seed)
        ks = jax.random.split(key, 20)
        s = 0.02
        inp = {'x': jax.random.normal(ks[0], (4, 1024, D), jnp.float32), 'Wq': jax.random.normal(ks[1], (D, D), jnp.float32) * s, 'bq': jnp.zeros((D,), jnp.float32), 'Wk': jax.random.normal(ks[2], (D, D), jnp.float32) * s, 'bk': jnp.zeros((D,), jnp.float32), 'Wv': jax.random.normal(ks[3], (D, D), jnp.float32) * s, 'bv': jnp.zeros((D,), jnp.float32), 'Wo': jax.random.normal(ks[4], (D, D), jnp.float32) * s, 'bo': jnp.zeros((D,), jnp.float32), 'g1': jnp.ones((D,), jnp.float32), 'beta1': jnp.zeros((D,), jnp.float32), 'g2': jnp.ones((D,), jnp.float32), 'beta2': jnp.zeros((D,), jnp.float32), 'Wg': jax.random.normal(ks[5], (D, E), jnp.float32) * s, 'bg': jnp.zeros((E,), jnp.float32), 'W1': jax.random.normal(ks[6], (E, D, HID), jnp.float32) * s, 'b1': jnp.zeros((E, HID), jnp.float32), 'W2': jax.random.normal(ks[7], (E, HID, D), jnp.float32) * s, 'b2': jnp.zeros((E, D), jnp.float32)}
        return inp
    _L1_ffn_all = _L1_ffn_setup()
    _L1_ffn_in = {k: v for k, v in _L1_ffn_all.items() if k in ('Wq', 'bq', 'Wk', 'bk', 'Wv', 'bv', 'Wo', 'bo', 'g1', 'beta1', 'g2', 'beta2', 'Wg', 'bg', 'W1', 'b1', 'W2', 'b2')}
    del _L1_ffn_all

    def _L2_gnn_setup():
        import jax, jax.numpy as jnp
        import numpy as np
        N_NODES = 1250
        N_EDGES = 20000
        D_IN = 512
        D_OUT = 512
        key = jax.random.key(seed)
        k1, k2, k3, k4, k5 = jax.random.split(key, 5)
        feature = jax.random.normal(k1, (N_NODES, D_IN), dtype=jnp.float32)
        src = jax.random.randint(k2, (N_EDGES,), 0, N_NODES, dtype=jnp.int64)
        dst = jax.random.randint(k3, (N_EDGES,), 0, N_NODES, dtype=jnp.int64)
        W = jax.random.normal(k4, (2 * D_IN, D_OUT), dtype=jnp.float32) * (1.0 / np.sqrt(2 * D_IN))
        b = jax.random.normal(k5, (D_OUT,), dtype=jnp.float32) * 0.01
        return {'feature': feature, 'src': src, 'dst': dst, 'W': W, 'b': b}
    _L2_gnn_all = _L2_gnn_setup()
    _L2_gnn_in = {k: v for k, v in _L2_gnn_all.items() if k in ('W', 'b')}
    del _L2_gnn_all

    def _L2_ffn_setup():
        import jax, jax.numpy as jnp
        import numpy as np

        def _haar_dwt2(x):
            a = x[:, ::2, ::2]
            b = x[:, ::2, 1::2]
            c = x[:, 1::2, ::2]
            d = x[:, 1::2, 1::2]
            ll = (a + b + c + d) * 0.5
            lh = (a + b - c - d) * 0.5
            hl = (a - b + c - d) * 0.5
            hh = (a - b - c + d) * 0.5
            return (ll, lh, hl, hh)

        def _haar_idwt2(ll, lh, hl, hh):
            a = (ll + lh + hl + hh) * 0.5
            b = (ll + lh - hl - hh) * 0.5
            c = (ll - lh + hl - hh) * 0.5
            d = (ll - lh - hl + hh) * 0.5
            B, H2, W2 = ll.shape
            out = jnp.zeros((B, 2 * H2, 2 * W2), ll.dtype)
            out = out.at[:, ::2, ::2].set(a)
            out = out.at[:, ::2, 1::2].set(b)
            out = out.at[:, 1::2, ::2].set(c)
            out = out.at[:, 1::2, 1::2].set(d)
            return out

        def _interp_linear_last(x, m):
            n = x.shape[-1]
            pos = jnp.linspace(0.0, 1.0, m, dtype=x.dtype) * (n - 1)
            i0 = jnp.clip(jnp.floor(pos).astype(jnp.int32), 0, n - 2)
            w = pos - i0.astype(x.dtype)
            return x[..., i0] * (1.0 - w) + x[..., i0 + 1] * w
        key = jax.random.key(seed)
        k0, k1, k2 = jax.random.split(key, 3)
        b, f, c, hidden = (128, 256, 512, 256)
        x = jax.random.normal(k0, (b, f, c), dtype=jnp.float32)
        fc1_w = jax.random.normal(k1, (hidden, c), dtype=jnp.float32) * 0.02
        fc1_b = jnp.zeros((hidden,), dtype=jnp.float32)
        fc2_w = jax.random.normal(k2, (c // 2, hidden), dtype=jnp.float32) * 0.02
        fc2_b = jnp.zeros((c // 2,), dtype=jnp.float32)
        return {'x': x, 'fc1_w': fc1_w, 'fc1_b': fc1_b, 'fc2_w': fc2_w, 'fc2_b': fc2_b}
    _L2_ffn_all = _L2_ffn_setup()
    _L2_ffn_in = {k: v for k, v in _L2_ffn_all.items() if k in ('fc1_w', 'fc1_b', 'fc2_w', 'fc2_b')}
    del _L2_ffn_all

    def _L3_gnn_setup():
        import jax, jax.numpy as jnp
        import numpy as np
        N_NODES = 6250
        N_EDGES = 18750
        D_IN = 512
        D_OUT = 512
        LN_EPS = 1e-05
        key = jax.random.key(seed)
        k_x, k_e, k_ws, k_wn = jax.random.split(key, 4)
        x = jax.random.normal(k_x, (N_NODES, D_IN), dtype=jnp.float32)
        edge_index = jax.random.randint(k_e, (2, N_EDGES), 0, N_NODES, dtype=jnp.int64)
        scale = 1.0 / np.sqrt(D_IN)
        w_self = jax.random.normal(k_ws, (D_OUT, D_IN), dtype=jnp.float32) * scale
        w_neigh = jax.random.normal(k_wn, (D_OUT, D_IN), dtype=jnp.float32) * scale
        bias = jnp.zeros((D_OUT,), dtype=jnp.float32)
        gamma = jnp.ones((D_OUT,), dtype=jnp.float32)
        beta = jnp.zeros((D_OUT,), dtype=jnp.float32)
        return {'x': x, 'edge_index': edge_index, 'w_self': w_self, 'w_neigh': w_neigh, 'bias': bias, 'gamma': gamma, 'beta': beta}
    _L3_gnn_all = _L3_gnn_setup()
    _L3_gnn_in = {k: v for k, v in _L3_gnn_all.items() if k in ('w_self', 'w_neigh', 'bias', 'gamma', 'beta')}
    del _L3_gnn_all

    def _L3_ffn_setup():
        import jax, jax.numpy as jnp
        import numpy as np
        B, S, D = (8, 256, 512)
        FF = 256
        E = 8
        key = jax.random.key(seed)
        ks = jax.random.split(key, 7)
        s = 1.0 / np.sqrt(D)
        sf = 1.0 / np.sqrt(FF)
        return {'x': jax.random.normal(ks[0], (B, S, D), dtype=jnp.float32), 'Wg': jax.random.uniform(ks[1], (D, E), jnp.float32, -s, s), 'bg': jax.random.uniform(ks[2], (E,), jnp.float32, -s, s), 'W1': jax.random.uniform(ks[3], (E, D, FF), jnp.float32, -s, s), 'b1': jax.random.uniform(ks[4], (E, FF), jnp.float32, -s, s), 'W2': jax.random.uniform(ks[5], (E, FF, D), jnp.float32, -sf, sf), 'b2': jax.random.uniform(ks[6], (E, D), jnp.float32, -sf, sf)}
    _L3_ffn_all = _L3_ffn_setup()
    _L3_ffn_in = {k: v for k, v in _L3_ffn_all.items() if k in ('Wg', 'bg', 'W1', 'b1', 'W2', 'b2')}
    del _L3_ffn_all
    return {'x': x, 'src': src, 'dst': dst, 'edge_attr_8': edge_attr_8, 'L0_gnn_W1': _L0_gnn_in['W1'], 'L0_gnn_b1': _L0_gnn_in['b1'], 'L0_gnn_W2': _L0_gnn_in['W2'], 'L0_gnn_b2': _L0_gnn_in['b2'], 'L0_ffn_router_w': _L0_ffn_in['router_w'], 'L0_ffn_w1': _L0_ffn_in['w1'], 'L0_ffn_b1': _L0_ffn_in['b1'], 'L0_ffn_w2': _L0_ffn_in['w2'], 'L0_ffn_b2': _L0_ffn_in['b2'], 'L1_gnn_Wq': _L1_gnn_in['Wq'], 'L1_gnn_bq': _L1_gnn_in['bq'], 'L1_gnn_Wk': _L1_gnn_in['Wk'], 'L1_gnn_bk': _L1_gnn_in['bk'], 'L1_gnn_Wv': _L1_gnn_in['Wv'], 'L1_gnn_bv': _L1_gnn_in['bv'], 'L1_gnn_Wo': _L1_gnn_in['Wo'], 'L1_gnn_bo': _L1_gnn_in['bo'], 'L1_ffn_Wq': _L1_ffn_in['Wq'], 'L1_ffn_bq': _L1_ffn_in['bq'], 'L1_ffn_Wk': _L1_ffn_in['Wk'], 'L1_ffn_bk': _L1_ffn_in['bk'], 'L1_ffn_Wv': _L1_ffn_in['Wv'], 'L1_ffn_bv': _L1_ffn_in['bv'], 'L1_ffn_Wo': _L1_ffn_in['Wo'], 'L1_ffn_bo': _L1_ffn_in['bo'], 'L1_ffn_g1': _L1_ffn_in['g1'], 'L1_ffn_beta1': _L1_ffn_in['beta1'], 'L1_ffn_g2': _L1_ffn_in['g2'], 'L1_ffn_beta2': _L1_ffn_in['beta2'], 'L1_ffn_Wg': _L1_ffn_in['Wg'], 'L1_ffn_bg': _L1_ffn_in['bg'], 'L1_ffn_W1': _L1_ffn_in['W1'], 'L1_ffn_b1': _L1_ffn_in['b1'], 'L1_ffn_W2': _L1_ffn_in['W2'], 'L1_ffn_b2': _L1_ffn_in['b2'], 'L2_gnn_W': _L2_gnn_in['W'], 'L2_gnn_b': _L2_gnn_in['b'], 'L2_ffn_fc1_w': _L2_ffn_in['fc1_w'], 'L2_ffn_fc1_b': _L2_ffn_in['fc1_b'], 'L2_ffn_fc2_w': _L2_ffn_in['fc2_w'], 'L2_ffn_fc2_b': _L2_ffn_in['fc2_b'], 'L3_gnn_w_self': _L3_gnn_in['w_self'], 'L3_gnn_w_neigh': _L3_gnn_in['w_neigh'], 'L3_gnn_bias': _L3_gnn_in['bias'], 'L3_gnn_gamma': _L3_gnn_in['gamma'], 'L3_gnn_beta': _L3_gnn_in['beta'], 'L3_ffn_Wg': _L3_ffn_in['Wg'], 'L3_ffn_bg': _L3_ffn_in['bg'], 'L3_ffn_W1': _L3_ffn_in['W1'], 'L3_ffn_b1': _L3_ffn_in['b1'], 'L3_ffn_W2': _L3_ffn_in['W2'], 'L3_ffn_b2': _L3_ffn_in['b2']}

def reference(x, src, dst, edge_attr_8, L0_gnn_W1, L0_gnn_b1, L0_gnn_W2, L0_gnn_b2, L0_ffn_router_w, L0_ffn_w1, L0_ffn_b1, L0_ffn_w2, L0_ffn_b2, L1_gnn_Wq, L1_gnn_bq, L1_gnn_Wk, L1_gnn_bk, L1_gnn_Wv, L1_gnn_bv, L1_gnn_Wo, L1_gnn_bo, L1_ffn_Wq, L1_ffn_bq, L1_ffn_Wk, L1_ffn_bk, L1_ffn_Wv, L1_ffn_bv, L1_ffn_Wo, L1_ffn_bo, L1_ffn_g1, L1_ffn_beta1, L1_ffn_g2, L1_ffn_beta2, L1_ffn_Wg, L1_ffn_bg, L1_ffn_W1, L1_ffn_b1, L1_ffn_W2, L1_ffn_b2, L2_gnn_W, L2_gnn_b, L2_ffn_fc1_w, L2_ffn_fc1_b, L2_ffn_fc2_w, L2_ffn_fc2_b, L3_gnn_w_self, L3_gnn_w_neigh, L3_gnn_bias, L3_gnn_gamma, L3_gnn_beta, L3_ffn_Wg, L3_ffn_bg, L3_ffn_W1, L3_ffn_b1, L3_ffn_W2, L3_ffn_b2):
    import jax
    import jax.numpy as jnp

    def _L0_gnn_ref(z, edge_index, W1, b1, W2, b2):
        import jax, jax.numpy as jnp
        import numpy as np
        N = 12500
        IN_C = 512
        HID = 128
        OUT_C = 512
        E = 400000

        def _gcn_conv(x, W, b, src, dst, n):
            h = x @ W
            loop = jnp.arange(n, dtype=src.dtype)
            src2 = jnp.concatenate([src, loop])
            dst2 = jnp.concatenate([dst, loop])
            deg = jax.ops.segment_sum(jnp.ones_like(dst2, dtype=h.dtype), dst2, num_segments=n)
            dinv = jnp.where(deg > 0, jax.lax.rsqrt(deg), 0.0)
            norm = dinv[src2] * dinv[dst2]
            msgs = h[src2] * norm[:, None]
            out = jax.ops.segment_sum(msgs, dst2, num_segments=n)
            return out + b
        src, dst = (edge_index[0], edge_index[1])
        h = jax.nn.relu(_gcn_conv(z, W1, b1, src, dst, z.shape[0]))
        out = _gcn_conv(h, W2, b2, src, dst, z.shape[0])
        return out

    def _L0_ffn_ref(x, router_w, w1, b1, w2, b2):
        import jax, jax.numpy as jnp
        import numpy as np
        D_MODEL = 512
        D_FF = 256
        N_EXPERTS = 8
        TOP_K = 2
        router_logits = jnp.einsum('bnc,ec->bne', x, router_w)
        router_probs = jax.nn.softmax(router_logits, axis=-1)
        expert_weights, expert_indices = jax.lax.top_k(router_probs, TOP_K)
        expert_weights = expert_weights / (jnp.sum(expert_weights, axis=-1, keepdims=True) + 1e-09)
        hidden = jnp.einsum('bnc,edc->bned', x, w1) + b1
        hidden = jax.nn.gelu(hidden, approximate=False)
        expert_outputs = jnp.einsum('bned,ecd->bnec', hidden, w2) + b2
        idx = expert_indices[..., None]
        selected = jnp.take_along_axis(expert_outputs, idx, axis=2)
        output = jnp.sum(selected * expert_weights[..., None], axis=2)
        return output

    def _L1_gnn_ref(x, edge_index, att_bias, Wq, bq, Wk, bk, Wv, bv, Wo, bo):
        import jax, jax.numpy as jnp
        import numpy as np
        N = 2500
        E = 40000
        D = 512
        H = 8
        DK = D // H
        n = x.shape[0]
        rows, cols = (edge_index[0], edge_index[1])
        q = (x @ Wq + bq).reshape(n, H, DK)
        k = (x @ Wk + bk).reshape(n, H, DK)
        v = (x @ Wv + bv).reshape(n, H, DK)
        scale = 1.0 / jnp.sqrt(jnp.asarray(DK, x.dtype))
        logits = jnp.einsum('ehd,ehd->eh', q[rows] * scale, k[cols]) + att_bias
        row_max = jax.ops.segment_max(logits, rows, num_segments=n)
        p = jnp.exp(logits - row_max[rows])
        denom = jax.ops.segment_sum(p, rows, num_segments=n)
        att = p / denom[rows]
        y = jax.ops.segment_sum(att[:, :, None] * v[cols], rows, num_segments=n)
        out = y.reshape(n, H * DK) @ Wo + bo
        return out

    def _L1_ffn_ref(x, Wq, bq, Wk, bk, Wv, bv, Wo, bo, g1, beta1, g2, beta2, Wg, bg, W1, b1, W2, b2):
        import jax, jax.numpy as jnp
        import numpy as np
        D, NH, HID, E = (512, 8, 256, 8)
        EPS = 1e-05

        def _layernorm(x, g, b):
            mu = jnp.mean(x, axis=-1, keepdims=True)
            var = jnp.mean(jnp.square(x - mu), axis=-1, keepdims=True)
            return (x - mu) * jax.lax.rsqrt(var + EPS) * g + b
        B, S, _ = x.shape
        dh = D // NH
        q = (x @ Wq + bq).reshape(B, S, NH, dh)
        k = (x @ Wk + bk).reshape(B, S, NH, dh)
        v = (x @ Wv + bv).reshape(B, S, NH, dh)
        scores = jnp.einsum('bqhd,bkhd->bhqk', q, k) / jnp.sqrt(jnp.float32(dh)).astype(x.dtype)
        attn = jax.nn.softmax(scores, axis=-1)
        ctx = jnp.einsum('bhqk,bkhd->bqhd', attn, v).reshape(B, S, D)
        sa = ctx @ Wo + bo
        x = _layernorm(x + sa, g1, beta1)
        t = x.reshape(-1, D)
        logits = t @ Wg + bg
        idx = jnp.argmax(logits, axis=-1)
        h = jax.nn.gelu(jnp.einsum('td,edh->teh', t, W1) + b1, approximate=False)
        y = jnp.einsum('teh,ehd->ted', h, W2) + b2
        onehot = jax.nn.one_hot(idx, E, dtype=t.dtype)
        moe = jnp.einsum('ted,te->td', y, onehot).reshape(B, S, D)
        return _layernorm(x + moe, g2, beta2)

    def _L2_gnn_ref(feature, src, dst, W, b):
        import jax, jax.numpy as jnp
        import numpy as np
        N_NODES = 1250
        N_EDGES = 20000
        D_IN = 512
        D_OUT = 512
        n = feature.shape[0]
        neigh = jax.ops.segment_sum(feature[src], dst, num_segments=n)
        degs = jax.ops.segment_sum(jnp.ones_like(dst, dtype=feature.dtype), dst, num_segments=n)
        hk_neigh = neigh / jnp.maximum(degs, 1.0)[:, None]
        hk = jnp.concatenate([feature, hk_neigh], axis=-1) @ W + b
        return jax.nn.relu(hk)

    def _L2_ffn_ref(x, fc1_w, fc1_b, fc2_w, fc2_b):
        import jax, jax.numpy as jnp
        import numpy as np

        def _haar_dwt2(x):
            a = x[:, ::2, ::2]
            b = x[:, ::2, 1::2]
            c = x[:, 1::2, ::2]
            d = x[:, 1::2, 1::2]
            ll = (a + b + c + d) * 0.5
            lh = (a + b - c - d) * 0.5
            hl = (a - b + c - d) * 0.5
            hh = (a - b - c + d) * 0.5
            return (ll, lh, hl, hh)

        def _haar_idwt2(ll, lh, hl, hh):
            a = (ll + lh + hl + hh) * 0.5
            b = (ll + lh - hl - hh) * 0.5
            c = (ll - lh + hl - hh) * 0.5
            d = (ll - lh - hl + hh) * 0.5
            B, H2, W2 = ll.shape
            out = jnp.zeros((B, 2 * H2, 2 * W2), ll.dtype)
            out = out.at[:, ::2, ::2].set(a)
            out = out.at[:, ::2, 1::2].set(b)
            out = out.at[:, 1::2, ::2].set(c)
            out = out.at[:, 1::2, 1::2].set(d)
            return out

        def _interp_linear_last(x, m):
            n = x.shape[-1]
            pos = jnp.linspace(0.0, 1.0, m, dtype=x.dtype) * (n - 1)
            i0 = jnp.clip(jnp.floor(pos).astype(jnp.int32), 0, n - 2)
            w = pos - i0.astype(x.dtype)
            return x[..., i0] * (1.0 - w) + x[..., i0 + 1] * w
        b, f, c = x.shape
        ll, lh, hl, hh = _haar_dwt2(x)
        ll_up = _interp_linear_last(ll, c)
        h = jax.nn.gelu(jnp.einsum('bfc,hc->bfh', ll_up, fc1_w) + fc1_b, approximate=False)
        ll_new = jnp.einsum('bfh,oh->bfo', h, fc2_w) + fc2_b
        return _haar_idwt2(ll_new, lh, hl, hh)

    def _L3_gnn_ref(x, edge_index, w_self, w_neigh, bias, gamma, beta):
        import jax, jax.numpy as jnp
        import numpy as np
        N_NODES = 6250
        N_EDGES = 18750
        D_IN = 512
        D_OUT = 512
        LN_EPS = 1e-05
        n = x.shape[0]
        s, d = (edge_index[0], edge_index[1])
        agg = jax.ops.segment_sum(x[s], d, num_segments=n)
        cnt = jax.ops.segment_sum(jnp.ones(s.shape[0], x.dtype), d, num_segments=n)
        agg = agg / jnp.maximum(cnt, 1.0)[:, None]
        h = x @ w_self.T + agg @ w_neigh.T + bias
        mu = jnp.mean(h, axis=-1, keepdims=True)
        var = jnp.mean(jnp.square(h - mu), axis=-1, keepdims=True)
        hn = (h - mu) * jax.lax.rsqrt(var + LN_EPS) * gamma + beta
        return jax.nn.relu(hn)

    def _L3_ffn_ref(x, Wg, bg, W1, b1, W2, b2):
        import jax, jax.numpy as jnp
        import numpy as np
        B, S, D = (8, 256, 512)
        FF = 256
        E = 8
        b, s, d = x.shape
        xf = x.reshape(-1, d)
        logits = xf @ Wg + bg
        probs = jax.nn.softmax(logits, axis=-1)
        pmax = jnp.max(probs, axis=-1)
        routes = jnp.argmax(probs, axis=-1)
        xs = xf * pmax[:, None]
        out_tok = jnp.zeros_like(xf)
        for e in range(E):
            h = jax.nn.relu(xs @ W1[e] + b1[e])
            y = h @ W2[e] + b2[e]
            out_tok = jnp.where((routes == e)[:, None], y, out_tok)
        order = jnp.argsort(routes)
        return out_tok[order].reshape(b, s, d)
    edge_index = jnp.stack([src, dst])
    x = x + _L0_gnn_ref(_layernorm(x, axis=-1), edge_index, L0_gnn_W1, L0_gnn_b1, L0_gnn_W2, L0_gnn_b2)
    x = x + _L0_ffn_ref(_layernorm(x, axis=-1)[None], L0_ffn_router_w, L0_ffn_w1, L0_ffn_b1, L0_ffn_w2, L0_ffn_b2)[0]
    x = x + _L1_gnn_ref(_layernorm(x, axis=-1), edge_index, edge_attr_8, L1_gnn_Wq, L1_gnn_bq, L1_gnn_Wk, L1_gnn_bk, L1_gnn_Wv, L1_gnn_bv, L1_gnn_Wo, L1_gnn_bo)
    x = x + _L1_ffn_ref(_layernorm(x, axis=-1)[None], L1_ffn_Wq, L1_ffn_bq, L1_ffn_Wk, L1_ffn_bk, L1_ffn_Wv, L1_ffn_bv, L1_ffn_Wo, L1_ffn_bo, L1_ffn_g1, L1_ffn_beta1, L1_ffn_g2, L1_ffn_beta2, L1_ffn_Wg, L1_ffn_bg, L1_ffn_W1, L1_ffn_b1, L1_ffn_W2, L1_ffn_b2)[0]
    x = x + _L2_gnn_ref(_layernorm(x, axis=-1), src, dst, L2_gnn_W, L2_gnn_b)
    x = x + _L2_ffn_ref(_layernorm(x, axis=-1)[None], L2_ffn_fc1_w, L2_ffn_fc1_b, L2_ffn_fc2_w, L2_ffn_fc2_b)[0]
    x = x + _L3_gnn_ref(_layernorm(x, axis=-1), edge_index, L3_gnn_w_self, L3_gnn_w_neigh, L3_gnn_bias, L3_gnn_gamma, L3_gnn_beta)
    x = x + _L3_ffn_ref(_layernorm(x, axis=-1)[None], L3_ffn_Wg, L3_ffn_bg, L3_ffn_W1, L3_ffn_b1, L3_ffn_W2, L3_ffn_b2)[0]
    return x

_drawn_inputs = setup_inputs


def setup_inputs(seed=0):
    import zlib

    import numpy as np

    out = dict(_drawn_inputs(seed))
    spreads = {'L0_gnn_b1': (0.0, 0.1),
     'L0_gnn_b2': (0.0, 0.1),
     'L0_ffn_b1': (0.0, 0.1),
     'L0_ffn_b2': (0.0, 0.1),
     'L1_gnn_bq': (0.0, 0.1),
     'L1_gnn_bk': (0.0, 0.8),
     'L1_gnn_bv': (0.0, 0.1),
     'L1_gnn_bo': (0.0, 0.1),
     'L1_ffn_bq': (0.0, 0.8),
     'L1_ffn_bk': (0.0, 0.8),
     'L1_ffn_bv': (0.0, 0.1),
     'L1_ffn_bo': (0.0, 0.1),
     'L1_ffn_g1': (1.0, 0.2),
     'L1_ffn_beta1': (0.0, 0.1),
     'L1_ffn_g2': (1.0, 0.2),
     'L1_ffn_beta2': (0.0, 0.1),
     'L1_ffn_bg': (0.0, 0.1),
     'L1_ffn_b1': (0.0, 0.405),
     'L1_ffn_b2': (0.0, 0.1),
     'L2_ffn_fc1_b': (0.0, 0.4),
     'L2_ffn_fc2_b': (0.0, 0.296),
     'L3_gnn_bias': (0.0, 0.1),
     'L3_gnn_gamma': (1.0, 0.2),
     'L3_gnn_beta': (0.0, 0.1)}
    factors = {'L1_ffn_Wq': 4.058,
     'L1_ffn_Wk': 4.056,
     'L2_gnn_b': 4.336,
     'L2_ffn_fc1_w': 3.002,
     'L2_ffn_fc2_w': 2.814,
     'L3_ffn_Wg': 3.083,
     'L3_ffn_bg': 3.396,
     'L3_ffn_W1': 3.509,
     'L3_ffn_b1': 8.0,
     'L3_ffn_W2': 2.803,
     'L3_ffn_b2': 4.926}
    for name, (base, spread) in spreads.items():
        noise = np.random.default_rng([zlib.crc32(name.encode()), seed]).standard_normal(out[name].shape)
        drawn = base * np.exp(spread * noise) if base else spread * noise
        out[name] = jnp.asarray(drawn.astype(out[name].dtype))
    for name, factor in factors.items():
        out[name] = (out[name] * factor).astype(out[name].dtype)
    return out
```

```python
from contextlib import ExitStack

import concourse.bass as bass
from concourse import mybir

F32 = mybir.dt.float32
BF16 = mybir.dt.bfloat16
I32 = mybir.dt.int32
ALU = mybir.AluOpType
ACT = mybir.ActivationFunctionType
X = mybir.AxisListType.X

N, D = 1250, 512
P = 125
T = N // P
K = D // 128
E = 20000
EC = E // P
S = 128
SC = (E + T * (S - 1)) // S + 1
MAGIC = 1.5 * 2.0 ** 23
NULL_ROW = S * SC
RW = 10
H, DH = 8, 64
NX = 8
FF = 256
NEG = -1.0e30
COLS = [(0, 500), (500, 500), (1000, 250)]
B = 4
LAST = 99


def build(nc, a, out, last=LAST):
    ctx = ExitStack()
    names = iter(range(10000))
    sems, cleared_sems = [], []

    def sb(name, shape, dt=F32, c=None):
        return (c or ctx).enter_context(nc.sbuf_tensor(f"{name}_{next(names)}", shape, dt))

    def dma_sem(name):
        return nc.alloc_semaphore(f"{name}_{next(names)}")

    def sem(name):
        sems.append(nc.alloc_semaphore(f"{name}_{next(names)}"))
        return sems[-1]

    def dram(name, shape, dt=F32):
        return nc.dram_tensor(name, shape, dt).ap()

    def row(v):
        return v.rearrange("(a n) -> a n", a=1)

    def spread(v, p=P):
        return v.partition_broadcast(p)

    with ctx:
        bank = ctx.enter_context(nc.psum_tensor("bank", [128, 8, 512], F32))
        x = sb("x", [P, T, D])
        xn = sb("xn", [P, T, D])
        xT = sb("xT", [128, K, N])
        ident = sb("ident", [128, 128])
        ones = sb("ones", [128, 128])
        below = sb("below", [128, 128])
        above = sb("above", [128, 128])
        iota = sb("iota", [128, N])
        lane = sb("lane", [128, 1])
        i8 = sb("i8", [P, NX])
        dinv = sb("dinv", [P, T])
        rdeg = sb("rdeg", [P, T])
        start = sb("start", [P, T])
        cnt = sb("cnt", [P, T])
        bounds = sb("bounds", [1, 32], I32)

        A_dram = dram("count_matrix", (P, T, N))
        table = dram("edge_table", (NULL_ROW + 1, RW))
        kv_dram = dram("kv_rows", (N, 2 * D))
        x_dram = dram("x_rows", (N, D))
        y_dram = dram("y_rows", (N, D))
        key_dram = dram("edge_keys", (2, E))

        def constants():
            iota_i = sb("iota_i", [128, N], I32, c)
            lane_i = sb("lane_i", [128, 1], I32, c)
            loaded, made, filled, masked = sem("x_loaded"), sem("iotas_made"), sem("ones_filled"), sem("masks_made")
            with nc.Block() as block:
                @block.sync
                def _(sp):
                    sp.dma_start(x[:], a["x"].rearrange("(t p) d -> p t d", p=P)).then_inc(loaded, 16)
                    sp.wait_ge(loaded, 16)

                @block.gpsimd
                def _(pool):
                    nc.gpsimd.iota(iota_i[:], [[1, N]], base=0, channel_multiplier=0).then_inc(made, 1)
                    nc.gpsimd.iota(lane_i[:], [[0, 1]], base=0, channel_multiplier=1).then_inc(made, 1)
                    nc.gpsimd.memset(ones[:], 1.0).then_inc(filled, 1)
                    pool.wait_ge(filled, 1)
                    for m, op, sign in ((ident, ALU.is_equal, 1), (below, ALU.is_gt, 1), (above, ALU.is_gt, -1)):
                        nc.gpsimd.affine_select(out=m[:], in_=ones[:], compare_op=op, fill=0.0, base=0,
                                                pattern=[[-sign, 128]], channel_multiplier=sign).then_inc(masked, 1)
                    pool.wait_ge(masked, 3)

                @block.vector
                def _(dve):
                    dve.wait_ge(made, 2)
                    nc.vector.tensor_copy(iota[:], iota_i[:]).then_inc(made, 1)
                    nc.vector.tensor_copy(lane[:], lane_i[:]).then_inc(made, 1)
                    dve.wait_ge(made, 4)
                    nc.vector.tensor_scalar(i8[:], iota[:P, 0:NX], float(NX), None, ALU.subtract).then_inc(made, 1)
                    dve.wait_ge(made, 5)

        def sort_edges():
            G = 8
            NB = EC // G
            cols_i = sb("cols_i", [128, 2, 2 * P], I32, c)
            cols_f = sb("cols_f", [128, 2, 2 * P], F32, c)
            rec = sb("rec", [P, EC, RW], F32, c)
            edge_j = sb("edge_j", [P, EC], F32, c)
            edge_t = sb("edge_t", [P, EC], F32, c)
            oht = sb("oht", [P, EC, T], F32, c)
            ohj = sb("ohj", [P, 2, G, P], F32, c)
            tiles = sb("tiles", [P, T], F32, c)
            hist = sb("hist", [P, EC, T], F32, c)
            cum = sb("cum", [P, T, EC], F32, c)
            one_row = sb("one_row", [P, EC], F32, c)
            tot = sb("tot", [P, 5, T], F32, c)
            fill = sb("fill", [S, SC, RW], F32, c)
            cols_j = sb("cols_j", [128, 2, 2 * P], F32, c)
            row = sb("row", [P, 2, 2, G * P], F32, c)
            ohjT = sb("ohjT", [P, 2, G, P], F32, c)
            same = sb("same", [P, G, P], F32, c)
            earlier = sb("earlier", [P, G, P], F32, c)
            part = sb("part", [P, G, T], F32, c)
            pos = sb("pos", [P, 2, EC], F32, c)
            lo = sb("lo", [P, EC], F32, c)
            pos_i = sb("pos_i", [P, EC], I32, c)
            ld, ld_attr, turned, step = sem("edges_loaded"), sem("attr_loaded"), sem("edges_turned"), sem("dve_step")
            ohj_made, hist_made, hist_kept = sem("ohj_made"), sem("hist_made"), sem("hist_kept")
            base_made, row_ld, row_free = sem("base_made"), sem("row_loaded"), sem("row_free")
            ohjT_made, looked, taken = sem("ohjT_made"), sem("looked_up"), sem("lookup_taken")
            null_made, null_put, put, ready = sem("null_made"), sem("null_put"), dma_sem("record_put"), sem("pos_ready")
            keys_made, keys_put = sem("keys_made"), sem("keys_put")
            spare = sb("spare", [1, RW], F32, c)
            with nc.Block() as block:
                @block.sync
                def _(sp):
                    for i, name in enumerate(("src", "dst")):
                        v = a[name].rearrange("(c p) -> c p", p=P)
                        sp.dma_start(cols_i[:, i, 0:P], v[0:128, :]).then_inc(ld, 16)
                        sp.dma_start(cols_i[0:EC - 128, i, P:2 * P], v[128:EC, :]).then_inc(ld, 16)
                    sp.dma_start(rec[:, :, 2:RW], a["edge_attr_8"].rearrange("(c p) h -> p c h", p=P)).then_inc(ld_attr, 16)
                    sp.wait_ge(null_made, 2)
                    sp.dma_start(table[0:NULL_ROW, :].rearrange("(p c) w -> p c w", p=S), fill[:]).then_inc(null_put, 16)
                    sp.dma_start(table[NULL_ROW:NULL_ROW + 1, :], spare[:]).then_inc(null_put, 16)
                    sp.wait_ge(keys_made, 1)
                    for i, keys in enumerate((cols_f[:, 0], cols_j[:, 1])):
                        v = key_dram[i, :].rearrange("(c p) -> c p", p=P)
                        sp.dma_start(v[0:128, :], keys[:, 0:P]).then_inc(keys_put, 16)
                        sp.dma_start(v[128:EC, :], keys[0:EC - 128, P:2 * P]).then_inc(keys_put, 16)
                    sp.wait_ge(keys_put, 64)
                    v = key_dram.rearrange("k (a n) -> k a n", n=G * P)
                    with sp.Fori(0, NB // 2) as b:
                        for h in range(2):
                            sp.wait_ge(row_free, b * 2 + (h + 1))
                            sp.dma_start(row[:, h], v[:, bass.ds(b * 2 + h, 1), :].rearrange("k a n -> k (a n)").partition_broadcast(P)).then_inc(row_ld, 16)

                @block.gpsimd
                def _(pool):
                    nc.gpsimd.memset(fill[:], 0.0).then_inc(null_made, 1)
                    nc.gpsimd.memset(spare[:], NEG).then_inc(ready, 1)
                    pool.wait_ge(null_made, 1)
                    pool.wait_ge(ready, 1)
                    nc.gpsimd.memset(spare[:, 0:2], 1.0e6)
                    nc.gpsimd.memset(fill[:, :, 0:1], -1.0).then_inc(null_made, 1)
                    pool.wait_ge(ready, 2)
                    pool.wait_ge(null_put, 32)
                    pool.wait_ge(ld_attr, 16)
                    for n in range(EC):
                        nc.gpsimd.indirect_dma_start(
                            out=table, out_offset=bass.IndirectOffsetOnAxis(ap=pos_i[:, n:n + 1], axis=0),
                            in_=rec[:, n, :], in_offset=None).then_inc(put, 16)
                    pool.wait_ge(put, 16 * EC)

                @block.tensor
                def _(pe):
                    pe.wait_ge(step, 2)
                    for i in range(2):
                        nc.tensor.transpose(bank[0:P, i, 0:128], cols_f[:, i, 0:P], ident[:])
                        last = nc.tensor.transpose(bank[0:P, i, 128:EC], cols_f[0:EC - 128, i, P:2 * P], ident[0:EC - 128, 0:EC - 128])
                    last.then_inc(turned, 1)
                    with pe.Fori(0, NB // 2) as b:
                        for h in range(2):
                            pe.wait_ge(ohj_made, b * 2 + h + 1)
                            pe.wait_ge(hist_kept, b * 2 + (h + 1))
                            for g in range(G):
                                last = nc.tensor.matmul(bank[0:P, 2, g * T:(g + 1) * T], ohj[:, h, g, :],
                                                        oht[:, bass.ds(b * (2 * G) + (h * G + g), 1), :].rearrange("p a t -> p (a t)"), start=True, stop=True)
                            last.then_inc(hist_made, 1)
                    pe.wait_ge(base_made, 1)
                    nc.tensor.matmul(bank[0:P, 0, 0:T], above[0:P, 0:P], cnt[:], start=True, stop=True)
                    nc.tensor.matmul(bank[0:P, 0, T:2 * T], ones[0:P, 0:P], cnt[:], start=True, stop=True).then_inc(base_made, 1)
                    with pe.Fori(0, NB // 2) as b:
                        for h in range(2):
                            pe.wait_ge(ohjT_made, b * 2 + h + 1)
                            pe.wait_ge(taken, b * 2 + (h + 1))
                            for g in range(G):
                                last = nc.tensor.matmul(bank[0:P, 3, g * T:(g + 1) * T], ohjT[:, h, g, :],
                                                        hist[:, bass.ds(b * (2 * G) + (h * G + g), 1), :].rearrange("p a t -> p (a t)"), start=True, stop=True)
                            last.then_inc(looked, 1)

                @block.scalar
                def _(act):
                    act.sem_inc(hist_kept, 1)
                    with act.Fori(0, NB) as b:
                        act.wait_ge(hist_made, b + 1)
                        nc.scalar.copy(hist[:, bass.ds(b * G, G), :].rearrange("p c t -> p (c t)"), bank[0:P, 2, 0:G * T]).then_inc(hist_kept, 1)

                @block.vector
                def _(dve):
                    v = [0]

                    def chain(ins):
                        v[0] += 1
                        ins.then_inc(step, 1)
                        dve.wait_ge(step, v[0])

                    for s in (row_free, taken):
                        dve.sem_inc(s, 1)
                    dve.wait_ge(ld, 64)
                    nc.vector.memset(one_row[:], 1.0)
                    nc.vector.tensor_scalar(tiles[:], iota[0:P, 0:T], float(P), None, ALU.mult)
                    chain(nc.vector.memset(cols_f[:], 0.0))
                    nc.vector.tensor_copy(cols_f[:, :, 0:P], cols_i[:, :, 0:P])
                    chain(nc.vector.tensor_copy(cols_f[0:EC - 128, :, P:2 * P], cols_i[0:EC - 128, :, P:2 * P]))
                    def within(out, q, v, n):
                        chain(nc.vector.tensor_scalar(q, v, -(n - 1) / 2, 1.0 / n, ALU.add, ALU.mult))
                        chain(nc.vector.tensor_scalar(q, q, MAGIC, MAGIC, ALU.add, ALU.subtract))
                        chain(nc.vector.scalar_tensor_tensor(out, q, -float(n), v, ALU.mult, ALU.add))

                    within(cols_j[:, 1], cols_j[:, 0], cols_f[:, 0], P)
                    nc.vector.tensor_copy(lo[:, 0:1], lane[0:P]).then_inc(keys_made, 1)
                    dve.wait_ge(turned, 1)
                    nc.vector.tensor_copy(rec[:, :, 0:1].rearrange("p c a -> p (c a)"), bank[0:P, 0, 0:EC])
                    chain(nc.vector.tensor_copy(rec[:, :, 1:2].rearrange("p c a -> p (c a)"), bank[0:P, 1, 0:EC]))
                    srcf = rec[:, :, 0:1].rearrange("p c a -> p (c a)")
                    within(edge_j[:], edge_t[:], srcf, P)
                    chain(nc.vector.tensor_tensor(edge_t[:], srcf, edge_j[:], ALU.subtract))
                    chain(nc.vector.tensor_tensor(oht[:], edge_t[:].unsqueeze(2).to_broadcast([P, EC, T]),
                                                  tiles[:].unsqueeze(1).to_broadcast([P, EC, T]), ALU.is_equal))
                    with dve.Fori(0, NB // 2) as b:
                        for h in range(2):
                            if h == 0:
                                dve.wait_ge(hist_kept, b * 2 + 1)
                            nc.vector.tensor_tensor(ohj[:, h], iota[0:P, 0:P].unsqueeze(1).to_broadcast([P, G, P]),
                                                    edge_j[:, bass.ds(b * (2 * G) + h * G, G)].unsqueeze(2).to_broadcast([P, G, P]),
                                                    ALU.is_equal).then_inc(ohj_made, 1)
                    dve.wait_ge(hist_kept, NB + 1)
                    for t in range(T):
                        last = nc.vector.tensor_tensor_scan(cum[:, t, :], one_row[:], hist[:, :, t], 0.0, ALU.mult, ALU.add)
                    chain(last)
                    chain(nc.vector.tensor_copy(cnt[:], cum[:, :, EC - 1]))
                    nc.vector.tensor_copy(tot[:, 4], cnt[:]).then_inc(base_made, 1)
                    dve.wait_ge(base_made, 2)
                    chain(nc.vector.tensor_scalar(tot[:, 0], bank[0:P, 0, T:2 * T], 1.0, float(S - 1), ALU.max, ALU.add))
                    within(tot[:, 2], tot[:, 1], tot[:, 0], S)
                    chain(nc.vector.tensor_tensor(tot[:, 0], tot[:, 0], tot[:, 2], ALU.subtract))
                    chain(nc.vector.tensor_tensor_scan(tot[:, 1], one_row[:, 0:T], tot[:, 0], 0.0, ALU.mult, ALU.add))
                    chain(nc.vector.tensor_tensor(tot[:, 2], tot[:, 1], tot[:, 0], ALU.subtract))
                    chain(nc.vector.tensor_tensor(start[:], tot[:, 2], bank[0:P, 0, 0:T], ALU.add))
                    chain(nc.vector.tensor_scalar(tot[:, 3], tot[:, 1], 1.0 / S, None, ALU.mult))
                    chain(nc.vector.memset(bounds[:], 0))
                    chain(nc.vector.tensor_copy(bounds[0:1, 1:T + 1], tot[0:1, 3, :]))
                    cumv = cum[:].rearrange("p t c -> p c t")
                    chain(nc.vector.tensor_tensor(hist[:], cumv, hist[:], ALU.subtract))
                    chain(nc.vector.tensor_tensor(hist[:], hist[:], start[:].unsqueeze(1).to_broadcast([P, EC, T]), ALU.add))
                    first = v[0]
                    with dve.Fori(0, NB // 2) as b:
                        for h in range(2):
                            n = b * 2 + h
                            dve.wait_ge(row_ld, n * 16 + 16)
                            nc.vector.tensor_scalar(ohjT[:, h].rearrange("p g e -> p (g e)"), row[:, h, 1], lane[0:P], None, ALU.is_equal).then_inc(ohjT_made, 1)
                            nc.vector.tensor_tensor(same[:], row[:, h, 0].rearrange("p (g e) -> p g e", g=G),
                                                    rec[:, bass.ds(n * G, G), 0:1].to_broadcast([P, G, P]), ALU.is_equal).then_inc(row_free, 1)
                            dve.wait_ge(row_free, n + 2)
                            nc.vector.tensor_tensor(earlier[:], same[:], below[0:P, 0:P].unsqueeze(1).to_broadcast([P, G, P]), ALU.mult).then_inc(step, 1)
                            dve.wait_ge(step, n * 3 + (first + 1))
                            nc.vector.tensor_reduce(pos[:, 0, bass.ds(n * G, G)], earlier[:], X, ALU.add).then_inc(step, 1)
                            dve.wait_ge(looked, n + 1)
                            nc.vector.tensor_tensor(part[:], bank[0:P, 3, 0:G * T].rearrange("p (g t) -> p g t", g=G),
                                                    oht[:, bass.ds(n * G, G), :], ALU.mult).then_inc(taken, 1)
                            dve.wait_ge(taken, n + 2)
                            nc.vector.tensor_reduce(pos[:, 1, bass.ds(n * G, G)], part[:], X, ALU.add).then_inc(step, 1)
                    v[0] = first + 3 * NB
                    dve.wait_ge(step, v[0])
                    chain(nc.vector.tensor_tensor(pos[:, 0], pos[:, 0], pos[:, 1], ALU.add))
                    within(lo[:], edge_t[:], pos[:, 0], S)
                    chain(nc.vector.scalar_tensor_tensor(pos[:, 1], lo[:], float(SC), edge_t[:], ALU.mult, ALU.add))
                    nc.vector.tensor_copy(pos_i[:], pos[:, 1]).then_inc(ready, 1)
                    dve.wait_ge(ready, 2)

        def count_matrix():
            recs = sb("recs", [S, SC, RW], F32, c)
            Asb = sb("A", [P, T, N], F32, c)
            w = sb("w", [S, 2, P], BF16, c)
            hot = sb("hot", [S, 2, N], BF16, c)
            zero = sb("zero", [S, 512], BF16, c)
            one = sb("one", [P, 2], F32, c)
            deg = sb("deg", [P, 3, T], F32, c)
            ld, zeroed, w_made, hot_made, used = (sem(n) for n in ("recs_loaded", "zeroed", "w_made", "hot_made", "hot_used"))
            tile_done, tile_kept, stored, degs, step = (sem(n) for n in ("tile_done", "tile_kept", "A_stored", "deg_made", "deg_step"))
            with nc.Block() as block:
                @block.sync
                def _(sp):
                    sp.dma_start(recs[:], table[0:NULL_ROW, :].rearrange("(p c) w -> p c w", p=S)).then_inc(ld, 16)
                    for t in range(T):
                        sp.wait_ge(tile_kept, t + 1)
                        sp.dma_start(A_dram[:, t, :], Asb[:, t, :]).then_inc(stored, 16)
                    sp.wait_ge(stored, 16 * T)

                @block.vector
                def _(dve):
                    nc.vector.memset(one[:], 1.0)
                    nc.vector.memset(zero[:], 0.0).then_inc(zeroed, 1)
                    dve.wait_ge(ld, 16)
                    for t in range(T):
                        lo = dve.value_load(bounds[0:1, t:t + 1], min_val=0, max_val=SC - 1)
                        hi = dve.value_load(bounds[0:1, t + 1:t + 2], min_val=1, max_val=SC)
                        with dve.Fori(lo, hi) as n:
                            dve.wait_ge(used, n + 1)
                            nc.vector.tensor_scalar(w[:, 0], iota[:, t * P:(t + 1) * P], recs[:, bass.ds(n, 1), 0:1].rearrange("p a b -> p (a b)"), None, ALU.is_equal).then_inc(w_made, 1)
                            nc.vector.tensor_scalar(hot[:, 0], iota[:], recs[:, bass.ds(n, 1), 1:2].rearrange("p a b -> p (a b)"), None, ALU.is_equal).then_inc(hot_made, 1)
                    dve.wait_ge(degs, 1)
                    nc.vector.tensor_scalar(deg[:, 0], bank[0:P, 6, 0:T], 1.0, None, ALU.max).then_inc(step, 1)
                    nc.vector.tensor_scalar(deg[:, 1], bank[0:P, 6, 0:T], 1.0, None, ALU.add).then_inc(step, 1)
                    dve.wait_ge(step, 3)
                    nc.vector.reciprocal(rdeg[:], deg[:, 0]).then_inc(step, 1)
                    nc.vector.reciprocal(dinv[:], deg[:, 2]).then_inc(step, 1)
                    dve.wait_ge(step, 5)

                @block.tensor
                def _(pe):
                    pe.sem_inc(used, 1)
                    pe.wait_ge(zeroed, 1)
                    for t in range(T):
                        if t >= 2:
                            pe.wait_ge(tile_kept, t - 1)
                        lo = pe.value_load(bounds[0:1, t:t + 1], min_val=0, max_val=SC - 1)
                        hi = pe.value_load(bounds[0:1, t + 1:t + 2], min_val=1, max_val=SC)
                        for j, (c0, cn) in enumerate(COLS):
                            nc.tensor.matmul(bank[0:P, 3 * (t % 2) + j, 0:cn], zero[:, 0:P], zero[:, 0:cn], start=True, stop=False, skip_group_check=True)
                        with pe.Fori(lo, hi) as n:
                            pe.wait_ge(w_made, n + 1)
                            pe.wait_ge(hot_made, n + 1)
                            for j, (c0, cn) in enumerate(COLS):
                                last = nc.tensor.matmul(bank[0:P, 3 * (t % 2) + j, 0:cn], w[:, 0], hot[:, 0, c0:c0 + cn], start=False, stop=False, skip_group_check=True)
                            last.then_inc(used, 1)
                        for j, (c0, cn) in enumerate(COLS):
                            last = nc.tensor.matmul(bank[0:P, 3 * (t % 2) + j, 0:cn], zero[:, 0:P], zero[:, 0:cn], start=False, stop=True, skip_group_check=True)
                        last.then_inc(tile_done, 1)
                    pe.wait_ge(tile_kept, T)
                    for d in range(T):
                        for s in range(T):
                            last = nc.tensor.matmul(bank[0:P, 6, d:d + 1], Asb[:, s, d * P:(d + 1) * P], one[:, 0:1], start=(s == 0), stop=(s == T - 1))
                    last.then_inc(degs, 1)

                @block.scalar
                def _(act):
                    for t in range(T):
                        act.wait_ge(tile_done, t + 1)
                        for j, (c0, cn) in enumerate(COLS):
                            last = nc.scalar.copy(Asb[:, t, c0:c0 + cn], bank[0:P, 3 * (t % 2) + j, 0:cn])
                        last.then_inc(tile_kept, 1)
                    act.wait_ge(step, 2)
                    nc.scalar.activation(deg[:, 2], deg[:, 1], ACT.Sqrt).then_inc(step, 1)

        def norm(src, dst, scale=None, shift=None, turn=True, relu=False, add_to=None):
            stats = sb("stats", [P, T, 6], F32, c)
            mv = sb("mv", [P, T, 2], F32, c)
            std = sb("std", [P, 3, T], F32, c)
            gb = sb("gb", [P, 2, D], F32, c)
            counted, merged, var_made, std_made, rstd_made = (sem(n) for n in ("counted", "merged", "var_made", "std_made", "rstd_made"))
            normed, scaled, shifted, turned, kept, ld = (sem(n) for n in ("normed", "scaled", "shifted", "turned", "kept", "affine_loaded"))
            done = normed if scale is None else shifted
            with nc.Block() as block:
                if scale is not None:
                    @block.sync
                    def _(sp):
                        sp.dma_start(gb[:, 0], spread(a[scale])).then_inc(ld, 16)
                        sp.dma_start(gb[:, 1], spread(a[shift])).then_inc(ld, 16)

                @block.vector
                def _(dve):
                    for t in range(T):
                        nc.vector.bn_stats(stats[:, t], src[:, t]).then_inc(counted, 1)
                    for t in range(T):
                        dve.wait_ge(counted, t + 1)
                        nc.vector.bn_aggr(mv[:, t], stats[:, t]).then_inc(merged, 1)
                    dve.wait_ge(merged, T)
                    nc.vector.tensor_scalar(std[:, 0], mv[:, :, 1], 1e-5, None, ALU.add).then_inc(var_made, 1)
                    dve.wait_ge(std_made, 1)
                    nc.vector.reciprocal(std[:, 2], std[:, 1]).then_inc(rstd_made, 1)
                    dve.wait_ge(rstd_made, 1)
                    for t in range(T):
                        nc.vector.tensor_scalar(dst[:, t], src[:, t], mv[:, t, 0:1], std[:, 2, t:t + 1], ALU.subtract, ALU.mult).then_inc(normed, 1)
                        if scale is not None:
                            if t == 0:
                                dve.wait_ge(ld, 32)
                            dve.wait_ge(normed, t + 1)
                            nc.vector.tensor_tensor(dst[:, t], dst[:, t], gb[:, 0], ALU.mult).then_inc(scaled, 1)
                            dve.wait_ge(scaled, t + 1)
                            nc.vector.tensor_tensor(dst[:, t], dst[:, t], gb[:, 1], ALU.add).then_inc(shifted, 1)
                        if add_to is not None:
                            dve.wait_ge(done, t + 1)
                            if relu:
                                nc.vector.scalar_tensor_tensor(add_to[:, t], dst[:, t], 0.0, add_to[:, t], ALU.max, ALU.add)
                            else:
                                nc.vector.tensor_tensor(add_to[:, t], dst[:, t], add_to[:, t], ALU.add)

                @block.scalar
                def _(act):
                    act.wait_ge(var_made, 1)
                    nc.scalar.activation(std[:, 1], std[:, 0], ACT.Sqrt).then_inc(std_made, 1)
                    if turn:
                        for t in range(T):
                            act.wait_ge(turned, t + 1)
                            nc.scalar.copy(xT[:, :, t * P:(t + 1) * P], bank[:, t % 2, 0:K * P].rearrange("p (k n) -> p k n", k=K)).then_inc(kept, 1)

                if turn:
                    @block.tensor
                    def _(pe):
                        for t in range(T):
                            pe.wait_ge(done, t + 1)
                            if t >= 2:
                                pe.wait_ge(kept, t - 1)
                            for k in range(K):
                                last = nc.tensor.transpose(bank[:, t % 2, k * P:(k + 1) * P], dst[:, t, k * 128:(k + 1) * 128], ident[0:P, 0:P])
                            last.then_inc(turned, 1)

        def turn_rows(src):
            turned, kept = sem("turned"), sem("kept")
            with nc.Block() as block:
                @block.tensor
                def _(pe):
                    for t in range(T):
                        if t >= 2:
                            pe.wait_ge(kept, t - 1)
                        for k in range(K):
                            last = nc.tensor.transpose(bank[:, t % 2, k * P:(k + 1) * P], src[:, t, k * 128:(k + 1) * 128], ident[0:P, 0:P])
                        last.then_inc(turned, 1)

                @block.scalar
                def _(act):
                    for t in range(T):
                        act.wait_ge(turned, t + 1)
                        nc.scalar.copy(xT[:, :, t * P:(t + 1) * P], bank[:, t % 2, 0:K * P].rearrange("p (k n) -> p k n", k=K)).then_inc(kept, 1)

        def project(lhs, k_n, w, bias, to):
            ws = sb("ws", [128, k_n, D], F32, c)
            bs = sb("bs", [P, D], F32, c)
            tmp = sb("tmp", [P, 2, D], F32, c)
            ld, made, moved, summed = (sem(n) for n in ("weights_loaded", "made", "moved", "summed"))
            with nc.Block() as block:
                @block.sync
                def _(sp):
                    sp.dma_start(ws[:], w.rearrange("(k p) n -> p k n", p=128)).then_inc(ld, 16)
                    sp.dma_start(bs[:], spread(bias)).then_inc(ld, 16)

                @block.tensor
                def _(pe):
                    pe.wait_ge(ld, 32)
                    for t in range(T):
                        if t >= 4:
                            pe.wait_ge(moved, t - 3)
                        for k in range(k_n):
                            last = nc.tensor.matmul(bank[0:P, t % 4, :], lhs[:, k, t * P:(t + 1) * P], ws[:, k, :], start=(k == 0), stop=(k == k_n - 1))
                        last.then_inc(made, 1)

                @block.vector
                def _(dve):
                    dve.wait_ge(ld, 32)
                    for t in range(T):
                        dve.wait_ge(made, t + 1)
                        nc.vector.tensor_tensor(tmp[:, t % 2], bank[0:P, t % 4, :], bs[:], ALU.add).then_inc(moved, 1)
                        dve.wait_ge(moved, t + 1)
                        nc.vector.tensor_tensor(to[:, t], to[:, t], tmp[:, t % 2], ALU.add).then_inc(summed, 1)

        def route(w, bias, gate, mode, pmax=None):
            wr = sb("wr", [128, K, NX], F32, c)
            br = sb("br", [P, NX], F32, c)
            lg = sb("lg", [P, T, NX], F32, c)
            p = sb("p", [P, T, NX], F32, c)
            q = sb("q", [P, T, NX], F32, c)
            oh = sb("oh", [P, 2, T, NX], F32, c)
            m = sb("m", [P, 6, T], F32, c)
            ld, made, step, shifted, exped = (sem(n) for n in ("router_loaded", "logits_made", "step", "logits_shifted", "exped"))
            with nc.Block() as block:
                @block.sync
                def _(sp):
                    sp.dma_start(wr[:], a[w].rearrange("(k p) n -> p k n", p=128)).then_inc(ld, 16)
                    if bias is not None:
                        sp.dma_start(br[:], spread(a[bias])).then_inc(ld, 16)

                @block.tensor
                def _(pe):
                    pe.wait_ge(ld, 16 if bias is None else 32)
                    for t in range(T):
                        for k in range(K):
                            last = nc.tensor.matmul(bank[0:P, 0, t * NX:(t + 1) * NX], xT[:, k, t * P:(t + 1) * P], wr[:, k, :], start=(k == 0), stop=(k == K - 1))
                    last.then_inc(made, 1)

                if mode == "two" or pmax is not None:
                    @block.scalar
                    def _(act):
                        act.wait_ge(shifted, 1)
                        nc.scalar.activation(p[:], q[:], ACT.Exp).then_inc(exped, 1)

                @block.vector
                def _(dve):
                    v = [0]

                    def chain(ins):
                        v[0] += 1
                        ins.then_inc(step, 1)
                        dve.wait_ge(step, v[0])

                    def wide(col):
                        return col.unsqueeze(2).to_broadcast([P, T, NX])

                    def first_best(oh_, vals, i):
                        chain(nc.vector.tensor_reduce(m[:, i], vals, X, ALU.max))
                        chain(nc.vector.tensor_tensor(oh_, vals, wide(m[:, i]), ALU.is_ge))
                        chain(nc.vector.tensor_tensor(oh_, oh_, i8[:].unsqueeze(1).to_broadcast([P, T, NX]), ALU.mult))
                        chain(nc.vector.tensor_reduce(m[:, 5], oh_, X, ALU.min))
                        chain(nc.vector.tensor_tensor(oh_, i8[:].unsqueeze(1).to_broadcast([P, T, NX]), wide(m[:, 5]), ALU.is_equal))

                    dve.wait_ge(ld, 16 if bias is None else 32)
                    dve.wait_ge(made, 1)
                    raw = bank[0:P, 0, 0:T * NX].rearrange("p (t e) -> p t e", t=T)
                    if bias is None:
                        chain(nc.vector.tensor_copy(lg[:], raw))
                    else:
                        chain(nc.vector.tensor_tensor(lg[:], raw, br[:].unsqueeze(1).to_broadcast([P, T, NX]), ALU.add))
                    if mode == "one" and pmax is None:
                        first_best(gate[:], lg[:], 0)
                        return
                    chain(nc.vector.tensor_reduce(m[:, 1], lg[:], X, ALU.max))
                    nc.vector.tensor_tensor(q[:], lg[:], wide(m[:, 1]), ALU.subtract).then_inc(shifted, 1)
                    dve.wait_ge(exped, 1)
                    chain(nc.vector.tensor_reduce(m[:, 2], p[:], X, ALU.add))
                    chain(nc.vector.reciprocal(m[:, 3], m[:, 2]))
                    chain(nc.vector.tensor_tensor(p[:], p[:], wide(m[:, 3]), ALU.mult))
                    if mode == "one":
                        first_best(gate[:], p[:], 0)
                        chain(nc.vector.tensor_copy(pmax[:], m[:, 0]))
                        return
                    first_best(oh[:, 0], p[:], 0)
                    chain(nc.vector.scalar_tensor_tensor(q[:], oh[:, 0], -4.0, p[:], ALU.mult, ALU.add))
                    first_best(oh[:, 1], q[:], 4)
                    chain(nc.vector.tensor_tensor(oh[:, 0], oh[:, 0], oh[:, 1], ALU.add))
                    chain(nc.vector.tensor_tensor(p[:], p[:], oh[:, 0], ALU.mult))
                    chain(nc.vector.tensor_reduce(m[:, 2], p[:], X, ALU.add))
                    chain(nc.vector.tensor_scalar(m[:, 2], m[:, 2], 1e-9, None, ALU.add))
                    chain(nc.vector.reciprocal(m[:, 3], m[:, 2]))
                    chain(nc.vector.tensor_tensor(gate[:], p[:], wide(m[:, 3]), ALU.mult))

        def experts(w1, b1, w2, b2, gate, func, acc):
            w1s = sb("w1s", [128, 2, K, FF], F32, c)
            w2s = sb("w2s", [128, 2, FF // 128, D], F32, c)
            b1s = sb("b1s", [128, 2, FF // 128], F32, c)
            b2s = sb("b2s", [NX, D], F32, c)
            gT = sb("gT", [NX, T, P], F32, c)
            hid = sb("hid", [128, FF // 128, N], F32, c)
            ld0 = sem("bias_loaded")
            w_ld = [sem(f"w_loaded{h}") for h in range(2)]
            w_used = [sem(f"w_used{h}") for h in range(2)]
            h_kept = [sem(f"hidden_kept{h}") for h in range(2)]
            y_kept = [sem(f"y_added{h}") for h in range(2)]
            h_made, y_made, g_turned, g_kept, bias_made, bias_added = (sem(n) for n in ("hidden_made", "y_made", "gate_turned", "gate_kept", "bias_made", "bias_added"))
            with nc.Block() as block:
                @block.sync
                def _(sp):
                    sp.dma_start(b2s[:], a[b2]).then_inc(ld0, 16)
                    with sp.Fori(0, NX // 2) as i:
                        for h in range(2):
                            sp.wait_ge(w_used[h], i + 1)
                            sp.dma_start(b1s[:, h], a[b1][bass.ds(i * 2 + h, 1)].rearrange("e (f p) -> p (e f)", p=128), allow_slow_non_contiguous=True).then_inc(w_ld[h], 16)
                            sp.dma_start(w1s[:, h], a[w1][bass.ds(i * 2 + h, 1)].rearrange("e (k p) n -> p (e k) n", p=128)).then_inc(w_ld[h], 16)
                            sp.dma_start(w2s[:, h], a[w2][bass.ds(i * 2 + h, 1)].rearrange("e (k p) n -> p (e k) n", p=128)).then_inc(w_ld[h], 16)

                @block.tensor
                def _(pe):
                    for s in w_used:
                        pe.sem_inc(s, 1)
                    for t in range(T):
                        last = nc.tensor.transpose(bank[0:NX, 4 + t // 4, (t % 4) * P:(t % 4 + 1) * P], gate[:, t, :], ident[0:P, 0:P])
                    last.then_inc(g_turned, 1)
                    pe.wait_ge(g_kept, 1)
                    pe.wait_ge(ld0, 16)
                    for t in range(T):
                        if t >= 2:
                            pe.wait_ge(bias_added, t - 1)
                        nc.tensor.matmul(bank[0:P, 2 + t % 2, :], gT[:, t, :], b2s[:], start=True, stop=True).then_inc(bias_made, 1)
                    pe.wait_ge(bias_added, T)
                    with pe.Fori(0, NX // 2) as i:
                        for h in range(2):
                            e = i * 2 + h
                            pe.wait_ge(w_ld[h], i * 48 + 48)
                            g = 0
                            for c0, cn in COLS:
                                for f in range(FF // 128):
                                    pe.wait_ge(h_kept[g % 2], i * 6 + (h * 3 + g // 2 + 1))
                                    for k in range(K):
                                        last = nc.tensor.matmul(bank[:, g % 2, 0:cn], w1s[:, h, k, f * 128:(f + 1) * 128], xT[:, k, c0:c0 + cn], start=(k == 0), stop=(k == K - 1))
                                    last.then_inc(h_made, 1)
                                    g += 1
                            for b in range(2):
                                pe.wait_ge(h_kept[b], i * 6 + (h * 3 + 4))
                            for t in range(T):
                                pe.wait_ge(y_kept[t % 2], i * T + (h * (T // 2) + t // 2 + 1))
                                for f in range(FF // 128):
                                    last = nc.tensor.matmul(bank[0:P, 2 + t % 2, :], hid[:, f, t * P:(t + 1) * P], w2s[:, h, f, :], start=(f == 0), stop=(f == FF // 128 - 1))
                                last.then_inc(y_made, 1)
                            nc.tensor.matmul(bank[0:1, 7, 0:1], ident[:, 0:1], ident[:, 0:1], start=True, stop=True).then_inc(w_used[h], 1)

                @block.scalar
                def _(act):
                    for s in h_kept:
                        act.sem_inc(s, 1)
                    with act.Fori(0, NX // 2) as i:
                        for h in range(2):
                            g = 0
                            for c0, cn in COLS:
                                for f in range(FF // 128):
                                    act.wait_ge(h_made, i * 12 + (h * 6 + g + 1))
                                    nc.scalar.activation(hid[:, f, c0:c0 + cn], bank[:, g % 2, 0:cn], func,
                                                         bias=b1s[:, h, f:f + 1]).then_inc(h_kept[g % 2], 1)
                                    g += 1

                @block.vector
                def _(dve):
                    for s in y_kept:
                        dve.sem_inc(s, 1)
                    dve.wait_ge(g_turned, 1)
                    for j, n in enumerate((4, 4, 2)):
                        last = nc.vector.tensor_copy(gT[:, 4 * j:4 * j + n, :].rearrange("p t n -> p (t n)"), bank[0:NX, 4 + j, 0:n * P])
                    last.then_inc(g_kept, 1)
                    for t in range(T):
                        dve.wait_ge(bias_made, t + 1)
                        nc.vector.tensor_tensor(acc[:, t], bank[0:P, 2 + t % 2, :], acc[:, t], ALU.add).then_inc(bias_added, 1)
                    with dve.Fori(0, NX // 2) as i:
                        for h in range(2):
                            for t in range(T):
                                dve.wait_ge(y_made, i * (2 * T) + (h * T + t + 1))
                                nc.vector.scalar_tensor_tensor(acc[:, t], bank[0:P, 2 + t % 2, :], gate[:, t, bass.ds(i * 2 + h, 1)], acc[:, t],
                                                               ALU.mult, ALU.add).then_inc(y_kept[t % 2], 1)

        def gcn():
            HID = 128
            Asb = sb("A", [P, T, N], F32, c)
            w1s = sb("w1s", [128, K, HID], F32, c)
            w2s = sb("w2s", [128, D], F32, c)
            b1s = sb("b1s", [P, HID], F32, c)
            b2s = sb("b2s", [P, D], F32, c)
            hs = sb("hs", [P, 2, T, HID], F32, c)
            u = sb("u", [P, 2, T, HID], F32, c)
            uT = sb("uT", [HID, T, P], F32, c)
            tmp = sb("tmp", [P, 2, D], F32, c)
            ld, A_ld, h_made, h_kept, agg, agg_kept, step = (sem(n) for n in ("loaded", "A_loaded", "h_made", "h_kept", "aggregated", "agg_kept", "step"))
            s2_made, uT_made, uT_kept, made, moved, u_made = (sem(n) for n in ("s2_made", "uT_made", "uT_kept", "made", "moved", "u_made"))
            with nc.Block() as block:
                @block.sync
                def _(sp):
                    sp.dma_start(w1s[:], a["L0_gnn_W1"].rearrange("(k p) n -> p k n", p=128)).then_inc(ld, 16)
                    sp.dma_start(Asb[:], A_dram).then_inc(A_ld, 16)
                    sp.dma_start(w2s[:], a["L0_gnn_W2"]).then_inc(ld, 16)
                    sp.dma_start(b1s[:], spread(a["L0_gnn_b1"])).then_inc(ld, 16)
                    sp.dma_start(b2s[:], spread(a["L0_gnn_b2"])).then_inc(ld, 16)

                @block.tensor
                def _(pe):
                    pe.wait_ge(ld, 64)
                    for t in range(T):
                        if t >= 2:
                            pe.wait_ge(h_kept, t - 1)
                        for k in range(K):
                            last = nc.tensor.matmul(bank[0:P, t % 2, 0:HID], xT[:, k, t * P:(t + 1) * P], w1s[:, k, :], start=(k == 0), stop=(k == K - 1))
                        last.then_inc(h_made, 1)
                    pe.wait_ge(h_kept, T)
                    pe.wait_ge(A_ld, 16)
                    for r in range(2):
                        if r == 1:
                            pe.wait_ge(s2_made, T)
                        for d in range(T):
                            if r * T + d >= 2:
                                pe.wait_ge(agg_kept, r * T + d - 1)
                            for s in range(T):
                                last = nc.tensor.matmul(bank[0:P, 2 + d % 2, 0:HID], Asb[:, s, d * P:(d + 1) * P], hs[:, r, s, :], start=(s == 0), stop=(s == T - 1))
                            last.then_inc(agg, 1)
                    pe.wait_ge(u_made, T)
                    for t in range(T):
                        if t >= 2:
                            pe.wait_ge(uT_kept, t - 1)
                        nc.tensor.transpose(bank[0:HID, 4 + t % 2, 0:P], u[:, 1, t, :], ident[0:P, 0:P]).then_inc(uT_made, 1)
                        pe.wait_ge(uT_kept, t + 1)
                        if t >= 2:
                            pe.wait_ge(moved, t - 1)
                        nc.tensor.matmul(bank[0:P, 6 + t % 2, :], uT[:, t, :], w2s[:], start=True, stop=True).then_inc(made, 1)

                @block.scalar
                def _(act):
                    for t in range(T):
                        act.wait_ge(h_made, t + 1)
                        nc.scalar.activation(hs[:, 0, t, :], bank[0:P, t % 2, 0:HID], ACT.Copy, scale=dinv[:, t:t + 1]).then_inc(h_kept, 1)
                    for t in range(T):
                        act.wait_ge(uT_made, t + 1)
                        nc.scalar.copy(uT[:, t, :], bank[0:HID, 4 + t % 2, 0:P]).then_inc(uT_kept, 1)

                @block.vector
                def _(dve):
                    v = [0]

                    def chain(ins):
                        v[0] += 1
                        ins.then_inc(step, 1)
                        dve.wait_ge(step, v[0])

                    dve.wait_ge(ld, 64)
                    dve.wait_ge(h_kept, T)
                    for r in range(2):
                        for d in range(T):
                            dve.wait_ge(agg, r * T + d + 1)
                            nc.vector.tensor_tensor(u[:, r, d, :], bank[0:P, 2 + d % 2, 0:HID], hs[:, r, d, :], ALU.add).then_inc(agg_kept, 1)
                            dve.wait_ge(agg_kept, r * T + d + 1)
                            if r == 1:
                                nc.vector.tensor_scalar(u[:, 1, d, :], u[:, 1, d, :], dinv[:, d:d + 1], None, ALU.mult).then_inc(u_made, 1)
                                continue
                            chain(nc.vector.scalar_tensor_tensor(u[:, 0, d, :], u[:, 0, d, :], dinv[:, d:d + 1], b1s[:], ALU.mult, ALU.add))
                            nc.vector.tensor_scalar(hs[:, 1, d, :], u[:, 0, d, :], 0.0, dinv[:, d:d + 1], ALU.max, ALU.mult).then_inc(s2_made, 1)
                        if r == 0:
                            dve.wait_ge(s2_made, T)
                    for t in range(T):
                        dve.wait_ge(made, t + 1)
                        nc.vector.tensor_tensor(tmp[:, t % 2], bank[0:P, 6 + t % 2, :], b2s[:], ALU.add).then_inc(moved, 1)
                        dve.wait_ge(moved, t + 1)
                        nc.vector.tensor_tensor(x[:, t], x[:, t], tmp[:, t % 2], ALU.add).then_inc(step, 1)

        def edge_attention():
            ws = sb("ws", [128, 3, K, D], F32, c)
            bs = sb("bs", [P, 3, D], F32, c)
            qs = sb("qs", [P, T, D], F32, c)
            kvs = sb("kvs", [P, 2, 2 * D], F32, c)
            most = sb("most", [T, 4, P], F32, c)
            seg = sb("seg", [1, 4, T], F32, c)
            cT = sb("cT", [T, 1], F32, c)
            ld, made, kept, put, m1, step = (sem(n) for n in ("weights_loaded", "made", "kept", "kv_put", "turned", "step"))
            with nc.Block() as block:
                @block.sync
                def _(sp):
                    for i, n in enumerate("qkv"):
                        sp.dma_start(ws[:, i], a[f"L1_gnn_W{n}"].rearrange("(k p) n -> p k n", p=128)).then_inc(ld, 16)
                        sp.dma_start(bs[:, i], spread(a[f"L1_gnn_b{n}"])).then_inc(ld, 16)
                    for t in range(T):
                        sp.wait_ge(kept, 3 * t + 3)
                        sp.dma_start(kv_dram[t * P:(t + 1) * P, :], kvs[:, t % 2]).then_inc(put, 16)
                        sp.wait_ge(put, 16 * t + 16)

                @block.tensor
                def _(pe):
                    nc.tensor.transpose(bank[0:T, 6, 0:P], cnt[:], ident[0:P, 0:P]).then_inc(m1, 1)
                    pe.wait_ge(step, 1)
                    nc.tensor.transpose(bank[0:1, 7, 0:T], cT[:], ident[0:T, 0:T]).then_inc(m1, 1)
                    pe.wait_ge(ld, 96)
                    for t in range(T):
                        for i in range(3):
                            if t >= 2:
                                pe.wait_ge(kept, 3 * (t - 2) + i + 1)
                            for k in range(K):
                                last = nc.tensor.matmul(bank[0:P, 3 * (t % 2) + i, :], xT[:, k, t * P:(t + 1) * P], ws[:, i, k, :], start=(k == 0), stop=(k == K - 1))
                            last.then_inc(made, 1)

                @block.vector
                def _(dve):
                    v = [0]

                    def chain(ins):
                        v[0] += 1
                        ins.then_inc(step, 1)
                        dve.wait_ge(step, v[0])

                    dve.wait_ge(m1, 1)
                    chain(nc.vector.tensor_reduce(cT[:], bank[0:T, 6, 0:P], X, ALU.max))
                    dve.wait_ge(m1, 2)
                    chain(nc.vector.tensor_scalar(seg[:, 0], bank[0:1, 7, 0:T], 1.0, float(2 * B - 1) / 2, ALU.max, ALU.add))
                    chain(nc.vector.tensor_scalar(seg[:, 0], seg[:, 0], 1.0 / (2 * B), MAGIC, ALU.mult, ALU.add))
                    chain(nc.vector.tensor_scalar(seg[:, 0], seg[:, 0], MAGIC, None, ALU.subtract))
                    chain(nc.vector.tensor_tensor_scan(seg[:, 1], ones[0:1, 0:T], seg[:, 0], 0.0, ALU.mult, ALU.add))
                    chain(nc.vector.tensor_copy(bounds[0:1, 17:17 + T], seg[:, 1]))
                    dve.wait_ge(ld, 96)
                    for t in range(T):
                        for i in range(3):
                            dve.wait_ge(made, 3 * t + i + 1)
                            if i == 1 and t >= 2:
                                dve.wait_ge(put, 16 * (t - 1))
                            dst = qs[:, t] if i == 0 else kvs[:, t % 2, (i - 1) * D:i * D]
                            nc.vector.tensor_tensor(dst, bank[0:P, 3 * (t % 2) + i, :], bs[:, i], ALU.add).then_inc(kept, 1)

            kv = sb("kv", [P, 2, B, 2 * D], F32, c)
            rec = sb("rec", [P, 2, B, RW], F32, c)
            row_i = sb("row_i", [P, 2, B], I32, c)
            kv_i = sb("kv_i", [P, 2, B], I32, c)
            rr = sb("rr", [P, B], F32, c)
            f = sb("f", [P, 5, B], F32, c)
            tmp = ws[0:P].rearrange("p i k n -> p (i k n)")[:, 0:B * D].rearrange("p (b n) -> p b n", b=B)
            lg = sb("lg", [P, B + 1, H], F32, c)
            ex = sb("ex", [P, B + 1, H], F32, c)
            mx = sb("mx", [P, 2, H], F32, c)
            den = sb("den", [P, 3, H], F32, c)
            yy = sb("yy", [P, 2, D], F32, c)
            row_ready = [sem(f"row_ready{h}") for h in range(2)]
            rec_ld = [dma_sem(f"record_loaded{h}") for h in range(2)]
            kv_ready = [sem(f"kv_index_ready{h}") for h in range(2)]
            kv_ld = [dma_sem(f"kv_loaded{h}") for h in range(2)]
            shifted, exped, cleared, st = sem("logits_shifted"), sem("exped"), sem("cleared"), sem("st")
            passed = [sem("pool_passed"), sem("dve_passed")]
            with nc.Block() as block:
                @block.gpsimd
                def _(pool):
                    def fetch(h, n):
                        pool.wait_ge(row_ready[h], n)
                        pool.sem_inc(passed[0], 1)
                        for b in range(B):
                            nc.gpsimd.indirect_dma_start(out=rec[:, h, b, :], out_offset=None, in_=table,
                                                         in_offset=bass.IndirectOffsetOnAxis(ap=row_i[:, h, b:b + 1], axis=0)).then_inc(rec_ld[h], 16)
                        pool.wait_ge(kv_ready[h], n)
                        pool.sem_inc(passed[0], 1)
                        for b in range(B):
                            nc.gpsimd.indirect_dma_start(out=kv[:, h, b, :], out_offset=None, in_=kv_dram,
                                                         in_offset=bass.IndirectOffsetOnAxis(ap=kv_i[:, h, b:b + 1], axis=0),
                                                         bounds_check=N - 1, oob_is_err=False).then_inc(kv_ld[h], 16)

                    pool.wait_ge(cleared, 1)
                    for t in range(T):
                        lo = pool.value_load(bounds[0:1, 16 + t:17 + t], min_val=0, max_val=E)
                        hi = pool.value_load(bounds[0:1, 17 + t:18 + t], min_val=1, max_val=E)
                        fetch(0, lo + (t + 1))
                        with pool.Fori(lo, hi) as n:
                            fetch(1, n + 1)
                            fetch(0, n + (t + 2))

                @block.scalar
                def _(act):
                    hi = act.value_load(bounds[0:1, 16 + T:17 + T], min_val=1, max_val=E)
                    with act.Fori(0, hi) as n:
                        for h in range(2):
                            act.wait_ge(shifted, n * 2 + (h + 1))
                            nc.scalar.activation(ex[:], lg[:], ACT.Exp).then_inc(exped, 1)

                @block.vector
                def _(dve):
                    nc.vector.memset(kv[:], 0.0).then_inc(cleared, 1)
                    count = {"n": 0, "s": None}

                    def chain(ins):
                        count["n"] += 1
                        ins.then_inc(st, 1)
                        at = count["n"]
                        dve.wait_ge(st, at if count["s"] is None else count["s"] + at)

                    def rows(h, t):
                        chain(nc.vector.tensor_scalar(f[:, 0], rr[:], start[:, t:t + 1], None, ALU.add))
                        chain(nc.vector.tensor_scalar(f[:, 1], f[:, 0], -(S - 1) / 2, 1.0 / S, ALU.add, ALU.mult))
                        chain(nc.vector.tensor_scalar(f[:, 1], f[:, 1], MAGIC, MAGIC, ALU.add, ALU.subtract))
                        chain(nc.vector.scalar_tensor_tensor(f[:, 2], f[:, 1], -float(S), f[:, 0], ALU.mult, ALU.add))
                        chain(nc.vector.scalar_tensor_tensor(f[:, 3], f[:, 2], float(SC), f[:, 1], ALU.mult, ALU.add))
                        chain(nc.vector.tensor_scalar(f[:, 4], rr[:], cnt[:, t:t + 1], None, ALU.is_lt))
                        chain(nc.vector.scalar_tensor_tensor(f[:, 3], f[:, 3], -float(NULL_ROW), f[:, 4], ALU.add, ALU.mult))
                        chain(nc.vector.tensor_scalar(rr[:], rr[:], float(B), None, ALU.add))
                        nc.vector.tensor_scalar(row_i[:, h], f[:, 3], float(NULL_ROW), None, ALU.add).then_inc(row_ready[h], 1)

                    def kv_rows(h, n):
                        dve.wait_ge(rec_ld[h], n * (16 * B))
                        nc.vector.tensor_copy(kv_i[:, h], rec[:, h, :, 1]).then_inc(kv_ready[h], 1)

                    def wide(v, shape):
                        return v.to_broadcast(shape)

                    def first_half(h, t, n):
                        dve.wait_ge(kv_ld[h], n * (16 * B))
                        chain(nc.vector.tensor_tensor(tmp, kv[:, h, :, 0:D], qs[:, t].unsqueeze(1).to_broadcast([P, B, D]), ALU.mult))
                        chain(nc.vector.tensor_reduce(lg[:, 0:B], tmp.rearrange("p b (h d) -> p b h d", h=H), X, ALU.add))
                        chain(nc.vector.scalar_tensor_tensor(lg[:, 0:B], lg[:, 0:B], DH ** -0.5, rec[:, h, :, 2:RW], ALU.mult, ALU.add))
                        chain(nc.vector.tensor_reduce(mx[:, 1], lg[:, 0:B].rearrange("p b h -> p h b"), X, ALU.max))
                        chain(nc.vector.tensor_tensor(mx[:, 1], mx[:, 1], mx[:, 0], ALU.max))
                        chain(nc.vector.tensor_copy(lg[:, B], mx[:, 0]))
                        nc.vector.tensor_copy(mx[:, 0], mx[:, 1])
                        chain(nc.vector.tensor_tensor(lg[:], lg[:], mx[:, 1].unsqueeze(1).to_broadcast([P, B + 1, H]), ALU.subtract))
                        nc.vector.tensor_copy(f[:, 0, 0:1], lane[0:P]).then_inc(shifted, 1)

                    def second_half(h, n):
                        dve.wait_ge(exped, n)
                        chain(nc.vector.tensor_tensor(tmp.rearrange("p b (h d) -> p b h d", h=H), kv[:, h, :, D:2 * D].rearrange("p b (h d) -> p b h d", h=H),
                                                      ex[:, 0:B].unsqueeze(3).to_broadcast([P, B, H, DH]), ALU.mult))
                        chain(nc.vector.tensor_reduce(den[:, 1], ex[:, 0:B].rearrange("p b h -> p h b"), X, ALU.add))
                        chain(nc.vector.tensor_tensor(den[:, 0], den[:, 0], ex[:, B], ALU.mult))
                        chain(nc.vector.tensor_tensor(den[:, 0], den[:, 0], den[:, 1], ALU.add))
                        y3 = yy[:, 0].rearrange("p (h d) -> p h d", h=H)
                        chain(nc.vector.tensor_tensor(y3, y3, ex[:, B].unsqueeze(2).to_broadcast([P, H, DH]), ALU.mult))
                        chain(nc.vector.tensor_reduce(yy[:, 1], tmp.rearrange("p b n -> p n b"), X, ALU.add))
                        chain(nc.vector.tensor_tensor(yy[:, 0], yy[:, 0], yy[:, 1], ALU.add))

                    steps = None
                    tile_base = 0
                    LOOP = 2 * (8 + 7 + 7)
                    for t in range(T):
                        dve.sem_inc(passed[1], 1)
                        lo = dve.value_load(bounds[0:1, 16 + t:17 + t], min_val=0, max_val=E)
                        hi = dve.value_load(bounds[0:1, 17 + t:18 + t], min_val=1, max_val=E)
                        count["s"] = lo * LOOP
                        nc.vector.tensor_copy(rr[:], iota[0:P, 0:B])
                        nc.vector.memset(den[:, 0], 0.0)
                        nc.vector.memset(mx[:, 0], NEG)
                        chain(nc.vector.memset(yy[:, 0], 0.0))
                        rows(0, t)
                        kv_rows(0, lo + (t + 1))
                        before = count["n"]
                        with dve.Fori(lo, hi) as n:
                            count["s"], count["n"] = n * LOOP, before
                            rows(1, t)
                            first_half(0, t, n + (t + 1))
                            kv_rows(1, n + 1)
                            second_half(0, n * 2 + 1)
                            rows(0, t)
                            first_half(1, t, n + 1)
                            kv_rows(0, n + (t + 2))
                            second_half(1, n * 2 + 2)
                            dve.sem_inc(passed[1], 1)
                        assert count["n"] == before + LOOP
                        count["s"], count["n"] = hi * LOOP, before
                        chain(nc.vector.reciprocal(den[:, 1], den[:, 0]))
                        chain(nc.vector.tensor_scalar(den[:, 2], den[:, 1], 1.0, None, ALU.mult))
                        chain(nc.vector.tensor_scalar(f[:, 1, 0:1], cnt[:, t:t + 1], 1.0, None, ALU.min))
                        chain(nc.vector.tensor_scalar(den[:, 2], den[:, 1], f[:, 1, 0:1], None, ALU.mult))
                        chain(nc.vector.tensor_tensor(xn[:, t].rearrange("p (h d) -> p h d", h=H), yy[:, 0].rearrange("p (h d) -> p h d", h=H),
                                                      den[:, 2].unsqueeze(2).to_broadcast([P, H, DH]), ALU.mult))
                    dve.wait_ge(rec_ld[0], (hi + T) * (16 * B))
                    dve.wait_ge(kv_ld[0], (hi + T) * (16 * B))
                    dve.sem_inc(passed[1], 1)

        def full_attention():
            wq = sb("wq", [128, 2, 3, K, 128], F32, c)
            bqk = sb("bqk", [128, 2], F32, c)
            bv = sb("bv", [P, D], F32, c)
            qT = sb("qT", [128, N], F32, c)
            kT = sb("kT", [128, N], F32, c)
            vs = sb("vs", [P, T, 128], F32, c)
            pr = sb("pr", [P, 2, N], F32, c)
            pT = sb("pT", [P, T, N], F32, c)
            oT = sb("oT", [128, K, N], F32, c)
            mx = sb("mx", [P, 2, 4], F32, c)
            ld0, w_ld, w_used = sem("bias_loaded"), sem("w_loaded"), sem("w_used")
            s_made, maxed, exped, summed, scaled, small_made = (sem(n) for n in ("scores_made", "maxed", "exped", "inverted", "p_scaled", "small_made"))
            s_free = [sem(f"scores_free{i}") for i in range(2)]
            small_free = [sem(f"small_free{i}") for i in range(2)]
            SM = 76
            VG = [(0, 3), (3, 3), (6, 3), (9, 1)]
            TG = [(0, 4), (4, 4), (8, 2)]
            SCALE = DH ** -0.5
            with nc.Block() as block:
                @block.sync
                def _(sp):
                    sp.dma_start(bv[:], spread(a["L1_ffn_bv"])).then_inc(ld0, 16)
                    with sp.Fori(0, K) as m:
                        sp.wait_ge(w_used, m + 1)
                        for i, n in enumerate("qk"):
                            sp.dma_start(bqk[:, i:i + 1], a[f"L1_ffn_b{n}"].rearrange("(m p a) -> m p a", p=128, a=1)[bass.ds(m, 1)].rearrange("m p a -> (m p) a"), allow_slow_non_contiguous=True).then_inc(w_ld, 16)
                        for i, n in enumerate("qkv"):
                            sp.dma_start(wq[:, 0, i], a[f"L1_ffn_W{n}"].rearrange("(k p) (m n) -> p k m n", p=128, n=128)[:, :, bass.ds(m, 1), :].rearrange("p k m n -> p k (m n)")).then_inc(w_ld, 16)

                @block.tensor
                def _(pe):
                    def group(m, g):
                        pe.wait_ge(small_free[g % 2], m * (SM // 2) + (g // 2 + 1))
                        return 6 + g % 2

                    pe.sem_inc(w_used, 1)
                    with pe.Fori(0, K) as m:
                        g = 0
                        pe.wait_ge(w_ld, m * 80 + 80)
                        for i in range(2):
                            for c0, cn in COLS:
                                b = group(m, g)
                                for k in range(K):
                                    last = nc.tensor.matmul(bank[:, b, 0:cn], wq[:, 0, i, k, :], xT[:, k, c0:c0 + cn], start=(k == 0), stop=(k == K - 1))
                                last.then_inc(small_made, 1)
                                g += 1
                        for t0, tn in VG:
                            b = group(m, g)
                            for t in range(t0, t0 + tn):
                                for k in range(K):
                                    last = nc.tensor.matmul(bank[0:P, b, (t - t0) * 128:(t - t0 + 1) * 128], xT[:, k, t * P:(t + 1) * P], wq[:, 0, 2, k, :], start=(k == 0), stop=(k == K - 1))
                            last.then_inc(small_made, 1)
                            g += 1
                        for b in range(2):
                            pe.wait_ge(small_free[b], m * (SM // 2) + (g // 2 + 1))
                        nc.tensor.matmul(bank[0:1, 6, 511:512], ident[:, 0:1], ident[:, 0:1], start=True, stop=True).then_inc(w_used, 1)

                        def scores(h, t):
                            n = h * T + t
                            pe.wait_ge(s_free[t % 2], m * T + (n // 2 + 1))
                            for j, (c0, cn) in enumerate(COLS):
                                last = nc.tensor.matmul(bank[0:P, 3 * (t % 2) + j, 0:cn], qT[h * DH:(h + 1) * DH, t * P:(t + 1) * P], kT[h * DH:(h + 1) * DH, c0:c0 + cn], start=True, stop=True)
                            last.then_inc(s_made, 1)

                        for h in range(2):
                            scores(h, 0)
                            for t in range(T):
                                if t + 1 < T:
                                    scores(h, t + 1)
                                pe.wait_ge(scaled, m * (2 * T) + (h * T + t + 1))
                                for k0, kn in TG:
                                    b = group(m, g)
                                    for k in range(k0, k0 + kn):
                                        last = nc.tensor.transpose(bank[0:P, b, (k - k0) * P:(k - k0 + 1) * P], pr[:, t % 2, k * P:(k + 1) * P], ident[0:P, 0:P])
                                    last.then_inc(small_made, 1)
                                    g += 1
                            for c0, cn in COLS:
                                b = group(m, g)
                                pe.wait_ge(small_free[(g + 1) % 2], m * (SM // 2) + ((g + 1) // 2 + 1)) if c0 == 0 else None
                                for k in range(T):
                                    last = nc.tensor.matmul(bank[0:DH, b, 0:cn], vs[:, k, h * DH:(h + 1) * DH], pT[:, k, c0:c0 + cn], start=(k == 0), stop=(k == T - 1))
                                last.then_inc(small_made, 1)
                                g += 1
                        assert g == SM

                @block.scalar
                def _(act):
                    with act.Fori(0, K) as m:
                        g = 0

                        def small():
                            act.wait_ge(small_made, m * SM + (g + 1))

                        for i, dst in enumerate((qT, kT)):
                            for c0, cn in COLS:
                                small()
                                nc.scalar.activation(dst[:, c0:c0 + cn], bank[:, 6 + g % 2, 0:cn], ACT.Identity, bias=bqk[:, i:i + 1]).then_inc(small_free[g % 2], 1)
                                g += 1
                        g += len(VG)

                        def expo(h, t):
                            n = h * T + t
                            act.wait_ge(maxed, m * (2 * T) + (n + 1))
                            nc.scalar.activation(pr[:, t % 2, :].rearrange("p (a b) -> p a b", a=5)[:, 0:4, :].rearrange("p (u v) b -> p u (v b)", u=2),
                                                 bank[0:P, 3 * (t % 2):3 * (t % 2) + 2, 0:500], ACT.Exp, bias=mx[:, t % 2, 1:2], scale=SCALE, accum_out=mx[:, t % 2, 2:3])
                            nc.scalar.activation(pr[:, t % 2, 1000:N], bank[0:P, 3 * (t % 2) + 2, 0:250], ACT.Exp, bias=mx[:, t % 2, 1:2], scale=SCALE, accum_out=mx[:, t % 2, 3:4]).then_inc(exped, 1)

                        for h in range(2):
                            expo(h, 0)
                            for t in range(T):
                                if t + 1 < T:
                                    expo(h, t + 1)
                                for k0, kn in TG:
                                    small()
                                    nc.scalar.copy(pT[:, k0:k0 + kn, t * P:(t + 1) * P], bank[0:P, 6 + g % 2, 0:kn * P].rearrange("p (k n) -> p k n", k=kn)).then_inc(small_free[g % 2], 1)
                                    g += 1
                            for c0, cn in COLS:
                                small()
                                nc.scalar.copy(oT[h * DH:(h + 1) * DH, bass.ds(m, 1), c0:c0 + cn].rearrange("p a n -> p (a n)"), bank[0:DH, 6 + g % 2, 0:cn]).then_inc(small_free[g % 2], 1)
                                g += 1

                @block.vector
                def _(dve):
                    for s in small_free + s_free:
                        dve.sem_inc(s, 1)
                    dve.wait_ge(ld0, 16)
                    with dve.Fori(0, K) as m:
                        g = 6
                        for t0, tn in VG:
                            dve.wait_ge(small_made, m * SM + (g + 1))
                            nc.vector.tensor_tensor(vs[:, t0:t0 + tn, :], bank[0:P, 6 + g % 2, 0:tn * 128].rearrange("p (t n) -> p t n", t=tn),
                                                    bv[:, bass.ds(m * 128, 128)].unsqueeze(1).to_broadcast([P, tn, 128]), ALU.add).then_inc(small_free[g % 2], 1)
                            g += 1

                        def top(h, t):
                            n = m * (2 * T) + (h * T + t)
                            dve.wait_ge(s_made, n + 1)
                            nc.vector.tensor_reduce(mx[:, t % 2, 2:4], bank[0:P, 3 * (t % 2):3 * (t % 2) + 2, 0:500], X, ALU.max).then_inc(summed, 1)
                            nc.vector.tensor_reduce(mx[:, t % 2, 0:1], bank[0:P, 3 * (t % 2) + 2, 0:250], X, ALU.max).then_inc(summed, 1)
                            dve.wait_ge(summed, n * 7 + 2)
                            nc.vector.tensor_tensor(mx[:, t % 2, 0:1], mx[:, t % 2, 0:1], mx[:, t % 2, 2:3], ALU.max).then_inc(summed, 1)
                            dve.wait_ge(summed, n * 7 + 3)
                            nc.vector.tensor_tensor(mx[:, t % 2, 0:1], mx[:, t % 2, 0:1], mx[:, t % 2, 3:4], ALU.max).then_inc(summed, 1)
                            dve.wait_ge(summed, n * 7 + 4)
                            nc.vector.tensor_scalar(mx[:, t % 2, 1:2], mx[:, t % 2, 0:1], -SCALE, None, ALU.mult).then_inc(maxed, 1)

                        def scale(h, t):
                            n = m * (2 * T) + (h * T + t)
                            dve.wait_ge(exped, n + 1)
                            nc.vector.tensor_tensor(mx[:, t % 2, 0:1], mx[:, t % 2, 2:3], mx[:, t % 2, 3:4], ALU.add).then_inc(summed, 1)
                            dve.wait_ge(summed, n * 7 + 5)
                            nc.vector.reciprocal(mx[:, t % 2, 2:3], mx[:, t % 2, 0:1]).then_inc(summed, 1)
                            dve.wait_ge(summed, n * 7 + 6)
                            nc.vector.tensor_scalar(pr[:, t % 2, :], pr[:, t % 2, :], mx[:, t % 2, 2:3], None, ALU.mult).then_inc(scaled, 1)
                            dve.wait_ge(scaled, n + 1)
                            nc.vector.tensor_copy(mx[:, t % 2, 0:1], lane[0:P]).then_inc(summed, 1)
                            nc.vector.tensor_copy(mx[:, t % 2, 1:2], lane[0:P]).then_inc(s_free[t % 2], 1)

                        for h in range(2):
                            for t in range(T):
                                top(h, t)
                                scale(h, t)

            moved = sem("moved")
            with nc.Block() as block:
                @block.scalar
                def _(act):
                    for k in range(K):
                        nc.scalar.copy(xT[:, k, :], oT[:, k, :]).then_inc(moved, 1)

        def mean_layer(w_self, w_neigh, bias, relu, to):
            Asb = sb("A", [P, T, N], F32, c)
            aT = sb("aT", [128, K, N], F32, c)
            ws = sb("ws", [128, 2, K, D], F32, c)
            bs = sb("bs", [P, D], F32, c)
            tmp = sb("tmp", [P, 2, D], F32, c)
            ld, A_ld, agg, agg_kept, made, moved, step = (sem(n) for n in ("loaded", "A_loaded", "aggregated", "agg_kept", "made", "moved", "step"))
            with nc.Block() as block:
                @block.sync
                def _(sp):
                    sp.dma_start(Asb[:], A_dram).then_inc(A_ld, 16)
                    for i, w in enumerate((w_self, w_neigh)):
                        sp.dma_start(ws[:, i], w.rearrange("(k p) n -> p k n", p=128)).then_inc(ld, 16)
                    sp.dma_start(bs[:], spread(bias)).then_inc(ld, 16)

                @block.tensor
                def _(pe):
                    pe.wait_ge(A_ld, 16)
                    g = 0
                    for c0, cn in COLS:
                        for k in range(K):
                            if g >= 4:
                                pe.wait_ge(agg_kept, g - 3)
                            for s in range(T):
                                last = nc.tensor.matmul(bank[:, g % 4, 0:cn], xn[:, s, k * 128:(k + 1) * 128], Asb[:, s, c0:c0 + cn], start=(s == 0), stop=(s == T - 1))
                            last.then_inc(agg, 1)
                            g += 1
                    pe.wait_ge(agg_kept, g)
                    pe.wait_ge(ld, 48)
                    for t in range(T):
                        if t >= 2:
                            pe.wait_ge(moved, t - 1)
                        for i, lhs in enumerate((xT, aT)):
                            for k in range(K):
                                last = nc.tensor.matmul(bank[0:P, 4 + 2 * (t % 2) + i, :], lhs[:, k, t * P:(t + 1) * P], ws[:, i, k, :], start=(k == 0), stop=(k == K - 1))
                        last.then_inc(made, 1)

                @block.scalar
                def _(act):
                    g = 0
                    for c0, cn in COLS:
                        for k in range(K):
                            act.wait_ge(agg, g + 1)
                            nc.scalar.copy(aT[:, k, c0:c0 + cn], bank[:, g % 4, 0:cn]).then_inc(agg_kept, 1)
                            g += 1

                @block.vector
                def _(dve):
                    v = [0]

                    def chain(ins):
                        v[0] += 1
                        ins.then_inc(step, 1)
                        dve.wait_ge(step, v[0])

                    dve.wait_ge(ld, 48)
                    for t in range(T):
                        dve.wait_ge(made, t + 1)
                        o = tmp[:, t % 2]
                        chain(nc.vector.tensor_tensor(o, bank[0:P, 4 + 2 * (t % 2), :], bs[:], ALU.add))
                        nc.vector.scalar_tensor_tensor(o, bank[0:P, 5 + 2 * (t % 2), :], rdeg[:, t:t + 1], o, ALU.mult, ALU.add).then_inc(moved, 1)
                        dve.wait_ge(moved, t + 1)
                        if relu:
                            chain(nc.vector.scalar_tensor_tensor(to[:, t], o, 0.0, to[:, t], ALU.max, ALU.add))
                        else:
                            chain(nc.vector.tensor_copy(to[:, t], o))

        U = N // 2 // P
        PC = N // 2
        W2 = D // 2

        def to_pairs():
            put, got = sem("x_put"), sem("x_got")
            with nc.Block() as block:
                @block.sync
                def _(sp):
                    sp.dma_start(x_dram.rearrange("(t p) d -> p t d", p=P), x[:]).then_inc(put, 16)
                    sp.wait_ge(put, 16)
                    sp.dma_start(x[:].rearrange("p (u r) d -> p u (r d)", r=2), x_dram.rearrange("(u p r) d -> p u (r d)", p=P, r=2)).then_inc(got, 16)
                    sp.wait_ge(got, 16)

        def from_pairs():
            put, got = sem("x_put"), sem("x_got")
            with nc.Block() as block:
                @block.sync
                def _(sp):
                    sp.dma_start(x_dram.rearrange("(u p r) d -> p u (r d)", p=P, r=2), x[:].rearrange("p (u r) d -> p u (r d)", r=2)).then_inc(put, 16)
                    sp.wait_ge(put, 16)
                    sp.dma_start(x[:], x_dram.rearrange("(t p) d -> p t d", p=P)).then_inc(got, 16)
                    sp.wait_ge(got, 16)

        def wavelet():
            F = FF // 128
            C2 = [(0, 375), (375, 250)]
            wi = sb("wi", [128, 2, D], F32, c)
            w1s = sb("w1s", [128, K, FF], F32, c)
            w2s = sb("w2s", [128, F, W2], F32, c)
            b1s = sb("b1s", [128, F], F32, c)
            b2s = sb("b2s", [P, W2], F32, c)
            sums = sb("sums", [P, U, D], F32, c)
            difs = sb("difs", [P, U, D], F32, c)
            low = sb("low", [P, U, 4, W2], F32, c)
            llT = sb("llT", [128, 2, PC], F32, c)
            upT = sb("upT", [128, K, PC], F32, c)
            hT = sb("hT", [128, F, PC], F32, c)
            nl = sb("nl", [P, 2, W2], F32, c)
            o = sb("o", [P, 6, W2], F32, c)
            ld, made, step, turned, kept, mm, mm_kept, last_made, moved = (sem(n) for n in (
                "loaded", "parts_made", "step", "ll_turned", "ll_kept", "product_made", "product_kept", "new_made", "new_moved"))
            pairs = xn[:].rearrange("p (u r) d -> p u r d", r=2)
            xp = x[:].rearrange("p (u r) d -> p u r d", r=2)
            with nc.Block() as block:
                @block.sync
                def _(sp):
                    sp.dma_start(wi[:], a["stretch"].rearrange("(k p) n -> p k n", p=128)).then_inc(ld, 16)
                    sp.dma_start(w1s[:], a["L2_ffn_fc1_w"].rearrange("(k p) n -> p k n", p=128)).then_inc(ld, 16)
                    sp.dma_start(w2s[:], a["L2_ffn_fc2_w"].rearrange("(k p) n -> p k n", p=128)).then_inc(ld, 16)
                    sp.dma_start(b1s[:], a["L2_ffn_fc1_b"].rearrange("(f p) -> p f", p=128), allow_slow_non_contiguous=True).then_inc(ld, 16)
                    sp.dma_start(b2s[:], spread(a["L2_ffn_fc2_b"])).then_inc(ld, 16)

                @block.tensor
                def _(pe):
                    for u in range(U):
                        pe.wait_ge(made, u + 1)
                        if u >= 2:
                            pe.wait_ge(kept, u - 1)
                        for k in range(2):
                            last = nc.tensor.transpose(bank[:, u % 2, k * P:(k + 1) * P], low[:, u, 0, k * 128:(k + 1) * 128], ident[0:P, 0:P])
                        last.then_inc(turned, 1)
                    pe.wait_ge(kept, U)
                    pe.wait_ge(ld, 80)
                    g = 0
                    for lhs, rhs, k_n, m_n in ((wi, llT, 2, K), (w1s, upT, K, F)):
                        if m_n == F:
                            pe.wait_ge(mm_kept, g)
                        for c0, cn in C2:
                            for m in range(m_n):
                                if g >= 2:
                                    pe.wait_ge(mm_kept, g - 1)
                                for k in range(k_n):
                                    last = nc.tensor.matmul(bank[:, 2 + g % 2, 0:cn], lhs[:, k, m * 128:(m + 1) * 128], rhs[:, k, c0:c0 + cn], start=(k == 0), stop=(k == k_n - 1))
                                last.then_inc(mm, 1)
                                g += 1
                    pe.wait_ge(mm_kept, g)
                    for u in range(U):
                        if u >= 2:
                            pe.wait_ge(moved, u - 1)
                        for k in range(F):
                            last = nc.tensor.matmul(bank[0:P, 4 + u % 2, 0:W2], hT[:, k, u * P:(u + 1) * P], w2s[:, k, :], start=(k == 0), stop=(k == F - 1))
                        last.then_inc(last_made, 1)

                @block.scalar
                def _(act):
                    act.wait_ge(ld, 80)
                    for u in range(U):
                        act.wait_ge(turned, u + 1)
                        nc.scalar.copy(llT[:, :, u * P:(u + 1) * P], bank[:, u % 2, 0:2 * P].rearrange("p (k n) -> p k n", k=2)).then_inc(kept, 1)
                    g = 0
                    for dst, m_n in ((upT, K), (hT, F)):
                        for c0, cn in C2:
                            for m in range(m_n):
                                act.wait_ge(mm, g + 1)
                                if dst is upT:
                                    nc.scalar.copy(dst[:, m, c0:c0 + cn], bank[:, 2 + g % 2, 0:cn]).then_inc(mm_kept, 1)
                                else:
                                    nc.scalar.activation(dst[:, m, c0:c0 + cn], bank[:, 2 + g % 2, 0:cn], ACT.Gelu, bias=b1s[:, m:m + 1]).then_inc(mm_kept, 1)
                                g += 1

                @block.vector
                def _(dve):
                    v = [0]

                    def chain(ins):
                        v[0] += 1
                        ins.then_inc(step, 1)
                        dve.wait_ge(step, v[0])

                    def half_sum(out, p_, q_, op):
                        return nc.vector.tensor_tensor(out, p_, q_, op)

                    for u in range(U):
                        nc.vector.tensor_tensor(sums[:, u], pairs[:, u, 0], pairs[:, u, 1], ALU.add).then_inc(step, 1)
                        nc.vector.tensor_tensor(difs[:, u], pairs[:, u, 0], pairs[:, u, 1], ALU.subtract).then_inc(step, 1)
                        v[0] += 2
                        dve.wait_ge(step, v[0])
                        s2 = sums[:, u].rearrange("p (w e) -> p e w", e=2)
                        d2 = difs[:, u].rearrange("p (w e) -> p e w", e=2)
                        for i, (q, op) in enumerate(((s2, ALU.add), (d2, ALU.add), (s2, ALU.subtract), (d2, ALU.subtract))):
                            last = nc.vector.tensor_tensor(low[:, u, i], q[:, 0], q[:, 1], op)
                        chain(last)
                        nc.vector.tensor_scalar(low[:, u].rearrange("p i w -> p (i w)"), low[:, u].rearrange("p i w -> p (i w)"), 0.5, None, ALU.mult).then_inc(made, 1)
                    dve.wait_ge(ld, 80)
                    dve.wait_ge(made, U)
                    for u in range(U):
                        dve.wait_ge(last_made, u + 1)
                        nc.vector.tensor_tensor(nl[:, u % 2], bank[0:P, 4 + u % 2, 0:W2], b2s[:], ALU.add).then_inc(moved, 1)
                        dve.wait_ge(moved, u + 1)
                        nc.vector.tensor_tensor(o[:, 0], nl[:, u % 2], low[:, u, 1], ALU.add)
                        nc.vector.tensor_tensor(o[:, 1], nl[:, u % 2], low[:, u, 1], ALU.subtract)
                        nc.vector.tensor_tensor(o[:, 2], low[:, u, 2], low[:, u, 3], ALU.add)
                        chain(nc.vector.tensor_tensor(o[:, 3], low[:, u, 2], low[:, u, 3], ALU.subtract))
                        for r in range(2):
                            nc.vector.tensor_tensor(o[:, 4], o[:, r], o[:, 2 + r], ALU.add)
                            chain(nc.vector.tensor_tensor(o[:, 5], o[:, r], o[:, 2 + r], ALU.subtract))
                            for e in range(2):
                                to = xp[:, u, r].rearrange("p (w e) -> p e w", e=2)[:, e]
                                last = nc.vector.scalar_tensor_tensor(to, o[:, 4 + e], 0.5, to, ALU.mult, ALU.add)
                            chain(last)

        def scale_rows(pmax):
            s = sem("scaled")
            with nc.Block() as block:
                @block.vector
                def _(dve):
                    for t in range(T):
                        nc.vector.tensor_scalar(xn[:, t], xn[:, t], pmax[:, t:t + 1], None, ALU.mult).then_inc(s, 1)
                    nc.vector.memset(y_out[:], 0.0)

        def reorder(oh):
            f = sb("f", [P, 8, T, NX], F32, c)
            pos = sb("pos", [P, T], F32, c)
            pos_i = sb("pos_i", [P, T], I32, c)
            got = sb("got", [P, T, D], F32, c)
            counted, step, ready, put, back, added, stored = (sem(n) for n in ("counted", "step", "pos_ready", "rows_put", "rows_back", "added", "stored"))
            put = dma_sem("rows_put")
            with nc.Block() as block:
                @block.tensor
                def _(pe):
                    v = oh[:].rearrange("p t e -> p (t e)")
                    nc.tensor.matmul(bank[0:P, 0, 0:T * NX], above[0:P, 0:P], v, start=True, stop=True)
                    nc.tensor.matmul(bank[0:P, 1, 0:T * NX], ones[0:P, 0:P], v, start=True, stop=True).then_inc(counted, 1)

                @block.vector
                def _(dve):
                    v = [0]

                    def chain(ins):
                        v[0] += 1
                        ins.then_inc(step, 1)
                        dve.wait_ge(step, v[0])

                    dve.wait_ge(counted, 1)
                    nc.vector.tensor_copy(f[:, 0].rearrange("p t e -> p (t e)"), bank[0:P, 0, 0:T * NX])
                    chain(nc.vector.tensor_copy(f[:, 1].rearrange("p t e -> p (t e)"), bank[0:P, 1, 0:T * NX]))
                    for e in range(NX):
                        last = nc.vector.tensor_tensor_scan(f[:, 2, :, e], ones[0:P, 0:T], f[:, 1, :, e], 0.0, ALU.mult, ALU.add)
                    chain(last)
                    chain(nc.vector.tensor_tensor_scan(f[:, 3, 0, :], ones[0:P, 0:NX], f[:, 2, T - 1, :], 0.0, ALU.mult, ALU.add))
                    chain(nc.vector.tensor_tensor(f[:, 3, 1, :], f[:, 3, 0, :], f[:, 2, T - 1, :], ALU.subtract))
                    chain(nc.vector.tensor_tensor(f[:, 4], f[:, 2], f[:, 1], ALU.subtract))
                    chain(nc.vector.tensor_tensor(f[:, 4], f[:, 4], f[:, 0], ALU.add))
                    chain(nc.vector.tensor_tensor(f[:, 4], f[:, 4], f[:, 3, 1, :].unsqueeze(1).to_broadcast([P, T, NX]), ALU.add))
                    chain(nc.vector.tensor_tensor(f[:, 4], f[:, 4], oh[:], ALU.mult))
                    chain(nc.vector.tensor_reduce(pos[:], f[:, 4], X, ALU.add))
                    nc.vector.tensor_copy(pos_i[:], pos[:]).then_inc(ready, 1)
                    for t in range(T):
                        dve.wait_ge(back, 16 * T)
                        nc.vector.tensor_tensor(x[:, t], x[:, t], got[:, t], ALU.add).then_inc(added, 1)

                @block.gpsimd
                def _(pool):
                    pool.wait_ge(ready, 1)
                    for t in range(T):
                        nc.gpsimd.indirect_dma_start(out=y_dram, out_offset=bass.IndirectOffsetOnAxis(ap=pos_i[:, t:t + 1], axis=0),
                                                     in_=y_out[:, t, :], in_offset=None).then_inc(put, 16)
                    pool.wait_ge(put, 16 * T)

                @block.sync
                def _(sp):
                    sp.wait_ge(put, 16 * T)
                    for t in range(T):
                        sp.dma_start(got[:, t], y_dram[t * P:(t + 1) * P, :]).then_inc(back, 16)
                    for t in range(T):
                        sp.wait_ge(added, t + 1)
                        sp.dma_start(out[t * P:(t + 1) * P, :], x[:, t]).then_inc(stored, 16)
                    sp.wait_ge(stored, 16 * T)

        def run(stage, *args, **kw):
            nonlocal c
            with ExitStack() as c:
                stage(*args, **kw)
            for s in cleared_sems:
                nc.release_semaphore(s)
            for s in sems:
                nc.gpsimd.sem_clear(s)
            cleared_sems[:] = sems
            sems.clear()

        c = None
        run(constants)
        run(sort_edges)
        run(count_matrix)
        if last == -1:
            return x, dict(A=A_dram, table=table)
        gate = sb("gate", [P, T, NX])
        pmax = sb("pmax", [P, T])
        none = dict()
        run(norm, x, xn)
        run(gcn)
        if last == 0:
            return x, none
        run(norm, x, xn)
        run(route, "L0_ffn_router_w", None, gate, "two")
        run(experts, "L0_ffn_w1", "L0_ffn_b1", "L0_ffn_w2", "L0_ffn_b2", gate, ACT.Gelu, x)
        if last == 1:
            return x, none
        run(norm, x, xn)
        run(edge_attention)
        run(turn_rows, xn)
        run(project, xT, K, a["L1_gnn_Wo"], a["L1_gnn_bo"], x)
        if last == 2:
            return x, none
        run(norm, x, xn)
        run(full_attention)
        run(project, xT, K, a["L1_ffn_Wo"], a["L1_ffn_bo"], xn)
        run(norm, xn, xn, "L1_ffn_g1", "L1_ffn_beta1")
        run(route, "L1_ffn_Wg", "L1_ffn_bg", gate, "one")
        run(experts, "L1_ffn_W1", "L1_ffn_b1", "L1_ffn_W2", "L1_ffn_b2", gate, ACT.Gelu, xn)
        run(norm, xn, xn, "L1_ffn_g2", "L1_ffn_beta2", False, False, x)
        if last == 3:
            return x, none
        run(norm, x, xn)
        run(mean_layer, a["L2_gnn_W"][0:D, :], a["L2_gnn_W"][D:2 * D, :], a["L2_gnn_b"], True, x)
        if last == 4:
            return x, none
        run(to_pairs)
        run(norm, x, xn, None, None, False)
        run(wavelet)
        run(from_pairs)
        if last == 5:
            return x, none
        run(norm, x, xn)
        run(mean_layer, a["L3_gnn_w_self"], a["L3_gnn_w_neigh"], a["L3_gnn_bias"], False, xn)
        run(norm, xn, xn, "L3_gnn_gamma", "L3_gnn_beta", False, True, x)
        if last == 6:
            return x, none
        run(norm, x, xn)
        run(route, "L3_ffn_Wg", "L3_ffn_bg", gate, "one", pmax)
        y_out = sb("y_out", [P, T, D])
        run(scale_rows, pmax)
        run(turn_rows, xn)
        run(experts, "L3_ffn_W1", "L3_ffn_b1", "L3_ffn_W2", "L3_ffn_b2", gate, ACT.Relu, y_out)
        run(reorder, gate)



def stretch_matrix():
    import numpy as np
    n, m = D // 2, D
    pos = np.linspace(0.0, 1.0, m, dtype=np.float32) * np.float32(n - 1)
    i0 = np.clip(np.floor(pos).astype(np.int32), 0, n - 2)
    w = pos - i0.astype(np.float32)
    out = np.zeros((n, m), np.float32)
    out[i0, np.arange(m)] = np.float32(1.0) - w
    out[i0 + 1, np.arange(m)] = w
    return out


def lay_out(inputs):
    import numpy as np
    arrays = {k: np.ascontiguousarray(np.asarray(v)) for k, v in inputs.items()}
    for name, axes in (("L0_ffn_router_w", (1, 0)), ("L0_ffn_w1", (0, 2, 1)), ("L0_ffn_w2", (0, 2, 1)),
                       ("L2_ffn_fc1_w", (1, 0)), ("L2_ffn_fc2_w", (1, 0)), ("L3_gnn_w_self", (1, 0)), ("L3_gnn_w_neigh", (1, 0))):
        arrays[name] = np.ascontiguousarray(arrays[name].transpose(axes))
    arrays["stretch"] = stretch_matrix()
    return arrays


def kernel(**inputs):
    import numpy as np
    import concourse.bacc as bacc
    from concourse.bass_utils import run_bass_kernel_spmd

    nc = bacc.Bacc("TRN2", target_bir_lowering=False, num_devices=1)
    arrays, views = {}, {}
    for name, array in lay_out(inputs).items():
        arrays[f"in_{name}_dram"] = array
        views[name] = nc.dram_tensor(f"in_{name}_dram", array.shape, mybir.dt.from_np(array.dtype), kind="ExternalInput").ap()
    out = nc.dram_tensor("out_0_dram", (N, D), F32, kind="ExternalOutput").ap()
    build(nc, views, out)
    result = run_bass_kernel_spmd(nc, [arrays], core_ids=[0])
    return np.asarray(result.results[0]["out_0_dram"])
```

```python
from contextlib import ExitStack

import concourse.bass as bass
from concourse import mybir

F32 = mybir.dt.float32
BF16 = mybir.dt.bfloat16
I32 = mybir.dt.int32
ALU = mybir.AluOpType
ACT = mybir.ActivationFunctionType
X = mybir.AxisListType.X

N, D = 1250, 512
P = 125
T = N // P
K = D // 128
E = 20000
EC = E // P
S = 128
S2 = 2 * S
G = 4
PAIRS = (E + T * (S2 - 1)) // S2
SC = 2 * PAIRS
assert SC % (2 * G) == 0
MAGIC = 1.5 * 2.0 ** 23
ROWS = S * SC
RW = 11
H, DH = 8, 64
NX = 8
FF = 256
SLOT_TILES = 28
NEG = -1.0e30
COLS = [(0, 500), (500, 500), (1000, 250)]
LAST = 99


def build(nc, a, out, last=LAST):
    ctx = ExitStack()
    names = iter(range(10000))
    sems, cleared_sems = [], []

    def sb(name, shape, dt=F32, c=None):
        return (c or ctx).enter_context(nc.sbuf_tensor(f"{name}_{next(names)}", shape, dt))

    def dma_sem(name):
        return nc.alloc_semaphore(f"{name}_{next(names)}")

    def sem(name):
        sems.append(nc.alloc_semaphore(f"{name}_{next(names)}"))
        return sems[-1]

    def dram(name, shape, dt=F32):
        return nc.dram_tensor(name, shape, dt).ap()

    def row(v):
        return v.rearrange("(a n) -> a n", a=1)

    def spread(v, p=P):
        return v.partition_broadcast(p)

    with ctx:
        bank = ctx.enter_context(nc.psum_tensor("bank", [128, 8, 512], F32))
        x = sb("x", [P, T, D])
        xn = sb("xn", [P, T, D])
        xT = sb("xT", [128, K, N])
        ident = sb("ident", [128, 128])
        ones = sb("ones", [128, 128])
        below = sb("below", [128, 128])
        above = sb("above", [128, 128])
        iota = sb("iota", [128, N])
        lane = sb("lane", [128, 1])
        i8 = sb("i8", [P, NX])
        dinv = sb("dinv", [P, T])
        rdeg = sb("rdeg", [P, T])
        last_row = sb("last_row", [P, T], I32)
        bounds = sb("bounds", [1, T + 1], I32)

        A_dram = dram("count_matrix", (P, T, N))
        table = dram("edge_table", (ROWS, RW))
        k_dram = dram("k_rows", (N, D))
        v_dram = dram("v_rows", (N, D))
        run_dram = dram("running_max", (ROWS, H))
        x_dram = dram("x_rows", (N, D))
        y_dram = dram("y_rows", (N, D))
        x_slots = dram("x_slots", (SLOT_TILES * 128, D))
        y_slots = dram("y_slots", (SLOT_TILES * 128, D))
        key_dram = dram("edge_keys", (2, E))

        def constants():
            iota_i = sb("iota_i", [128, N], I32, c)
            lane_i = sb("lane_i", [128, 1], I32, c)
            loaded, made, filled, masked = sem("x_loaded"), sem("iotas_made"), sem("ones_filled"), sem("masks_made")
            with nc.Block() as block:
                @block.sync
                def _(sp):
                    sp.dma_start(x[:], a["x"].rearrange("(t p) d -> p t d", p=P)).then_inc(loaded, 16)
                    sp.wait_ge(loaded, 16)

                @block.gpsimd
                def _(pool):
                    nc.gpsimd.iota(iota_i[:], [[1, N]], base=0, channel_multiplier=0).then_inc(made, 1)
                    nc.gpsimd.iota(lane_i[:], [[0, 1]], base=0, channel_multiplier=1).then_inc(made, 1)
                    nc.gpsimd.memset(ones[:], 1.0).then_inc(filled, 1)
                    pool.wait_ge(filled, 1)
                    for m, op, sign in ((ident, ALU.is_equal, 1), (below, ALU.is_gt, 1), (above, ALU.is_gt, -1)):
                        nc.gpsimd.affine_select(out=m[:], in_=ones[:], compare_op=op, fill=0.0, base=0,
                                                pattern=[[-sign, 128]], channel_multiplier=sign).then_inc(masked, 1)
                    pool.wait_ge(masked, 3)

                @block.vector
                def _(dve):
                    dve.wait_ge(made, 2)
                    nc.vector.tensor_copy(iota[:], iota_i[:]).then_inc(made, 1)
                    nc.vector.tensor_copy(lane[:], lane_i[:]).then_inc(made, 1)
                    dve.wait_ge(made, 4)
                    nc.vector.tensor_scalar(i8[:], iota[:P, 0:NX], float(NX), None, ALU.subtract).then_inc(made, 1)
                    dve.wait_ge(made, 5)

        def sort_edges():
            G = 8
            NB = EC // G
            start = sb("start", [P, T], F32, c)
            cnt = sb("cnt", [P, T], F32, c)
            cols_i = sb("cols_i", [128, 2, 2 * P], I32, c)
            cols_f = sb("cols_f", [128, 2, 2 * P], F32, c)
            rec = sb("rec", [P, EC, RW], F32, c)
            edge_j = sb("edge_j", [P, EC], F32, c)
            edge_t = sb("edge_t", [P, EC], F32, c)
            oht = sb("oht", [P, EC, T], F32, c)
            ohj = sb("ohj", [P, 2, G, P], F32, c)
            tiles = sb("tiles", [P, T], F32, c)
            hist = sb("hist", [P, EC, T], F32, c)
            cum = sb("cum", [P, T, EC], F32, c)
            one_row = sb("one_row", [P, EC], F32, c)
            tot = sb("tot", [P, 5, T], F32, c)
            fill = sb("fill", [S, SC, RW], F32, c)
            blank = sb("blank", [128, 2, D], F32, c)
            cols_j = sb("cols_j", [128, 2, 2 * P], F32, c)
            row = sb("row", [P, 2, 2, G * P], F32, c)
            ohjT = sb("ohjT", [P, 2, G, P], F32, c)
            same = sb("same", [P, G, P], F32, c)
            earlier = sb("earlier", [P, G, P], F32, c)
            part = sb("part", [P, G, T], F32, c)
            pos = sb("pos", [P, 2, EC], F32, c)
            lo = sb("lo", [P, EC], F32, c)
            pos_i = sb("pos_i", [P, EC], I32, c)
            ld, ld_attr, turned, step = sem("edges_loaded"), sem("attr_loaded"), sem("edges_turned"), sem("dve_step")
            ohj_made, hist_made, hist_kept = sem("ohj_made"), sem("hist_made"), sem("hist_kept")
            base_made, row_free = sem("base_made"), sem("row_free")
            row_ld = [sem(f"row_loaded{h}") for h in range(2)]
            ohjT_made, looked, taken = sem("ohjT_made"), sem("looked_up"), sem("lookup_taken")
            null_made, null_put, put, ready = sem("null_made"), sem("null_put"), dma_sem("record_put"), sem("pos_ready")
            keys_made, keys_put = sem("keys_made"), sem("keys_put")
            blank_made, blank_put = sem("blank_made"), sem("blank_put")
            with nc.Block() as block:
                @block.sync
                def _(sp):
                    for i, name in enumerate(("src", "dst")):
                        v = a[name].rearrange("(c p) -> c p", p=P)
                        sp.dma_start(cols_i[:, i, 0:P], v[0:128, :]).then_inc(ld, 16)
                        sp.dma_start(cols_i[0:EC - 128, i, P:2 * P], v[128:EC, :]).then_inc(ld, 16)
                    sp.dma_start(rec[:, :, 2:2 + H], a["edge_attr_8"].rearrange("(c p) h -> p c h", p=P)).then_inc(ld_attr, 16)
                    sp.wait_ge(null_made, 2)
                    sp.dma_start(table.rearrange("(p c) w -> p c w", p=S), fill[:]).then_inc(null_put, 16)
                    sp.wait_ge(keys_made, 1)
                    for i, keys in enumerate((cols_f[:, 0], cols_j[:, 1])):
                        v = key_dram[i, :].rearrange("(c p) -> c p", p=P)
                        sp.dma_start(v[0:128, :], keys[:, 0:P]).then_inc(keys_put, 16)
                        sp.dma_start(v[128:EC, :], keys[0:EC - 128, P:2 * P]).then_inc(keys_put, 16)
                    sp.wait_ge(keys_put, 64)
                    v = key_dram.rearrange("k (a n) -> k a n", n=G * P)
                    with sp.Fori(0, NB // 2) as b:
                        for h in range(2):
                            sp.wait_ge(row_free, b * 2 + (h + 1))
                            sp.dma_start(row[:, h], v[:, bass.ds(b * 2 + h, 1), :].rearrange("k a n -> k (a n)").partition_broadcast(P)).then_inc(row_ld[h], 16)
                    sp.wait_ge(blank_made, 1)
                    v = x_slots.rearrange("(n u p) d -> n p u d", u=2, p=128)
                    for n in range(SLOT_TILES // 2):
                        sp.dma_start(v[n], blank[:]).then_inc(blank_put, 16)
                    sp.wait_ge(blank_put, 8 * SLOT_TILES)

                @block.gpsimd
                def _(pool):
                    nc.gpsimd.memset(blank[:], 0.0).then_inc(blank_made, 1)
                    nc.gpsimd.memset(fill[:], 0.0).then_inc(null_made, 1)
                    pool.wait_ge(null_made, 1)
                    nc.gpsimd.memset(fill[:, :, RW - 1:RW], -1.0)
                    nc.gpsimd.memset(fill[:, :, 0:1], -1.0).then_inc(null_made, 1)
                    pool.wait_ge(ready, 1)
                    pool.wait_ge(null_put, 16)
                    pool.wait_ge(ld_attr, 16)
                    for n in range(EC):
                        nc.gpsimd.indirect_dma_start(
                            out=table, out_offset=bass.IndirectOffsetOnAxis(ap=pos_i[:, n:n + 1], axis=0),
                            in_=rec[:, n, :], in_offset=None).then_inc(put, 16)
                    pool.wait_ge(put, 16 * EC)

                @block.tensor
                def _(pe):
                    pe.wait_ge(step, 2)
                    for i in range(2):
                        nc.tensor.transpose(bank[0:P, i, 0:128], cols_f[:, i, 0:P], ident[:])
                        last = nc.tensor.transpose(bank[0:P, i, 128:EC], cols_f[0:EC - 128, i, P:2 * P], ident[0:EC - 128, 0:EC - 128])
                    last.then_inc(turned, 1)
                    with pe.Fori(0, NB // 2) as b:
                        for h in range(2):
                            pe.wait_ge(ohj_made, b * 2 + h + 1)
                            pe.wait_ge(hist_kept, b * 2 + (h + 1))
                            for g in range(G):
                                last = nc.tensor.matmul(bank[0:P, 2, g * T:(g + 1) * T], ohj[:, h, g, :],
                                                        oht[:, bass.ds(b * (2 * G) + (h * G + g), 1), :].rearrange("p a t -> p (a t)"), start=True, stop=True)
                            last.then_inc(hist_made, 1)
                    pe.wait_ge(base_made, 1)
                    nc.tensor.matmul(bank[0:P, 0, 0:T], above[0:P, 0:P], cnt[:], start=True, stop=True)
                    nc.tensor.matmul(bank[0:P, 0, T:2 * T], ones[0:P, 0:P], cnt[:], start=True, stop=True).then_inc(base_made, 1)
                    with pe.Fori(0, NB // 2) as b:
                        for h in range(2):
                            pe.wait_ge(ohjT_made, b * 2 + h + 1)
                            pe.wait_ge(taken, b * 2 + (h + 1))
                            for g in range(G):
                                last = nc.tensor.matmul(bank[0:P, 3, g * T:(g + 1) * T], ohjT[:, h, g, :],
                                                        hist[:, bass.ds(b * (2 * G) + (h * G + g), 1), :].rearrange("p a t -> p (a t)"), start=True, stop=True)
                            last.then_inc(looked, 1)

                @block.scalar
                def _(act):
                    act.sem_inc(hist_kept, 1)
                    with act.Fori(0, NB) as b:
                        act.wait_ge(hist_made, b + 1)
                        nc.scalar.copy(hist[:, bass.ds(b * G, G), :].rearrange("p c t -> p (c t)"), bank[0:P, 2, 0:G * T]).then_inc(hist_kept, 1)

                @block.vector
                def _(dve):
                    v = [0]

                    def chain(ins):
                        v[0] += 1
                        ins.then_inc(step, 1)
                        dve.wait_ge(step, v[0])

                    for s in (row_free, row_free, taken):
                        dve.sem_inc(s, 1)
                    dve.wait_ge(ld, 64)
                    nc.vector.memset(one_row[:], 1.0)
                    nc.vector.tensor_scalar(tiles[:], iota[0:P, 0:T], float(P), None, ALU.mult)
                    chain(nc.vector.memset(cols_f[:], 0.0))
                    nc.vector.tensor_copy(cols_f[:, :, 0:P], cols_i[:, :, 0:P])
                    chain(nc.vector.tensor_copy(cols_f[0:EC - 128, :, P:2 * P], cols_i[0:EC - 128, :, P:2 * P]))
                    def within(out, q, v, n):
                        chain(nc.vector.tensor_scalar(q, v, -(n - 1) / 2, 1.0 / n, ALU.add, ALU.mult))
                        chain(nc.vector.tensor_scalar(q, q, MAGIC, MAGIC, ALU.add, ALU.subtract))
                        chain(nc.vector.scalar_tensor_tensor(out, q, -float(n), v, ALU.mult, ALU.add))

                    within(cols_j[:, 1], cols_j[:, 0], cols_f[:, 0], P)
                    nc.vector.tensor_copy(lo[:, 0:1], lane[0:P]).then_inc(keys_made, 1)
                    dve.wait_ge(turned, 1)
                    nc.vector.tensor_copy(rec[:, :, RW - 1:RW].rearrange("p c a -> p (c a)"), bank[0:P, 0, 0:EC])
                    chain(nc.vector.tensor_copy(rec[:, :, 1:2].rearrange("p c a -> p (c a)"), bank[0:P, 1, 0:EC]))
                    srcf = rec[:, :, RW - 1:RW].rearrange("p c a -> p (c a)")
                    within(edge_j[:], edge_t[:], srcf, P)
                    nc.vector.tensor_copy(rec[:, :, 0:1].rearrange("p c a -> p (c a)"), edge_j[:])
                    chain(nc.vector.tensor_tensor(edge_t[:], srcf, edge_j[:], ALU.subtract))
                    chain(nc.vector.tensor_tensor(oht[:], edge_t[:].unsqueeze(2).to_broadcast([P, EC, T]),
                                                  tiles[:].unsqueeze(1).to_broadcast([P, EC, T]), ALU.is_equal))
                    with dve.Fori(0, NB // 2) as b:
                        for h in range(2):
                            if h == 0:
                                dve.wait_ge(hist_kept, b * 2 + 1)
                            nc.vector.tensor_tensor(ohj[:, h], iota[0:P, 0:P].unsqueeze(1).to_broadcast([P, G, P]),
                                                    edge_j[:, bass.ds(b * (2 * G) + h * G, G)].unsqueeze(2).to_broadcast([P, G, P]),
                                                    ALU.is_equal).then_inc(ohj_made, 1)
                    dve.wait_ge(hist_kept, NB + 1)
                    for t in range(T):
                        last = nc.vector.tensor_tensor_scan(cum[:, t, :], one_row[:], hist[:, :, t], 0.0, ALU.mult, ALU.add)
                    chain(last)
                    chain(nc.vector.tensor_copy(cnt[:], cum[:, :, EC - 1]))
                    nc.vector.tensor_copy(tot[:, 4], cnt[:]).then_inc(base_made, 1)
                    dve.wait_ge(base_made, 2)
                    chain(nc.vector.tensor_scalar(tot[:, 0], bank[0:P, 0, T:2 * T], 1.0, float(S2 - 1), ALU.max, ALU.add))
                    within(tot[:, 2], tot[:, 1], tot[:, 0], S2)
                    chain(nc.vector.tensor_tensor(tot[:, 0], tot[:, 0], tot[:, 2], ALU.subtract))
                    chain(nc.vector.tensor_tensor_scan(tot[:, 1], one_row[:, 0:T], tot[:, 0], 0.0, ALU.mult, ALU.add))
                    chain(nc.vector.tensor_tensor(tot[:, 2], tot[:, 1], tot[:, 0], ALU.subtract))
                    chain(nc.vector.tensor_tensor(start[:], tot[:, 2], bank[0:P, 0, 0:T], ALU.add))
                    chain(nc.vector.tensor_scalar(tot[:, 3], tot[:, 1], 1.0 / S2, None, ALU.mult))
                    chain(nc.vector.memset(tot[:, 3, T - 1:T], float(PAIRS)))
                    chain(nc.vector.memset(bounds[:], 0))
                    chain(nc.vector.tensor_copy(bounds[0:1, 1:T + 1], tot[0:1, 3, :]))
                    chain(nc.vector.tensor_tensor(tot[:, 0], start[:], cnt[:], ALU.add))
                    chain(nc.vector.tensor_scalar(tot[:, 0], tot[:, 0], -1.0, 0.0, ALU.add, ALU.max))
                    within(tot[:, 2], tot[:, 1], tot[:, 0], S)
                    chain(nc.vector.scalar_tensor_tensor(tot[:, 0], tot[:, 2], float(SC), tot[:, 1], ALU.mult, ALU.add))
                    chain(nc.vector.tensor_copy(last_row[:], tot[:, 0]))
                    cumv = cum[:].rearrange("p t c -> p c t")
                    chain(nc.vector.tensor_tensor(hist[:], cumv, hist[:], ALU.subtract))
                    chain(nc.vector.tensor_tensor(hist[:], hist[:], start[:].unsqueeze(1).to_broadcast([P, EC, T]), ALU.add))
                    first = v[0]
                    with dve.Fori(0, NB // 2) as b:
                        for h in range(2):
                            n = b * 2 + h
                            dve.wait_ge(row_ld[h], b * 16 + 16)
                            nc.vector.tensor_scalar(ohjT[:, h].rearrange("p g e -> p (g e)"), row[:, h, 1], lane[0:P], None, ALU.is_equal).then_inc(ohjT_made, 1)
                            nc.vector.tensor_tensor(same[:], row[:, h, 0].rearrange("p (g e) -> p g e", g=G),
                                                    rec[:, bass.ds(n * G, G), RW - 1:RW].to_broadcast([P, G, P]), ALU.is_equal).then_inc(row_free, 1)
                            dve.wait_ge(row_free, n + 3)
                            nc.vector.tensor_tensor(earlier[:], same[:], below[0:P, 0:P].unsqueeze(1).to_broadcast([P, G, P]), ALU.mult).then_inc(step, 1)
                            dve.wait_ge(step, n * 3 + (first + 1))
                            nc.vector.tensor_reduce(pos[:, 0, bass.ds(n * G, G)], earlier[:], X, ALU.add).then_inc(step, 1)
                            dve.wait_ge(looked, n + 1)
                            nc.vector.tensor_tensor(part[:], bank[0:P, 3, 0:G * T].rearrange("p (g t) -> p g t", g=G),
                                                    oht[:, bass.ds(n * G, G), :], ALU.mult).then_inc(taken, 1)
                            dve.wait_ge(taken, n + 2)
                            nc.vector.tensor_reduce(pos[:, 1, bass.ds(n * G, G)], part[:], X, ALU.add).then_inc(step, 1)
                    v[0] = first + 3 * NB
                    dve.wait_ge(step, v[0])
                    chain(nc.vector.tensor_tensor(pos[:, 0], pos[:, 0], pos[:, 1], ALU.add))
                    within(lo[:], edge_t[:], pos[:, 0], S)
                    chain(nc.vector.scalar_tensor_tensor(pos[:, 1], lo[:], float(SC), edge_t[:], ALU.mult, ALU.add))
                    nc.vector.tensor_copy(pos_i[:], pos[:, 1]).then_inc(ready, 1)
                    dve.wait_ge(ready, 1)

        def count_matrix():
            recs = sb("recs", [S, SC, RW], F32, c)
            Asb = sb("A", [P, T, N], F32, c)
            w = sb("w", [S, 2, P], BF16, c)
            hot = sb("hot", [S, 2, N], BF16, c)
            zero = sb("zero", [S, 512], BF16, c)
            one = sb("one", [P, 2], F32, c)
            deg = sb("deg", [P, 3, T], F32, c)
            ld, zeroed, w_made, hot_made = (sem(n) for n in ("recs_loaded", "zeroed", "w_made", "hot_made"))
            used = [sem(f"hot_used{h}") for h in range(2)]
            tile_done, tile_kept, stored, degs, step = (sem(n) for n in ("tile_done", "tile_kept", "A_stored", "deg_made", "deg_step"))
            with nc.Block() as block:
                @block.sync
                def _(sp):
                    sp.dma_start(recs[:], table.rearrange("(p c) w -> p c w", p=S)).then_inc(ld, 16)
                    for t in range(T):
                        sp.wait_ge(tile_kept, t + 1)
                        sp.dma_start(A_dram[:, t, :], Asb[:, t, :]).then_inc(stored, 16)
                    sp.wait_ge(stored, 16 * T)

                @block.vector
                def _(dve):
                    nc.vector.memset(one[:], 1.0)
                    nc.vector.memset(zero[:], 0.0).then_inc(zeroed, 1)
                    dve.wait_ge(ld, 16)
                    with dve.Fori(0, PAIRS) as n:
                        for h in range(2):
                            dve.wait_ge(used[h], n + 1)
                            nc.vector.tensor_scalar(w[:, h], iota[:, 0:P], recs[:, bass.ds(n * 2 + h, 1), 0:1].rearrange("p a b -> p (a b)"), None, ALU.is_equal).then_inc(w_made, 1)
                            nc.vector.tensor_scalar(hot[:, h], iota[:], recs[:, bass.ds(n * 2 + h, 1), 1:2].rearrange("p a b -> p (a b)"), None, ALU.is_equal).then_inc(hot_made, 1)
                    dve.wait_ge(degs, 1)
                    nc.vector.tensor_scalar(deg[:, 0], bank[0:P, 6, 0:T], 1.0, None, ALU.max).then_inc(step, 1)
                    nc.vector.tensor_scalar(deg[:, 1], bank[0:P, 6, 0:T], 1.0, None, ALU.add).then_inc(step, 1)
                    dve.wait_ge(step, 3)
                    nc.vector.reciprocal(rdeg[:], deg[:, 0]).then_inc(step, 1)
                    nc.vector.reciprocal(dinv[:], deg[:, 2]).then_inc(step, 1)
                    dve.wait_ge(step, 5)

                @block.tensor
                def _(pe):
                    for s in used:
                        pe.sem_inc(s, 1)
                    pe.wait_ge(zeroed, 1)
                    for t in range(T):
                        if t >= 2:
                            pe.wait_ge(tile_kept, t - 1)
                        lo = pe.value_load(bounds[0:1, t:t + 1], min_val=0, max_val=PAIRS - 1)
                        hi = pe.value_load(bounds[0:1, t + 1:t + 2], min_val=1, max_val=PAIRS)
                        for j, (c0, cn) in enumerate(COLS):
                            nc.tensor.matmul(bank[0:P, 3 * (t % 2) + j, 0:cn], zero[:, 0:P], zero[:, 0:cn], start=True, stop=False, skip_group_check=True)
                        with pe.Fori(lo, hi) as n:
                            for h in range(2):
                                pe.wait_ge(w_made, n * 2 + (h + 1))
                                pe.wait_ge(hot_made, n * 2 + (h + 1))
                                for j, (c0, cn) in enumerate(COLS):
                                    last = nc.tensor.matmul(bank[0:P, 3 * (t % 2) + j, 0:cn], w[:, h], hot[:, h, c0:c0 + cn], start=False, stop=False, skip_group_check=True)
                                last.then_inc(used[h], 1)
                        for j, (c0, cn) in enumerate(COLS):
                            last = nc.tensor.matmul(bank[0:P, 3 * (t % 2) + j, 0:cn], zero[:, 0:P], zero[:, 0:cn], start=False, stop=True, skip_group_check=True)
                        last.then_inc(tile_done, 1)
                    pe.wait_ge(tile_kept, T)
                    for d in range(T):
                        for s in range(T):
                            last = nc.tensor.matmul(bank[0:P, 6, d:d + 1], Asb[:, s, d * P:(d + 1) * P], one[:, 0:1], start=(s == 0), stop=(s == T - 1))
                    last.then_inc(degs, 1)

                @block.scalar
                def _(act):
                    for t in range(T):
                        act.wait_ge(tile_done, t + 1)
                        for j, (c0, cn) in enumerate(COLS):
                            last = nc.scalar.copy(Asb[:, t, c0:c0 + cn], bank[0:P, 3 * (t % 2) + j, 0:cn])
                        last.then_inc(tile_kept, 1)
                    act.wait_ge(step, 2)
                    nc.scalar.activation(deg[:, 2], deg[:, 1], ACT.Sqrt).then_inc(step, 1)

        def norm(src, dst, scale=None, shift=None, turn=True, relu=False, add_to=None):
            stats = sb("stats", [P, T, 6], F32, c)
            mv = sb("mv", [P, T, 2], F32, c)
            std = sb("std", [P, 3, T], F32, c)
            gb = sb("gb", [P, 2, D], F32, c)
            counted, merged, var_made, std_made, rstd_made = (sem(n) for n in ("counted", "merged", "var_made", "std_made", "rstd_made"))
            normed, scaled, shifted, turned, kept, ld = (sem(n) for n in ("normed", "scaled", "shifted", "turned", "kept", "affine_loaded"))
            done = normed if scale is None else shifted
            with nc.Block() as block:
                if scale is not None:
                    @block.sync
                    def _(sp):
                        sp.dma_start(gb[:, 0], spread(a[scale])).then_inc(ld, 16)
                        sp.dma_start(gb[:, 1], spread(a[shift])).then_inc(ld, 16)

                @block.vector
                def _(dve):
                    for t in range(T):
                        nc.vector.bn_stats(stats[:, t], src[:, t]).then_inc(counted, 1)
                    for t in range(T):
                        dve.wait_ge(counted, t + 1)
                        nc.vector.bn_aggr(mv[:, t], stats[:, t]).then_inc(merged, 1)
                    dve.wait_ge(merged, T)
                    nc.vector.tensor_scalar(std[:, 0], mv[:, :, 1], 1e-5, None, ALU.add).then_inc(var_made, 1)
                    dve.wait_ge(std_made, 1)
                    nc.vector.reciprocal(std[:, 2], std[:, 1]).then_inc(rstd_made, 1)
                    dve.wait_ge(rstd_made, 1)
                    for t in range(T):
                        nc.vector.tensor_scalar(dst[:, t], src[:, t], mv[:, t, 0:1], std[:, 2, t:t + 1], ALU.subtract, ALU.mult).then_inc(normed, 1)
                        if scale is not None:
                            if t == 0:
                                dve.wait_ge(ld, 32)
                            dve.wait_ge(normed, t + 1)
                            nc.vector.tensor_tensor(dst[:, t], dst[:, t], gb[:, 0], ALU.mult).then_inc(scaled, 1)
                            dve.wait_ge(scaled, t + 1)
                            nc.vector.tensor_tensor(dst[:, t], dst[:, t], gb[:, 1], ALU.add).then_inc(shifted, 1)
                        if add_to is not None:
                            dve.wait_ge(done, t + 1)
                            if relu:
                                nc.vector.scalar_tensor_tensor(add_to[:, t], dst[:, t], 0.0, add_to[:, t], ALU.max, ALU.add)
                            else:
                                nc.vector.tensor_tensor(add_to[:, t], dst[:, t], add_to[:, t], ALU.add)

                @block.scalar
                def _(act):
                    act.wait_ge(var_made, 1)
                    nc.scalar.activation(std[:, 1], std[:, 0], ACT.Sqrt).then_inc(std_made, 1)
                    if turn:
                        for t in range(T):
                            act.wait_ge(turned, t + 1)
                            nc.scalar.copy(xT[:, :, t * P:(t + 1) * P], bank[:, t % 2, 0:K * P].rearrange("p (k n) -> p k n", k=K)).then_inc(kept, 1)

                if turn:
                    @block.tensor
                    def _(pe):
                        for t in range(T):
                            pe.wait_ge(done, t + 1)
                            if t >= 2:
                                pe.wait_ge(kept, t - 1)
                            for k in range(K):
                                last = nc.tensor.transpose(bank[:, t % 2, k * P:(k + 1) * P], dst[:, t, k * 128:(k + 1) * 128], ident[0:P, 0:P])
                            last.then_inc(turned, 1)

        def turn_rows(src):
            turned, kept = sem("turned"), sem("kept")
            with nc.Block() as block:
                @block.tensor
                def _(pe):
                    for t in range(T):
                        if t >= 2:
                            pe.wait_ge(kept, t - 1)
                        for k in range(K):
                            last = nc.tensor.transpose(bank[:, t % 2, k * P:(k + 1) * P], src[:, t, k * 128:(k + 1) * 128], ident[0:P, 0:P])
                        last.then_inc(turned, 1)

                @block.scalar
                def _(act):
                    for t in range(T):
                        act.wait_ge(turned, t + 1)
                        nc.scalar.copy(xT[:, :, t * P:(t + 1) * P], bank[:, t % 2, 0:K * P].rearrange("p (k n) -> p k n", k=K)).then_inc(kept, 1)

        def project(lhs, k_n, w, bias, to):
            ws = sb("ws", [128, k_n, D], F32, c)
            bs = sb("bs", [P, D], F32, c)
            tmp = sb("tmp", [P, 2, D], F32, c)
            ld, made, moved, summed = (sem(n) for n in ("weights_loaded", "made", "moved", "summed"))
            with nc.Block() as block:
                @block.sync
                def _(sp):
                    sp.dma_start(ws[:], w.rearrange("(k p) n -> p k n", p=128)).then_inc(ld, 16)
                    sp.dma_start(bs[:], spread(bias)).then_inc(ld, 16)

                @block.tensor
                def _(pe):
                    pe.wait_ge(ld, 32)
                    for t in range(T):
                        if t >= 4:
                            pe.wait_ge(moved, t - 3)
                        for k in range(k_n):
                            last = nc.tensor.matmul(bank[0:P, t % 4, :], lhs[:, k, t * P:(t + 1) * P], ws[:, k, :], start=(k == 0), stop=(k == k_n - 1))
                        last.then_inc(made, 1)

                @block.vector
                def _(dve):
                    dve.wait_ge(ld, 32)
                    for t in range(T):
                        dve.wait_ge(made, t + 1)
                        nc.vector.tensor_tensor(tmp[:, t % 2], bank[0:P, t % 4, :], bs[:], ALU.add).then_inc(moved, 1)
                        dve.wait_ge(moved, t + 1)
                        nc.vector.tensor_tensor(to[:, t], to[:, t], tmp[:, t % 2], ALU.add).then_inc(summed, 1)

        def route(w, bias, gate, mode, pmax=None, picks=None):
            wr = sb("wr", [128, K, NX], F32, c)
            br = sb("br", [P, NX], F32, c)
            lg = sb("lg", [P, T, NX], F32, c)
            p = sb("p", [P, T, NX], F32, c)
            q = sb("q", [P, T, NX], F32, c)
            oh = sb("oh", [P, T, NX], F32, c)
            m = sb("m", [P, 6, T], F32, c)
            ld, made, step, shifted, exped = (sem(n) for n in ("router_loaded", "logits_made", "step", "logits_shifted", "exped"))
            with nc.Block() as block:
                @block.sync
                def _(sp):
                    sp.dma_start(wr[:], a[w].rearrange("(k p) n -> p k n", p=128)).then_inc(ld, 16)
                    if bias is not None:
                        sp.dma_start(br[:], spread(a[bias])).then_inc(ld, 16)

                @block.tensor
                def _(pe):
                    pe.wait_ge(ld, 16 if bias is None else 32)
                    for t in range(T):
                        for k in range(K):
                            last = nc.tensor.matmul(bank[0:P, 0, t * NX:(t + 1) * NX], xT[:, k, t * P:(t + 1) * P], wr[:, k, :], start=(k == 0), stop=(k == K - 1))
                    last.then_inc(made, 1)

                if mode == "two" or pmax is not None:
                    @block.scalar
                    def _(act):
                        act.wait_ge(shifted, 1)
                        nc.scalar.activation(p[:], q[:], ACT.Exp).then_inc(exped, 1)

                @block.vector
                def _(dve):
                    v = [0]

                    def chain(ins):
                        v[0] += 1
                        ins.then_inc(step, 1)
                        dve.wait_ge(step, v[0])

                    def wide(col):
                        return col.unsqueeze(2).to_broadcast([P, T, NX])

                    def first_best(oh_, vals, i):
                        chain(nc.vector.tensor_reduce(m[:, i], vals, X, ALU.max))
                        chain(nc.vector.tensor_tensor(oh_, vals, wide(m[:, i]), ALU.is_ge))
                        chain(nc.vector.tensor_tensor(oh_, oh_, i8[:].unsqueeze(1).to_broadcast([P, T, NX]), ALU.mult))
                        chain(nc.vector.tensor_reduce(m[:, 5], oh_, X, ALU.min))
                        chain(nc.vector.tensor_tensor(oh_, i8[:].unsqueeze(1).to_broadcast([P, T, NX]), wide(m[:, 5]), ALU.is_equal))

                    dve.wait_ge(ld, 16 if bias is None else 32)
                    dve.wait_ge(made, 1)
                    raw = bank[0:P, 0, 0:T * NX].rearrange("p (t e) -> p t e", t=T)
                    if bias is None:
                        chain(nc.vector.tensor_copy(lg[:], raw))
                    else:
                        chain(nc.vector.tensor_tensor(lg[:], raw, br[:].unsqueeze(1).to_broadcast([P, T, NX]), ALU.add))
                    if mode == "one" and pmax is None:
                        first_best(gate[:], lg[:], 0)
                        return
                    chain(nc.vector.tensor_reduce(m[:, 1], lg[:], X, ALU.max))
                    nc.vector.tensor_tensor(q[:], lg[:], wide(m[:, 1]), ALU.subtract).then_inc(shifted, 1)
                    dve.wait_ge(exped, 1)
                    chain(nc.vector.tensor_reduce(m[:, 2], p[:], X, ALU.add))
                    chain(nc.vector.reciprocal(m[:, 3], m[:, 2]))
                    chain(nc.vector.tensor_tensor(p[:], p[:], wide(m[:, 3]), ALU.mult))
                    if mode == "one":
                        first_best(gate[:], p[:], 0)
                        chain(nc.vector.tensor_copy(pmax[:], m[:, 0]))
                        return
                    first_best(picks[:, 0], p[:], 0)
                    chain(nc.vector.scalar_tensor_tensor(q[:], picks[:, 0], -4.0, p[:], ALU.mult, ALU.add))
                    first_best(picks[:, 1], q[:], 4)
                    chain(nc.vector.tensor_tensor(oh[:], picks[:, 0], picks[:, 1], ALU.add))
                    chain(nc.vector.tensor_tensor(p[:], p[:], oh[:], ALU.mult))
                    chain(nc.vector.tensor_reduce(m[:, 2], p[:], X, ALU.add))
                    chain(nc.vector.tensor_scalar(m[:, 2], m[:, 2], 1e-9, None, ALU.add))
                    chain(nc.vector.reciprocal(m[:, 3], m[:, 2]))
                    chain(nc.vector.tensor_tensor(gate[:], p[:], wide(m[:, 3]), ALU.mult))

        def experts(w1, b1, w2, b2, gate, picks, func, acc):
            top = len(picks)
            MT = -(-((top * N + NX * 128 - 1) // 128) // 2) * 2
            MTL = -(-MT // 4) * 4
            assert MTL <= SLOT_TILES
            F2 = FF // 128
            w1s = sb("w1s", [128, 2, K, FF], F32, c)
            w2s = sb("w2s", [128, 2, F2, D], F32, c)
            b1r = sb("b1r", [NX * F2, 128], F32, c)
            b1T = sb("b1T", [128, NX * F2], F32, c)
            b2s = sb("b2s", [NX, D], F32, c)
            gT = sb("gT", [NX, T, P], F32, c)
            picked = sb("picked", [P, T, NX], F32, c)
            f = sb("f", [P, 5, T, NX], F32, c)
            g8 = sb("g8", [P, 6, NX], F32, c)
            pos = sb("pos", [P, top, T], F32, c)
            pos_i = sb("pos_i", [P, top, T], I32, c)
            wgt = sb("wgt", [P, top, T], F32, c)
            tiles = sb("expert_tiles", [1, NX + 1], I32, c)
            xs = sb("xs", [128, 2, 2, D], F32, c)
            turned_ = sb("xs_turned", [128, K * MTL * 128], F32, c)
            xsT = turned_[:].rearrange("p (k n) -> p k n", k=K)
            got = turned_[0:P, 0:top * T * D].rearrange("p (s t d) -> p s t d", s=top, t=T)
            hid = sb("hid", [128, F2, 128], F32, c)
            ys = sb("ys", [128, 2, D], F32, c)
            ld0, w_used, picked_made, counted, step, ready = (sem(n) for n in ("bias_loaded", "w_used", "picked", "counted", "step", "positions_ready"))
            w_ld = [sem(f"w_loaded{b}") for b in range(2)]
            xs_ld = [sem(f"xs_loaded{b}") for b in range(2)]
            y_stored = [sem(f"y_stored{b}") for b in range(2)]
            g_turned, g_kept, bias_made, bias_added, b_turned, b_kept = (sem(n) for n in (
                "gate_turned", "gate_kept", "bias_made", "bias_added", "b1_turned", "b1_kept"))
            t_made, t_kept, h_made, h_kept, y_made, y_kept, summed = (sem(n) for n in (
                "turned", "turned_kept", "hidden_made", "hidden_kept", "y_made", "y_kept", "summed"))
            rows_put, fetched = dma_sem("rows_put"), dma_sem("fetched")

            def load_weights(eng, e):
                b = e % 2
                eng.dma_start(w1s[:, b], a[w1][e:e + 1].rearrange("e (k p) n -> p (e k) n", p=128)).then_inc(w_ld[b], 16)
                eng.dma_start(w2s[:, b], a[w2][e:e + 1].rearrange("e (k p) n -> p (e k) n", p=128)).then_inc(w_ld[b], 16)

            with nc.Block() as block:
                @block.sync
                def _(sp):
                    sp.dma_start(b1r[:], a[b1].rearrange("e (f p) -> (e f) p", p=128)).then_inc(ld0, 16)
                    sp.dma_start(b2s[:], a[b2]).then_inc(ld0, 16)
                    for e in range(2):
                        load_weights(sp, e)
                    sp.wait_ge(rows_put, 16 * top * T)
                    v = x_slots.rearrange("(n u p) d -> p n u d", u=2, p=128)
                    with sp.Fori(0, MTL // 4) as j:
                        for b in range(2):
                            sp.wait_ge(t_kept, j * 4 + (b * 2 + 2))
                            sp.dma_start(xs[:, b], v[:, bass.ds(j * 2 + b, 1)].rearrange("p n u d -> p (n u) d")).then_inc(xs_ld[b], 16)
                    v = y_slots.rearrange("(n p) d -> p n d", p=128)
                    with sp.Fori(0, MT // 2) as j:
                        for b in range(2):
                            sp.wait_ge(y_kept, j * 2 + (b + 2))
                            sp.dma_start(v[:, bass.ds(j * 2 + b, 1), :].rearrange("p n d -> p (n d)"), ys[:, b]).then_inc(y_stored[b], 16)
                    for b in range(2):
                        sp.wait_ge(y_stored[b], 8 * MT + 16)

                @block.gpsimd
                def _(pool):
                    pool.wait_ge(ready, 1)
                    for s in range(top):
                        for t in range(T):
                            nc.gpsimd.indirect_dma_start(out=x_slots, out_offset=bass.IndirectOffsetOnAxis(ap=pos_i[:, s, t:t + 1], axis=0),
                                                         in_=xn[:, t, :], in_offset=None).then_inc(rows_put, 16)
                    pool.wait_ge(rows_put, 16 * top * T)
                    for b in range(2):
                        pool.wait_ge(y_stored[b], 8 * MT + 16)
                    for s in range(top):
                        for t in range(T):
                            nc.gpsimd.indirect_dma_start(out=got[:, s, t, :], out_offset=None, in_=y_slots,
                                                         in_offset=bass.IndirectOffsetOnAxis(ap=pos_i[:, s, t:t + 1], axis=0)).then_inc(fetched, 16)

                @block.tensor
                def _(pe):
                    pe.wait_ge(picked_made, 1)
                    v = picked[:].rearrange("p t e -> p (t e)")
                    nc.tensor.matmul(bank[0:P, 0, 0:T * NX], above[0:P, 0:P], v, start=True, stop=True)
                    nc.tensor.matmul(bank[0:P, 1, 0:T * NX], ones[0:P, 0:P], v, start=True, stop=True).then_inc(counted, 1)
                    pe.wait_ge(ld0, 32)
                    nc.tensor.transpose(bank[:, 7, 0:NX * F2], b1r[:], ident[0:NX * F2, 0:NX * F2]).then_inc(b_turned, 1)
                    for t in range(T):
                        last = nc.tensor.transpose(bank[0:NX, 4 + t // 4, (t % 4) * P:(t % 4 + 1) * P], gate[:, t, :], ident[0:P, 0:P])
                    last.then_inc(g_turned, 1)
                    pe.wait_ge(g_kept, 1)
                    for t in range(T):
                        if t >= 2:
                            pe.wait_ge(bias_added, t - 1)
                        nc.tensor.matmul(bank[0:P, 2 + t % 2, :], gT[:, t, :], b2s[:], start=True, stop=True).then_inc(bias_made, 1)
                    with pe.Fori(0, MTL // 4) as j:
                        for b in range(2):
                            pe.wait_ge(xs_ld[b], j * 16 + 16)
                            for u in range(2):
                                pe.wait_ge(t_kept, j * 4 + (b * 2 + u + 3))
                                for k in range(K):
                                    last = nc.tensor.transpose(bank[:, 4 + u, k * 128:(k + 1) * 128], xs[:, b, u, k * 128:(k + 1) * 128], ident[:])
                                last.then_inc(t_made, 1)
                    pe.wait_ge(t_kept, MTL + 4)
                    pe.wait_ge(bias_added, T)
                    for e in range(NX):
                        b = e % 2
                        pe.wait_ge(w_ld[b], 32 * (e // 2 + 1))
                        lo = pe.value_load(tiles[0:1, e:e + 1], min_val=0, max_val=MT - 1)
                        hi = pe.value_load(tiles[0:1, e + 1:e + 2], min_val=1, max_val=MT)
                        with pe.Fori(lo, hi) as n:
                            for g in range(F2):
                                for k in range(K):
                                    last = nc.tensor.matmul(bank[:, g, 0:128], w1s[:, b, k, g * 128:(g + 1) * 128], xsT[:, k, bass.ds(n * 128, 128)], start=(k == 0), stop=(k == K - 1))
                                last.then_inc(h_made, 1)
                            pe.wait_ge(y_kept, n + 1)
                            for g in range(F2):
                                pe.wait_ge(h_kept, n * F2 + (g + 1))
                                last = nc.tensor.matmul(bank[:, 2, :], hid[:, g, :], w2s[:, b, g, :], start=(g == 0), stop=(g == F2 - 1))
                            last.then_inc(y_made, 1)
                        nc.tensor.matmul(bank[0:1, 7, 511:512], ident[:, 0:1], ident[:, 0:1], start=True, stop=True).then_inc(w_used, 1)

                @block.scalar
                def _(act):
                    act.sem_inc(t_kept, 4)
                    act.wait_ge(b_turned, 1)
                    nc.scalar.copy(b1T[:], bank[:, 7, 0:NX * F2]).then_inc(b_kept, 1)
                    with act.Fori(0, MTL // 2) as j:
                        for u in range(2):
                            act.wait_ge(t_made, j * 2 + (u + 1))
                            nc.scalar.copy(xsT[:, :, bass.ds(j * 256 + u * 128, 128)], bank[:, 4 + u, :].rearrange("p (k n) -> p k n", k=K)).then_inc(t_kept, 1)
                    act.wait_ge(b_kept, 1)
                    act.wait_ge(ready, 1)
                    for e in range(NX):
                        if e >= 1 and e + 1 < NX:
                            act.wait_ge(w_used, e)
                            load_weights(act, e + 1)
                        lo = act.value_load(tiles[0:1, e:e + 1], min_val=0, max_val=MT - 1)
                        hi = act.value_load(tiles[0:1, e + 1:e + 2], min_val=1, max_val=MT)
                        with act.Fori(lo, hi) as n:
                            for g in range(F2):
                                act.wait_ge(h_made, n * F2 + (g + 1))
                                nc.scalar.activation(hid[:, g, :], bank[:, g, 0:128], func, bias=b1T[:, e * F2 + g:e * F2 + g + 1]).then_inc(h_kept, 1)

                @block.vector
                def _(dve):
                    v = [0]

                    def chain(ins):
                        v[0] += 1
                        ins.then_inc(step, 1)
                        dve.wait_ge(step, v[0])

                    dve.sem_inc(y_kept, 1)
                    for s in y_stored:
                        dve.sem_inc(s, 16)
                    if top == 2:
                        nc.vector.tensor_tensor(picked[:], picks[0], picks[1], ALU.add).then_inc(picked_made, 1)
                        for s in range(2):
                            chain(nc.vector.tensor_tensor(f[:, s], gate[:], picks[s], ALU.mult))
                            chain(nc.vector.tensor_reduce(wgt[:, s], f[:, s], X, ALU.add))
                    else:
                        nc.vector.tensor_copy(picked[:], picks[0]).then_inc(picked_made, 1)
                    dve.wait_ge(counted, 1)
                    nc.vector.tensor_copy(f[:, 0].rearrange("p t e -> p (t e)"), bank[0:P, 0, 0:T * NX])
                    chain(nc.vector.tensor_copy(f[:, 1].rearrange("p t e -> p (t e)"), bank[0:P, 1, 0:T * NX]))
                    for e in range(NX):
                        last = nc.vector.tensor_tensor_scan(f[:, 2, :, e], ones[0:P, 0:T], f[:, 1, :, e], 0.0, ALU.mult, ALU.add)
                    chain(last)
                    chain(nc.vector.tensor_scalar(g8[:, 0], f[:, 2, T - 1, :], 1.0, 127.0, ALU.max, ALU.add))
                    chain(nc.vector.tensor_scalar(g8[:, 1], g8[:, 0], -63.5, 1.0 / 128, ALU.add, ALU.mult))
                    chain(nc.vector.tensor_scalar(g8[:, 1], g8[:, 1], MAGIC, MAGIC, ALU.add, ALU.subtract))
                    chain(nc.vector.tensor_tensor_scan(g8[:, 2], ones[0:P, 0:NX], g8[:, 1], 0.0, ALU.mult, ALU.add))
                    chain(nc.vector.tensor_tensor(g8[:, 3], g8[:, 2], g8[:, 1], ALU.subtract))
                    chain(nc.vector.tensor_scalar(g8[:, 4], g8[:, 3], 128.0, None, ALU.mult))
                    chain(nc.vector.memset(tiles[:], MT))
                    chain(nc.vector.tensor_copy(tiles[0:1, 0:NX], g8[0:1, 3]))
                    chain(nc.vector.tensor_tensor(f[:, 3], f[:, 2], f[:, 1], ALU.subtract))
                    chain(nc.vector.tensor_tensor(f[:, 3], f[:, 3], f[:, 0], ALU.add))
                    chain(nc.vector.tensor_tensor(f[:, 3], f[:, 3], g8[:, 4].unsqueeze(1).to_broadcast([P, T, NX]), ALU.add))
                    for s in range(top):
                        chain(nc.vector.tensor_tensor(f[:, 4], f[:, 3], picks[s], ALU.mult))
                        chain(nc.vector.tensor_reduce(pos[:, s], f[:, 4], X, ALU.add))
                    nc.vector.tensor_copy(pos_i[:], pos[:]).then_inc(ready, 1)
                    dve.wait_ge(g_turned, 1)
                    for j, n in enumerate((4, 4, 2)):
                        last = nc.vector.tensor_copy(gT[:, 4 * j:4 * j + n, :].rearrange("p t n -> p (t n)"), bank[0:NX, 4 + j, 0:n * P])
                    last.then_inc(g_kept, 1)
                    dve.wait_ge(rows_put, 16 * top * T)
                    for t in range(T):
                        dve.wait_ge(bias_made, t + 1)
                        nc.vector.tensor_tensor(acc[:, t], bank[0:P, 2 + t % 2, :], acc[:, t], ALU.add).then_inc(bias_added, 1)
                    with dve.Fori(0, MT // 2) as j:
                        for b in range(2):
                            dve.wait_ge(y_made, j * 2 + (b + 1))
                            dve.wait_ge(y_stored[b], j * 16 + 16)
                            nc.vector.tensor_copy(ys[:, b], bank[:, 2, :]).then_inc(y_kept, 1)
                    dve.wait_ge(fetched, 16 * top * T)
                    for s in range(top):
                        for t in range(T):
                            if s:
                                dve.wait_ge(summed, t + 1)
                            w_ = wgt[:, s, t:t + 1] if top == 2 else 1.0
                            nc.vector.scalar_tensor_tensor(acc[:, t], got[:, s, t, :], w_, acc[:, t], ALU.mult, ALU.add).then_inc(summed, 1)

        def gcn():
            HID = 128
            Asb = sb("A", [P, T, N], F32, c)
            w1s = sb("w1s", [128, K, HID], F32, c)
            w2s = sb("w2s", [128, D], F32, c)
            b1s = sb("b1s", [P, HID], F32, c)
            b2s = sb("b2s", [P, D], F32, c)
            hs = sb("hs", [P, 2, T, HID], F32, c)
            u = sb("u", [P, 2, T, HID], F32, c)
            uT = sb("uT", [HID, T, P], F32, c)
            tmp = sb("tmp", [P, 2, D], F32, c)
            ld, A_ld, h_made, h_kept, agg, agg_kept, step = (sem(n) for n in ("loaded", "A_loaded", "h_made", "h_kept", "aggregated", "agg_kept", "step"))
            s2_made, uT_made, uT_kept, made, moved, u_made = (sem(n) for n in ("s2_made", "uT_made", "uT_kept", "made", "moved", "u_made"))
            with nc.Block() as block:
                @block.sync
                def _(sp):
                    sp.dma_start(w1s[:], a["L0_gnn_W1"].rearrange("(k p) n -> p k n", p=128)).then_inc(ld, 16)
                    sp.dma_start(Asb[:], A_dram).then_inc(A_ld, 16)
                    sp.dma_start(w2s[:], a["L0_gnn_W2"]).then_inc(ld, 16)
                    sp.dma_start(b1s[:], spread(a["L0_gnn_b1"])).then_inc(ld, 16)
                    sp.dma_start(b2s[:], spread(a["L0_gnn_b2"])).then_inc(ld, 16)

                @block.tensor
                def _(pe):
                    pe.wait_ge(ld, 64)
                    for t in range(T):
                        if t >= 2:
                            pe.wait_ge(h_kept, t - 1)
                        for k in range(K):
                            last = nc.tensor.matmul(bank[0:P, t % 2, 0:HID], xT[:, k, t * P:(t + 1) * P], w1s[:, k, :], start=(k == 0), stop=(k == K - 1))
                        last.then_inc(h_made, 1)
                    pe.wait_ge(h_kept, T)
                    pe.wait_ge(A_ld, 16)
                    for r in range(2):
                        if r == 1:
                            pe.wait_ge(s2_made, T)
                        for d in range(T):
                            if r * T + d >= 2:
                                pe.wait_ge(agg_kept, r * T + d - 1)
                            for s in range(T):
                                last = nc.tensor.matmul(bank[0:P, 2 + d % 2, 0:HID], Asb[:, s, d * P:(d + 1) * P], hs[:, r, s, :], start=(s == 0), stop=(s == T - 1))
                            last.then_inc(agg, 1)
                    pe.wait_ge(u_made, T)
                    for t in range(T):
                        if t >= 2:
                            pe.wait_ge(uT_kept, t - 1)
                        nc.tensor.transpose(bank[0:HID, 4 + t % 2, 0:P], u[:, 1, t, :], ident[0:P, 0:P]).then_inc(uT_made, 1)
                        pe.wait_ge(uT_kept, t + 1)
                        if t >= 2:
                            pe.wait_ge(moved, t - 1)
                        nc.tensor.matmul(bank[0:P, 6 + t % 2, :], uT[:, t, :], w2s[:], start=True, stop=True).then_inc(made, 1)

                @block.scalar
                def _(act):
                    for t in range(T):
                        act.wait_ge(h_made, t + 1)
                        nc.scalar.activation(hs[:, 0, t, :], bank[0:P, t % 2, 0:HID], ACT.Copy, scale=dinv[:, t:t + 1]).then_inc(h_kept, 1)
                    for t in range(T):
                        act.wait_ge(uT_made, t + 1)
                        nc.scalar.copy(uT[:, t, :], bank[0:HID, 4 + t % 2, 0:P]).then_inc(uT_kept, 1)

                @block.vector
                def _(dve):
                    v = [0]

                    def chain(ins):
                        v[0] += 1
                        ins.then_inc(step, 1)
                        dve.wait_ge(step, v[0])

                    dve.wait_ge(ld, 64)
                    dve.wait_ge(h_kept, T)
                    for r in range(2):
                        for d in range(T):
                            dve.wait_ge(agg, r * T + d + 1)
                            nc.vector.tensor_tensor(u[:, r, d, :], bank[0:P, 2 + d % 2, 0:HID], hs[:, r, d, :], ALU.add).then_inc(agg_kept, 1)
                            dve.wait_ge(agg_kept, r * T + d + 1)
                            if r == 1:
                                nc.vector.tensor_scalar(u[:, 1, d, :], u[:, 1, d, :], dinv[:, d:d + 1], None, ALU.mult).then_inc(u_made, 1)
                                continue
                            chain(nc.vector.scalar_tensor_tensor(u[:, 0, d, :], u[:, 0, d, :], dinv[:, d:d + 1], b1s[:], ALU.mult, ALU.add))
                            nc.vector.tensor_scalar(hs[:, 1, d, :], u[:, 0, d, :], 0.0, dinv[:, d:d + 1], ALU.max, ALU.mult).then_inc(s2_made, 1)
                        if r == 0:
                            dve.wait_ge(s2_made, T)
                    for t in range(T):
                        dve.wait_ge(made, t + 1)
                        nc.vector.tensor_tensor(tmp[:, t % 2], bank[0:P, 6 + t % 2, :], b2s[:], ALU.add).then_inc(moved, 1)
                        dve.wait_ge(moved, t + 1)
                        nc.vector.tensor_tensor(x[:, t], x[:, t], tmp[:, t % 2], ALU.add).then_inc(step, 1)

        def edge_qkv(q3):
            ws = sb("ws", [128, 3, K, D], F32, c)
            bs = sb("bs", [P, 3, D], F32, c)
            kvs = sb("kvs", [P, 2, 2, D], F32, c)
            qf = sb("qf", [P, 2, D], F32, c)
            ld, made, kept, split = (sem(n) for n in ("weights_loaded", "made", "kept", "split"))
            put = [sem(f"kv_put{b}") for b in range(2)]
            with nc.Block() as block:
                @block.sync
                def _(sp):
                    for i, n in enumerate("qkv"):
                        sp.dma_start(ws[:, i], a[f"L1_gnn_W{n}"].rearrange("(k p) n -> p k n", p=128)).then_inc(ld, 16)
                        sp.dma_start(bs[:, i], spread(a[f"L1_gnn_b{n}"])).then_inc(ld, 16)
                    for t in range(T):
                        sp.wait_ge(kept, 3 * t + 3)
                        sp.dma_start(k_dram[t * P:(t + 1) * P, :], kvs[:, t % 2, 0]).then_inc(put[t % 2], 16)
                        sp.dma_start(v_dram[t * P:(t + 1) * P, :], kvs[:, t % 2, 1]).then_inc(put[t % 2], 16)
                    for b in range(2):
                        sp.wait_ge(put[b], 16 * T)

                @block.tensor
                def _(pe):
                    pe.wait_ge(ld, 96)
                    for t in range(T):
                        for i in range(3):
                            if t >= 2:
                                pe.wait_ge(kept, 3 * (t - 2) + i + 1)
                            for k in range(K):
                                last = nc.tensor.matmul(bank[0:P, 3 * (t % 2) + i, :], xT[:, k, t * P:(t + 1) * P], ws[:, i, k, :], start=(k == 0), stop=(k == K - 1))
                            last.then_inc(made, 1)

                @block.vector
                def _(dve):
                    v = [0]

                    def chain(ins):
                        v[0] += 1
                        ins.then_inc(split, 1)
                        dve.wait_ge(split, v[0])

                    dve.wait_ge(ld, 96)
                    for t in range(T):
                        for i in range(3):
                            dve.wait_ge(made, 3 * t + i + 1)
                            if i == 1 and t >= 2:
                                dve.wait_ge(put[t % 2], 32 * (t // 2))
                            dst = qf[:, 0] if i == 0 else kvs[:, t % 2, i - 1]
                            nc.vector.tensor_tensor(dst, bank[0:P, 3 * (t % 2) + i, :], bs[:, i], ALU.add).then_inc(kept, 1)
                        dve.wait_ge(kept, 3 * t + 1)
                        chain(nc.vector.tensor_copy(q3[:, 0, t], qf[:, 0]))
                        chain(nc.vector.tensor_tensor(qf[:, 1], qf[:, 0], q3[:, 0, t], ALU.subtract))
                        chain(nc.vector.tensor_copy(q3[:, 1, t], qf[:, 1]))
                        chain(nc.vector.tensor_tensor(qf[:, 0], qf[:, 1], q3[:, 1, t], ALU.subtract))
                        chain(nc.vector.tensor_copy(q3[:, 2, t], qf[:, 0]))

        def gather_rows(pool, source, index, into, free, loaded, gone):
            with pool.Fori(0, SC // (2 * G)) as i:
                for h in range(2):
                    pool.wait_ge(free[h], i + 1)
                    pool.sem_inc(gone, 1)
                    for g in range(G):
                        nc.gpsimd.indirect_dma_start(out=into[:, h * G + g, :], out_offset=None, in_=source,
                                                     in_offset=bass.IndirectOffsetOnAxis(ap=index[:, h * G + g:h * G + g + 1], axis=0)).then_inc(loaded[h], 16)

        def edge_logits(q3, recs, lg, wT):
            kg = sb("kg", [S, 2 * G, D], F32, c)
            idx = sb("idx", [S, 2 * G], I32, c)
            w = sb("w", [S, 2, P], BF16, c)
            identb = sb("identb", [128, 128], BF16, c)
            prod = sb("prod", [S, 2, D], F32, c)
            wTp = bank[:, 4:6, 0:64].bitcast(BF16)
            recs_ld, cleared, w_made, w_turned, wT_kept, q_made, multiplied, reduced, dot = (sem(n) for n in (
                "recs_loaded", "cleared", "w_made", "w_turned", "wT_kept", "q_spread", "multiplied", "reduced", "scaled"))
            idx_made = [sem(f"index_made{h}") for h in range(2)]
            k_ld = [dma_sem(f"k_gathered{h}") for h in range(2)]
            gone = sem("pool_passed")
            with nc.Block() as block:
                @block.sync
                def _(sp):
                    sp.dma_start(recs[:], table.rearrange("(p c) w -> p c w", p=S)).then_inc(recs_ld, 16)

                @block.gpsimd
                def _(pool):
                    gather_rows(pool, k_dram, idx, kg, idx_made, k_ld, gone)

                @block.scalar
                def _(act):
                    nc.scalar.copy(identb[:], ident[:]).then_inc(cleared, 1)
                    with act.Fori(0, PAIRS) as n:
                        for h in range(2):
                            act.wait_ge(w_turned, n * 2 + (h + 1))
                            nc.scalar.copy(wT[:, bass.ds(n * (2 * S) + h * S, S)], wTp[0:P, h, :]).then_inc(wT_kept, 1)

                @block.tensor
                def _(pe):
                    pe.wait_ge(cleared, 1)
                    for t in range(T):
                        lo = pe.value_load(bounds[0:1, t:t + 1], min_val=0, max_val=PAIRS - 1)
                        hi = pe.value_load(bounds[0:1, t + 1:t + 2], min_val=1, max_val=PAIRS)
                        with pe.Fori(lo, hi) as n:
                            for h in range(2):
                                pe.wait_ge(w_made, n * 2 + (h + 1))
                                nc.tensor.transpose(wTp[0:P, h, :], w[:, h], identb[:]).then_inc(w_turned, 1)
                            for h in range(2):
                                pe.wait_ge(wT_kept, n * 2 + (h + 1))
                                pe.wait_ge(multiplied, n * 2 + (h + 1))
                                for i in range(3):
                                    last = nc.tensor.matmul(bank[:, h, :], wT[:, bass.ds(n * (2 * S) + h * S, S)], q3[:, i, t, :], start=(i == 0), stop=(i == 2))
                                last.then_inc(q_made, 1)

                @block.vector
                def _(dve):
                    dve.sem_inc(multiplied, 2)
                    dve.wait_ge(recs_ld, 16)
                    for h in range(2):
                        nc.vector.tensor_copy(idx[:, h * G:(h + 1) * G], recs[:, h * G:(h + 1) * G, 1]).then_inc(idx_made[h], 1)
                    for h in range(2):
                        nc.vector.tensor_scalar(w[:, h], iota[:, 0:P], recs[:, h, 0:1], None, ALU.is_equal).then_inc(w_made, 1)

                    def unit(i, tail):
                        for h in range(2):
                            dve.wait_ge(k_ld[h], i * (16 * G) + 16 * G)
                            for g in range(G):
                                n = i * (2 * G) + (h * G + g)
                                dve.wait_ge(q_made, n + 1)
                                nc.vector.tensor_tensor(prod[:, g % 2], kg[:, h * G + g, :], bank[:, g % 2, :], ALU.mult).then_inc(multiplied, 1)
                                if not (tail and h == 1 and g >= G - 2):
                                    nc.vector.tensor_scalar(w[:, g % 2], iota[:, 0:P], recs[:, bass.ds(n + 2, 1), 0:1].rearrange("p a b -> p (a b)"), None, ALU.is_equal).then_inc(w_made, 1)
                                dve.wait_ge(multiplied, n + 3)
                                nc.vector.tensor_reduce(lg[:, bass.ds(n, 1), :].rearrange("p a h -> p (a h)"), prod[:, g % 2].rearrange("p (h d) -> p h d", h=H), X, ALU.add).then_inc(reduced, 1)
                            if not tail:
                                nc.vector.tensor_copy(idx[:, h * G:(h + 1) * G], recs[:, bass.ds(i * (2 * G) + (h * G + 2 * G), G), 1:2].rearrange("p a b -> p (a b)")).then_inc(idx_made[h], 1)

                    with dve.Fori(0, SC // (2 * G) - 1) as i:
                        unit(i, False)
                    unit(SC // (2 * G) - 1, True)
                    dve.wait_ge(reduced, SC)
                    nc.vector.scalar_tensor_tensor(lg[:], lg[:], DH ** -0.5, recs[:, :, 2:2 + H], ALU.mult, ALU.add).then_inc(dot, 1)

        def edge_max(recs, lg, m3):
            PN = SC // 4
            key = sb("key", [S, SC, H], F32, c)
            krow = sb("krow", [H, 2, 4 * S + 1], F32, c)
            brk = sb("brk", [H, 2, 4 * S], F32, c)
            run_ = sb("run", [H, 2, 4 * S], F32, c)
            back = sb("back", [S, SC, H], F32, c)
            mm = sb("mm", [P, 3, T, H], F32, c)
            spread_, rows_made, krow_kept, l_free, step, scanned, turned, kept, put, cut = (sem(n) for n in (
                "key_spread", "rows_made", "krow_kept", "rows_used", "step", "scanned", "turned_back", "kept", "run_put", "cut"))
            got = dma_sem("max_gathered")
            with nc.Block() as block:
                @block.gpsimd
                def _(pool):
                    nc.gpsimd.memset(krow[:, 0, 0:1], -2.0).then_inc(cut, 1)
                    pool.wait_ge(put, 16)
                    for t in range(T):
                        nc.gpsimd.indirect_dma_start(out=mm[:, 0, t, :], out_offset=None, in_=run_dram,
                                                     in_offset=bass.IndirectOffsetOnAxis(ap=last_row[:, t:t + 1], axis=0)).then_inc(got, 16)

                @block.sync
                def _(sp):
                    sp.wait_ge(kept, PN)
                    sp.dma_start(run_dram.rearrange("(p c) h -> p c h", p=S), back[:]).then_inc(put, 16)

                @block.tensor
                def _(pe):
                    pe.wait_ge(spread_, 1)
                    for j in range(PN + 1):
                        if j < PN:
                            if j >= 2:
                                pe.wait_ge(scanned, j - 1)
                                pe.wait_ge(krow_kept, j - 1)
                            for g in range(4):
                                nc.tensor.transpose(bank[0:H, j % 2, g * S:(g + 1) * S], lg[:, 4 * j + g, :], ident[:])
                            for g in range(4):
                                last = nc.tensor.transpose(bank[0:H, 2 + j % 2, g * S:(g + 1) * S], key[:, 4 * j + g, :], ident[:])
                            last.then_inc(rows_made, 1)
                        if j >= 1:
                            i = j - 1
                            pe.wait_ge(scanned, i + 1)
                            if i >= 2:
                                pe.wait_ge(kept, i - 1)
                            for g in range(4):
                                last = nc.tensor.transpose(bank[:, 4 + i % 2, g * H:(g + 1) * H], run_[:, i % 2, g * S:(g + 1) * S], ident[0:H, 0:H])
                            last.then_inc(turned, 1)

                @block.scalar
                def _(act):
                    nc.scalar.copy(key[:], recs[:, :, RW - 1:RW].to_broadcast([S, SC, H])).then_inc(spread_, 1)
                    for j in range(PN):
                        act.wait_ge(rows_made, j + 1)
                        if j >= 2:
                            act.wait_ge(step, 2 * (j - 1))
                        nc.scalar.copy(krow[:, j % 2, 1:], bank[0:H, 2 + j % 2, :]).then_inc(krow_kept, 1)
                        if j >= 1:
                            act.wait_ge(turned, j)
                            nc.scalar.copy(back[:, 4 * (j - 1):4 * j, :].rearrange("p c h -> p (c h)"), bank[:, 4 + (j - 1) % 2, 0:4 * H]).then_inc(kept, 1)
                    act.wait_ge(turned, PN)
                    nc.scalar.copy(back[:, 4 * (PN - 1):4 * PN, :].rearrange("p c h -> p (c h)"), bank[:, 4 + (PN - 1) % 2, 0:4 * H]).then_inc(kept, 1)

                @block.vector
                def _(dve):
                    dve.wait_ge(cut, 1)
                    for j in range(PN):
                        dve.wait_ge(krow_kept, j + 1)
                        nc.vector.tensor_tensor(brk[:, j % 2], krow[:, j % 2, 1:], krow[:, j % 2, 0:4 * S], ALU.not_equal).then_inc(step, 1)
                        dve.wait_ge(step, 2 * j + 1)
                        nc.vector.tensor_scalar(brk[:, j % 2], brk[:, j % 2], NEG, None, ALU.mult)
                        nc.vector.tensor_copy(krow[:, (j + 1) % 2, 0:1], krow[:, j % 2, 4 * S:4 * S + 1]).then_inc(step, 1)
                        dve.wait_ge(step, 2 * j + 2)
                        if j >= 2:
                            dve.wait_ge(turned, j - 1)
                        if j >= 1:
                            dve.wait_ge(scanned, j)
                        first = NEG if j == 0 else run_[:, (j - 1) % 2, 4 * S - 1:4 * S]
                        nc.vector.tensor_tensor_scan(run_[:, j % 2], brk[:, j % 2], bank[0:H, j % 2, :], first, ALU.add, ALU.max).then_inc(scanned, 1)
                    dve.wait_ge(got, 16 * T)

                    v = [1]

                    def chain(ins):
                        v[0] += 1
                        ins.then_inc(cut, 1)
                        dve.wait_ge(cut, v[0])

                    chain(nc.vector.tensor_copy(m3[:, :, 0, :], mm[:, 0]))
                    chain(nc.vector.tensor_tensor(mm[:, 1], mm[:, 0], m3[:, :, 0, :], ALU.subtract))
                    chain(nc.vector.tensor_copy(m3[:, :, 1, :], mm[:, 1]))
                    chain(nc.vector.tensor_tensor(mm[:, 2], mm[:, 1], m3[:, :, 1, :], ALU.subtract))
                    chain(nc.vector.tensor_copy(m3[:, :, 2, :], mm[:, 2]))

        def edge_exp(recs, lg, wT, m3, p3):
            r = sb("r", [S, 2, SC, H], F32, c)
            PP = 8
            made, taken, exped, step = (sem(n) for n in ("max_spread", "max_taken", "exped", "step"))
            with nc.Block() as block:
                @block.tensor
                def _(pe):
                    for t in range(T):
                        lo = pe.value_load(bounds[0:1, t:t + 1], min_val=0, max_val=PAIRS - 1)
                        hi = pe.value_load(bounds[0:1, t + 1:t + 2], min_val=1, max_val=PAIRS)
                        with pe.Fori(lo, hi) as n:
                            for h in range(2):
                                pe.wait_ge(taken, n * 2 + (h + 1))
                                nc.tensor.matmul(bank[:, h, 0:3 * H], wT[:, bass.ds(n * (2 * S) + h * S, S)],
                                                 m3[:, t, :, :].rearrange("p i h -> p (i h)"), start=True, stop=True).then_inc(made, 1)

                @block.vector
                def _(dve):
                    v = [0]

                    def chain(ins):
                        v[0] += 1
                        ins.then_inc(step, 1)
                        dve.wait_ge(step, v[0])

                    dve.sem_inc(taken, 2)
                    with dve.Fori(0, PAIRS) as n:
                        for h in range(2):
                            dve.wait_ge(made, n * 2 + (h + 1))
                            nc.vector.tensor_reduce(r[:, 0, bass.ds(n * 2 + h, 1), :].rearrange("p a h -> p (a h)"),
                                                    bank[:, h, 0:3 * H].rearrange("p (i h) -> p h i", i=3), X, ALU.add).then_inc(taken, 1)
                    dve.wait_ge(taken, 2 * PAIRS + 2)
                    nc.vector.tensor_tensor(lg[:], lg[:], r[:, 0], ALU.subtract).then_inc(exped, 1)
                    dve.wait_ge(exped, 2)
                    chain(nc.vector.tensor_copy(p3[:, :, 0, :], lg[:]))
                    chain(nc.vector.tensor_tensor(r[:, 0], lg[:], p3[:, :, 0, :], ALU.subtract))
                    chain(nc.vector.tensor_copy(p3[:, :, 1, :], r[:, 0]))
                    chain(nc.vector.tensor_tensor(r[:, 1], r[:, 0], p3[:, :, 1, :], ALU.subtract))
                    chain(nc.vector.tensor_copy(p3[:, :, 2, :], r[:, 1]))

                @block.scalar
                def _(act):
                    act.wait_ge(exped, 1)
                    nc.scalar.activation(lg[:], lg[:], ACT.Exp).then_inc(exped, 1)

        def edge_sum(recs, lg, p3):
            vg = sb("vg", [S, 2 * G, D], F32, c)
            idx = sb("idx", [S, 2 * G], I32, c)
            w = sb("w", [S, 2, P], F32, c)
            wb = sb("wb", [S, 2, P], BF16, c)
            pv = sb("pv", [S, 2, D], F32, c)
            pb = sb("pb", [S, 2, 3 * H], BF16, c)
            zero = sb("zero", [S, 512], BF16, c)
            den = sb("den", [P, 2, T, H], F32, c)
            dparts = sb("dparts", [P, T, 3 * H], F32, c)
            zeroed, w_made, pv_made, tile_done, tile_kept, step = (sem(n) for n in ("zeroed", "w_made", "pv_made", "tile_done", "tile_kept", "step"))
            idx_made = [sem(f"index_made{h}") for h in range(2)]
            used = [sem(f"pv_used{h}") for h in range(2)]
            v_ld = [dma_sem(f"v_gathered{h}") for h in range(2)]
            gone = sem("pool_passed")
            with nc.Block() as block:
                @block.gpsimd
                def _(pool):
                    gather_rows(pool, v_dram, idx, vg, idx_made, v_ld, gone)

                @block.tensor
                def _(pe):
                    for s in used:
                        pe.sem_inc(s, 1)
                    pe.wait_ge(zeroed, 1)
                    for t in range(T):
                        if t >= 2:
                            pe.wait_ge(tile_kept, t - 1)
                        y, d = bank[0:P, 2 * (t % 2), :], bank[0:P, 2 * (t % 2) + 1, 0:3 * H]
                        lo = pe.value_load(bounds[0:1, t:t + 1], min_val=0, max_val=PAIRS - 1)
                        hi = pe.value_load(bounds[0:1, t + 1:t + 2], min_val=1, max_val=PAIRS)
                        for o, cn in ((y, D), (d, 3 * H)):
                            nc.tensor.matmul(o, zero[:, 0:P], zero[:, 0:cn], start=True, stop=False, skip_group_check=True)
                        with pe.Fori(lo, hi) as n:
                            for h in range(2):
                                pe.wait_ge(w_made, n * 2 + (h + 1))
                                nc.tensor.matmul(d, wb[:, h], pb[:, h], start=False, stop=False, skip_group_check=True)
                                pe.wait_ge(pv_made, n * 2 + (h + 1))
                                nc.tensor.matmul(y, w[:, h], pv[:, h], start=False, stop=False, skip_group_check=True).then_inc(used[h], 1)
                        for o, cn in ((y, D), (d, 3 * H)):
                            last = nc.tensor.matmul(o, zero[:, 0:P], zero[:, 0:cn], start=False, stop=True, skip_group_check=True)
                        last.then_inc(tile_done, 1)

                @block.scalar
                def _(act):
                    for t in range(T):
                        act.wait_ge(tile_done, t + 1)
                        nc.scalar.copy(xn[:, t], bank[0:P, 2 * (t % 2), :])
                        nc.scalar.copy(dparts[:, t], bank[0:P, 2 * (t % 2) + 1, 0:3 * H]).then_inc(tile_kept, 1)

                @block.vector
                def _(dve):
                    nc.vector.memset(zero[:], 0.0).then_inc(zeroed, 1)
                    for h in range(2):
                        nc.vector.tensor_copy(idx[:, h * G:(h + 1) * G], recs[:, h * G:(h + 1) * G, 1]).then_inc(idx_made[h], 1)

                    def unit(i, tail):
                        for h in range(2):
                            for g in range(G):
                                n = i * (2 * G) + (h * G + g)
                                b = g % 2
                                dve.wait_ge(used[b], i * G + (h * (G // 2) + g // 2 + 1))
                                nc.vector.tensor_scalar(w[:, b], iota[:, 0:P], recs[:, bass.ds(n, 1), 0:1].rearrange("p a b -> p (a b)"), None, ALU.is_equal)
                                nc.vector.tensor_scalar(wb[:, b], iota[:, 0:P], recs[:, bass.ds(n, 1), 0:1].rearrange("p a b -> p (a b)"), None, ALU.is_equal)
                                nc.vector.tensor_copy(pb[:, b], p3[:, bass.ds(n, 1), :, :].rearrange("p a i h -> p (a i h)")).then_inc(w_made, 1)
                                if g == 0:
                                    dve.wait_ge(v_ld[h], i * (16 * G) + 16 * G)
                                nc.vector.tensor_tensor(pv[:, b].rearrange("p (h d) -> p h d", h=H), vg[:, h * G + g, :].rearrange("p (h d) -> p h d", h=H),
                                                        lg[:, bass.ds(n, 1), :].rearrange("p a h -> p (a h)").unsqueeze(2).to_broadcast([S, H, DH]), ALU.mult).then_inc(pv_made, 1)
                                if g == G - 1:
                                    dve.wait_ge(pv_made, n + 1)
                            if not tail:
                                nc.vector.tensor_copy(idx[:, h * G:(h + 1) * G], recs[:, bass.ds(i * (2 * G) + (h * G + 2 * G), G), 1:2].rearrange("p a b -> p (a b)")).then_inc(idx_made[h], 1)

                    with dve.Fori(0, SC // (2 * G) - 1) as i:
                        unit(i, False)
                    unit(SC // (2 * G) - 1, True)

                    v = [0]

                    def chain(ins):
                        v[0] += 1
                        ins.then_inc(step, 1)
                        dve.wait_ge(step, v[0])

                    dve.wait_ge(tile_kept, T)
                    chain(nc.vector.tensor_reduce(den[:, 0], dparts[:].rearrange("p t (i h) -> p t h i", i=3), X, ALU.add))
                    chain(nc.vector.tensor_scalar(den[:, 0], den[:, 0], 1e-30, None, ALU.max))
                    chain(nc.vector.reciprocal(den[:, 1], den[:, 0]))
                    for t in range(T):
                        y3 = xn[:, t].rearrange("p (h d) -> p h d", h=H)
                        chain(nc.vector.tensor_tensor(y3, y3, den[:, 1, t].unsqueeze(2).to_broadcast([P, H, DH]), ALU.mult))

        def edge_attention():
            q3 = sb("q3", [P, 3, T, D], BF16, c)
            run(edge_qkv, q3)
            recs = sb("recs", [S, SC, RW], F32, c)
            lg = sb("lg", [S, SC, H], F32, c)
            wT = sb("wT", [P, SC * S], BF16, c)
            m3 = sb("m3", [P, T, 3, H], BF16, c)
            p3 = sb("p3", [S, SC, 3, H], BF16, c)
            run(edge_logits, q3, recs, lg, wT)
            run(edge_max, recs, lg, m3)
            run(edge_exp, recs, lg, wT, m3, p3)
            run(edge_sum, recs, lg, p3)

        def full_attention():
            wq = sb("wq", [128, 3, K, 128], F32, c)
            bqk = sb("bqk", [128, 2], F32, c)
            bv = sb("bv", [P, D], F32, c)
            qz = sb("qz", [128, 2, N], F32, c)
            kz = sb("kz", [128, 2, N], F32, c)
            EXTRA = (DH, 0)
            vs = sb("vs", [P, T, 128], F32, c)
            mxp = sb("mxp", [P, 2, T, 3], F32, c)
            nm = sb("nm", [P, 2, 2, T], F32, c)
            pT = sb("pT", [P, T, N], F32, c)
            psum_k = sb("psum_k", [P, N], F32, c)
            rden = sb("rden", [128, N], F32, c)
            oT = sb("oT", [128, K, N], F32, c)
            bias_ld, w_ld, w_used = sem("bias_loaded"), sem("w_loaded"), sem("w_used")
            zeroed, ones_set, row_zeroed, turns = (sem(n) for n in ("zeroed", "ones_set", "row_zeroed", "turns"))
            made, folded, negated, added, inverted, o_free = (sem(n) for n in (
                "group_made", "max_folded", "max_negated", "p_added", "inverted", "o_free"))
            RING = 6
            free = [sem(f"bank_free{i}") for i in range(RING)]
            V_T = [(0, 2), (2, 2), (4, 2), (6, 2), (8, 1), (9, 1)]
            R_T = [(0, 4), (4, 4), (8, 2)]
            groups = [("q", j) for j in range(3)] + [("k", j) for j in range(3)] + [("v", j) for j in range(6)]
            for h in range(2):
                groups += [("s", h, t, j) for t in range(T) for j in range(3)]
            for h in range(2):
                groups += [("row", h, j) for j in range(3)]
                for t in range(T):
                    groups += [("p", h, t, j) for j in range(3)]
                    if h == 1 and t == 1:
                        groups += [("den", 0, j) for j in range(3)]
            groups += [("den", 1, j) for j in range(3)]
            NG = len(groups)
            assert NG % RING == 0
            at = {g: i for i, g in enumerate(groups)}
            O_COLS = [(0, 313, 0, 6), (313, 312, 64, 6), (625, 313, 0, 7), (938, 312, 64, 7)]
            SCALE = DH ** -0.5

            def bank_of(*g):
                return at[g] % RING

            def wait_made(eng, m, *g):
                eng.wait_ge(made, m * NG + (at[g] + 1))

            def wait_copied(eng, m, *g):
                eng.wait_ge(free[at[g] % RING], m * (NG // RING) + (at[g] // RING + 2))

            with nc.Block() as block:
                @block.sync
                def _(sp):
                    sp.dma_start(bv[:], spread(a["L1_ffn_bv"])).then_inc(bias_ld, 16)
                    with sp.Fori(0, K) as m:
                        sp.wait_ge(w_used, m + 1)
                        for i, n in enumerate("qk"):
                            sp.dma_start(bqk[:, i:i + 1], a[f"L1_ffn_b{n}"].rearrange("(m p a) -> m p a", p=128, a=1)[bass.ds(m, 1)].rearrange("m p a -> (m p) a"), allow_slow_non_contiguous=True).then_inc(w_ld, 16)
                        for i, n in enumerate("qkv"):
                            sp.dma_start(wq[:, i], a[f"L1_ffn_W{n}"].rearrange("(k p) (m n) -> p k m n", p=128, n=128)[:, :, bass.ds(m, 1), :].rearrange("p k m n -> p k (m n)")).then_inc(w_ld, 16)

                @block.gpsimd
                def _(pool):
                    for b in (qz, kz):
                        nc.gpsimd.memset(b[DH:128, 0, :], 0.0).then_inc(zeroed, 1)
                        nc.gpsimd.memset(b[0:DH, 1, :], 0.0).then_inc(zeroed, 1)
                    pool.wait_ge(zeroed, 4)
                    for h in range(2):
                        nc.gpsimd.memset(kz[EXTRA[h]:EXTRA[h] + 1, h, :], 1.0).then_inc(ones_set, 1)
                    with pool.Fori(0, K) as m:
                        wait_made(pool, m, "q", 0)
                        pool.sem_inc(turns, 1)
                        for h in range(2):
                            nc.gpsimd.memset(qz[EXTRA[h]:EXTRA[h] + 1, h, :], 0.0).then_inc(row_zeroed, 1)

                @block.tensor
                def _(pe):
                    def wait_free(m, g):
                        pe.wait_ge(free[at[g] % RING], m * (NG // RING) + (at[g] // RING + 1))

                    def den(m, h):
                        pe.wait_ge(added, m * (2 * (T - 1)) + (h + 2) * (T - 1))
                        for j, (c0, cn) in enumerate(COLS):
                            wait_free(m, ("den", h, j))
                            nc.tensor.matmul(bank[:, bank_of("den", h, j), 0:cn], ones[0:P, :], psum_k[:, c0:c0 + cn], start=True, stop=True).then_inc(made, 1)

                    def outputs(m, h, t):
                        if t == 0:
                            pe.wait_ge(o_free, m * 2 + (h + 1))
                        for j in range(3):
                            wait_copied(pe, m, "p", h, t, j)
                        for c0, cn, p0, b in O_COLS:
                            nc.tensor.matmul(bank[p0:p0 + DH, b, 0:cn], vs[:, t, h * DH:(h + 1) * DH], pT[:, t, c0:c0 + cn], start=(t == 0), stop=(t == T - 1))

                    pe.sem_inc(w_used, 1)
                    pe.sem_inc(o_free, 1)
                    pe.wait_ge(zeroed, 4)
                    pe.wait_ge(ones_set, 2)
                    with pe.Fori(0, K) as m:
                        pe.wait_ge(w_ld, m * 80 + 80)
                        for i, n in enumerate("qk"):
                            for j, (c0, cn) in enumerate(COLS):
                                wait_free(m, (n, j))
                                for k in range(K):
                                    last = nc.tensor.matmul(bank[:, bank_of(n, j), 0:cn], wq[:, i, k, :], xT[:, k, c0:c0 + cn], start=(k == 0), stop=(k == K - 1))
                                last.then_inc(made, 1)
                        for j, (t0, tn) in enumerate(V_T):
                            wait_free(m, ("v", j))
                            for t in range(t0, t0 + tn):
                                for k in range(K):
                                    last = nc.tensor.matmul(bank[0:P, bank_of("v", j), (t - t0) * 128:(t - t0 + 1) * 128], xT[:, k, t * P:(t + 1) * P], wq[:, 2, k, :], start=(k == 0), stop=(k == K - 1))
                            last.then_inc(made, 1)
                        pe.wait_ge(row_zeroed, m * 2 + 2)
                        for j in range(3):
                            wait_copied(pe, m, "q", j)
                            wait_copied(pe, m, "k", j)
                        for h in range(2):
                            for t in range(T):
                                for j, (c0, cn) in enumerate(COLS):
                                    wait_free(m, ("s", h, t, j))
                                    ins = nc.tensor.matmul(bank[0:P, bank_of("s", h, t, j), 0:cn], qz[:, h, t * P:(t + 1) * P], kz[:, h, c0:c0 + cn], start=True, stop=True)
                                    ins.then_inc(made, 1)
                                    if (h, t, j) == (0, 0, 0):
                                        pe.wait_ge(made, m * NG + (at[("v", 5)] + 1))
                                        pe.sem_inc(w_used, 1)
                        for h in range(2):
                            pe.wait_ge(negated, m * 2 + (h + 1))
                            for j, (t0, tn) in enumerate(R_T):
                                wait_free(m, ("row", h, j))
                                for t in range(t0, t0 + tn):
                                    last = nc.tensor.matmul(bank[EXTRA[h]:EXTRA[h] + 1, bank_of("row", h, j), (t - t0) * P:(t - t0 + 1) * P], nm[:, h, 1, t:t + 1], ident[0:P, 0:P], start=True, stop=True)
                                last.then_inc(made, 1)
                            for j in range(3):
                                wait_copied(pe, m, "row", h, j)
                            if h == 0:
                                for j in range(6):
                                    wait_copied(pe, m, "v", j)
                            for t in range(T):
                                for j, (c0, cn) in enumerate(COLS):
                                    wait_free(m, ("p", h, t, j))
                                    nc.tensor.matmul(bank[0:P, bank_of("p", h, t, j), 0:cn], kz[:, h, t * P:(t + 1) * P], qz[:, h, c0:c0 + cn], start=True, stop=True).then_inc(made, 1)
                                if h == 1 and t == 1:
                                    den(m, 0)
                                if t >= 1:
                                    outputs(m, h, t - 1)
                            outputs(m, h, T - 1)
                        den(m, 1)

                @block.scalar
                def _(act):
                    act.wait_ge(zeroed, 4)
                    with act.Fori(0, K) as m:
                        for i, (n, z) in enumerate((("q", qz), ("k", kz))):
                            for j, (c0, cn) in enumerate(COLS):
                                wait_made(act, m, n, j)
                                for h in range(2):
                                    r = slice(h * DH, (h + 1) * DH)
                                    last = nc.scalar.activation(z[r, h, c0:c0 + cn], bank[r, bank_of(n, j), 0:cn], ACT.Identity, bias=bqk[r, i:i + 1])
                                last.then_inc(free[bank_of(n, j)], 1)
                        for h in range(2):
                            e = slice(EXTRA[h], EXTRA[h] + 1)
                            for j, (t0, tn) in enumerate(R_T):
                                wait_made(act, m, "row", h, j)
                                nc.scalar.copy(qz[e, h, t0 * P:(t0 + tn) * P], bank[e, bank_of("row", h, j), 0:tn * P]).then_inc(free[bank_of("row", h, j)], 1)
                            act.wait_ge(added, m * (2 * (T - 1)) + (h + 1) * (T - 1))
                            for t in range(T):
                                for j, (c0, cn) in enumerate(COLS):
                                    wait_made(act, m, "p", h, t, j)
                                    nc.scalar.activation(pT[:, t, c0:c0 + cn], bank[0:P, bank_of("p", h, t, j), 0:cn], ACT.Exp, scale=SCALE).then_inc(free[bank_of("p", h, t, j)], 1)

                @block.vector
                def _(dve):
                    for s in free:
                        dve.sem_inc(s, 1)
                    dve.sem_inc(added, T - 1)
                    dve.wait_ge(bias_ld, 16)
                    with dve.Fori(0, K) as m:
                        def finish(h):
                            for j, (c0, cn) in enumerate(COLS):
                                wait_made(dve, m, "den", h, j)
                                b = bank_of("den", h, j)
                                nc.vector.reciprocal(rden[:, c0:c0 + cn], bank[:, b, 0:cn]).then_inc(free[b], 1)
                            for j in range(3):
                                wait_copied(dve, m, "den", h, j)
                            for i, (c0, cn, p0, b) in enumerate(O_COLS):
                                last = nc.vector.tensor_tensor(oT[h * DH:(h + 1) * DH, bass.ds(m, 1), c0:c0 + cn].rearrange("p a n -> p (a n)"), bank[p0:p0 + DH, b, 0:cn], rden[p0:p0 + DH, c0:c0 + cn], ALU.mult)
                            last.then_inc(o_free, 1)

                        for j, (t0, tn) in enumerate(V_T):
                            wait_made(dve, m, "v", j)
                            b = bank_of("v", j)
                            nc.vector.tensor_tensor(vs[:, t0:t0 + tn, :], bank[0:P, b, 0:tn * 128].rearrange("p (t n) -> p t n", t=tn),
                                                    bv[:, bass.ds(m * 128, 128)].unsqueeze(1).to_broadcast([P, tn, 128]), ALU.add).then_inc(free[b], 1)
                        for h in range(2):
                            for t in range(T):
                                for j, (c0, cn) in enumerate(COLS):
                                    wait_made(dve, m, "s", h, t, j)
                                    b = bank_of("s", h, t, j)
                                    nc.vector.tensor_reduce(mxp[:, h, t, j:j + 1], bank[0:P, b, 0:cn], X, ALU.max).then_inc(free[b], 1)
                            for t in (T - 2, T - 1):
                                for j in range(3):
                                    wait_copied(dve, m, "s", h, t, j)
                            nc.vector.tensor_reduce(nm[:, h, 0, :], mxp[:, h], X, ALU.max).then_inc(folded, 1)
                            dve.wait_ge(folded, m * 2 + (h + 1))
                            nc.vector.tensor_scalar(nm[:, h, 1, :], nm[:, h, 0, :], -1.0, None, ALU.mult).then_inc(negated, 1)
                        for h in range(2):
                            if h == 1:
                                finish(0)
                            for t in range(1, T):
                                if t == 1:
                                    for j in range(3):
                                        wait_copied(dve, m, "p", h, 0, j)
                                else:
                                    dve.wait_ge(added, m * (2 * (T - 1)) + ((h + 1) * (T - 1) + t - 1))
                                for j in range(3):
                                    wait_copied(dve, m, "p", h, t, j)
                                nc.vector.tensor_tensor(psum_k[:], pT[:, 0, :] if t == 1 else psum_k[:], pT[:, t, :], ALU.add).then_inc(added, 1)
                        finish(1)

            moved = sem("moved")
            with nc.Block() as block:
                @block.scalar
                def _(act):
                    for k in range(K):
                        nc.scalar.copy(xT[:, k, :], oT[:, k, :]).then_inc(moved, 1)

        def mean_layer(w_self, w_neigh, bias, relu, to):
            Asb = sb("A", [P, T, N], F32, c)
            aT = sb("aT", [128, K, N], F32, c)
            ws = sb("ws", [128, 2, K, D], F32, c)
            bs = sb("bs", [P, D], F32, c)
            tmp = sb("tmp", [P, 2, D], F32, c)
            ld, A_ld, agg, agg_kept, made, moved, step = (sem(n) for n in ("loaded", "A_loaded", "aggregated", "agg_kept", "made", "moved", "step"))
            with nc.Block() as block:
                @block.sync
                def _(sp):
                    sp.dma_start(Asb[:], A_dram).then_inc(A_ld, 16)
                    for i, w in enumerate((w_self, w_neigh)):
                        sp.dma_start(ws[:, i], w.rearrange("(k p) n -> p k n", p=128)).then_inc(ld, 16)
                    sp.dma_start(bs[:], spread(bias)).then_inc(ld, 16)

                @block.tensor
                def _(pe):
                    pe.wait_ge(A_ld, 16)
                    g = 0
                    for c0, cn in COLS:
                        for k in range(K):
                            if g >= 4:
                                pe.wait_ge(agg_kept, g - 3)
                            for s in range(T):
                                last = nc.tensor.matmul(bank[:, g % 4, 0:cn], xn[:, s, k * 128:(k + 1) * 128], Asb[:, s, c0:c0 + cn], start=(s == 0), stop=(s == T - 1))
                            last.then_inc(agg, 1)
                            g += 1
                    pe.wait_ge(agg_kept, g)
                    pe.wait_ge(ld, 48)
                    for t in range(T):
                        if t >= 2:
                            pe.wait_ge(moved, t - 1)
                        for i, lhs in enumerate((xT, aT)):
                            for k in range(K):
                                last = nc.tensor.matmul(bank[0:P, 4 + 2 * (t % 2) + i, :], lhs[:, k, t * P:(t + 1) * P], ws[:, i, k, :], start=(k == 0), stop=(k == K - 1))
                        last.then_inc(made, 1)

                @block.scalar
                def _(act):
                    g = 0
                    for c0, cn in COLS:
                        for k in range(K):
                            act.wait_ge(agg, g + 1)
                            nc.scalar.copy(aT[:, k, c0:c0 + cn], bank[:, g % 4, 0:cn]).then_inc(agg_kept, 1)
                            g += 1

                @block.vector
                def _(dve):
                    v = [0]

                    def chain(ins):
                        v[0] += 1
                        ins.then_inc(step, 1)
                        dve.wait_ge(step, v[0])

                    dve.wait_ge(ld, 48)
                    for t in range(T):
                        dve.wait_ge(made, t + 1)
                        o = tmp[:, t % 2]
                        chain(nc.vector.tensor_tensor(o, bank[0:P, 4 + 2 * (t % 2), :], bs[:], ALU.add))
                        nc.vector.scalar_tensor_tensor(o, bank[0:P, 5 + 2 * (t % 2), :], rdeg[:, t:t + 1], o, ALU.mult, ALU.add).then_inc(moved, 1)
                        dve.wait_ge(moved, t + 1)
                        if relu:
                            chain(nc.vector.scalar_tensor_tensor(to[:, t], o, 0.0, to[:, t], ALU.max, ALU.add))
                        else:
                            chain(nc.vector.tensor_copy(to[:, t], o))

        U = N // 2 // P
        PC = N // 2
        W2 = D // 2

        def to_pairs():
            put, got = sem("x_put"), sem("x_got")
            with nc.Block() as block:
                @block.sync
                def _(sp):
                    sp.dma_start(x_dram.rearrange("(t p) d -> p t d", p=P), x[:]).then_inc(put, 16)
                    sp.wait_ge(put, 16)
                    sp.dma_start(x[:].rearrange("p (u r) d -> p u (r d)", r=2), x_dram.rearrange("(u p r) d -> p u (r d)", p=P, r=2)).then_inc(got, 16)
                    sp.wait_ge(got, 16)

        def from_pairs():
            put, got = sem("x_put"), sem("x_got")
            with nc.Block() as block:
                @block.sync
                def _(sp):
                    sp.dma_start(x_dram.rearrange("(u p r) d -> p u (r d)", p=P, r=2), x[:].rearrange("p (u r) d -> p u (r d)", r=2)).then_inc(put, 16)
                    sp.wait_ge(put, 16)
                    sp.dma_start(x[:], x_dram.rearrange("(t p) d -> p t d", p=P)).then_inc(got, 16)
                    sp.wait_ge(got, 16)

        def wavelet():
            F = FF // 128
            C2 = [(0, 375), (375, 250)]
            wi = sb("wi", [128, 2, D], F32, c)
            w1s = sb("w1s", [128, K, FF], F32, c)
            w2s = sb("w2s", [128, F, W2], F32, c)
            b1s = sb("b1s", [128, F], F32, c)
            b2s = sb("b2s", [P, W2], F32, c)
            sums = sb("sums", [P, U, D], F32, c)
            difs = sb("difs", [P, U, D], F32, c)
            low = sb("low", [P, U, 4, W2], F32, c)
            llT = sb("llT", [128, 2, PC], F32, c)
            upT = sb("upT", [128, K, PC], F32, c)
            hT = sb("hT", [128, F, PC], F32, c)
            nl = sb("nl", [P, 2, W2], F32, c)
            o = sb("o", [P, 6, W2], F32, c)
            ld, made, step, turned, kept, mm, mm_kept, last_made, moved = (sem(n) for n in (
                "loaded", "parts_made", "step", "ll_turned", "ll_kept", "product_made", "product_kept", "new_made", "new_moved"))
            pairs = xn[:].rearrange("p (u r) d -> p u r d", r=2)
            xp = x[:].rearrange("p (u r) d -> p u r d", r=2)
            with nc.Block() as block:
                @block.sync
                def _(sp):
                    sp.dma_start(wi[:], a["stretch"].rearrange("(k p) n -> p k n", p=128)).then_inc(ld, 16)
                    sp.dma_start(w1s[:], a["L2_ffn_fc1_w"].rearrange("(k p) n -> p k n", p=128)).then_inc(ld, 16)
                    sp.dma_start(w2s[:], a["L2_ffn_fc2_w"].rearrange("(k p) n -> p k n", p=128)).then_inc(ld, 16)
                    sp.dma_start(b1s[:], a["L2_ffn_fc1_b"].rearrange("(f p) -> p f", p=128), allow_slow_non_contiguous=True).then_inc(ld, 16)
                    sp.dma_start(b2s[:], spread(a["L2_ffn_fc2_b"])).then_inc(ld, 16)

                @block.tensor
                def _(pe):
                    for u in range(U):
                        pe.wait_ge(made, u + 1)
                        if u >= 2:
                            pe.wait_ge(kept, u - 1)
                        for k in range(2):
                            last = nc.tensor.transpose(bank[:, u % 2, k * P:(k + 1) * P], low[:, u, 0, k * 128:(k + 1) * 128], ident[0:P, 0:P])
                        last.then_inc(turned, 1)
                    pe.wait_ge(kept, U)
                    pe.wait_ge(ld, 80)
                    g = 0
                    for lhs, rhs, k_n, m_n in ((wi, llT, 2, K), (w1s, upT, K, F)):
                        if m_n == F:
                            pe.wait_ge(mm_kept, g)
                        for c0, cn in C2:
                            for m in range(m_n):
                                if g >= 2:
                                    pe.wait_ge(mm_kept, g - 1)
                                for k in range(k_n):
                                    last = nc.tensor.matmul(bank[:, 2 + g % 2, 0:cn], lhs[:, k, m * 128:(m + 1) * 128], rhs[:, k, c0:c0 + cn], start=(k == 0), stop=(k == k_n - 1))
                                last.then_inc(mm, 1)
                                g += 1
                    pe.wait_ge(mm_kept, g)
                    for u in range(U):
                        if u >= 2:
                            pe.wait_ge(moved, u - 1)
                        for k in range(F):
                            last = nc.tensor.matmul(bank[0:P, 4 + u % 2, 0:W2], hT[:, k, u * P:(u + 1) * P], w2s[:, k, :], start=(k == 0), stop=(k == F - 1))
                        last.then_inc(last_made, 1)

                @block.scalar
                def _(act):
                    act.wait_ge(ld, 80)
                    for u in range(U):
                        act.wait_ge(turned, u + 1)
                        nc.scalar.copy(llT[:, :, u * P:(u + 1) * P], bank[:, u % 2, 0:2 * P].rearrange("p (k n) -> p k n", k=2)).then_inc(kept, 1)
                    g = 0
                    for dst, m_n in ((upT, K), (hT, F)):
                        for c0, cn in C2:
                            for m in range(m_n):
                                act.wait_ge(mm, g + 1)
                                if dst is upT:
                                    nc.scalar.copy(dst[:, m, c0:c0 + cn], bank[:, 2 + g % 2, 0:cn]).then_inc(mm_kept, 1)
                                else:
                                    nc.scalar.activation(dst[:, m, c0:c0 + cn], bank[:, 2 + g % 2, 0:cn], ACT.Gelu, bias=b1s[:, m:m + 1]).then_inc(mm_kept, 1)
                                g += 1

                @block.vector
                def _(dve):
                    v = [0]

                    def chain(ins):
                        v[0] += 1
                        ins.then_inc(step, 1)
                        dve.wait_ge(step, v[0])

                    def half_sum(out, p_, q_, op):
                        return nc.vector.tensor_tensor(out, p_, q_, op)

                    for u in range(U):
                        nc.vector.tensor_tensor(sums[:, u], pairs[:, u, 0], pairs[:, u, 1], ALU.add).then_inc(step, 1)
                        nc.vector.tensor_tensor(difs[:, u], pairs[:, u, 0], pairs[:, u, 1], ALU.subtract).then_inc(step, 1)
                        v[0] += 2
                        dve.wait_ge(step, v[0])
                        s2 = sums[:, u].rearrange("p (w e) -> p e w", e=2)
                        d2 = difs[:, u].rearrange("p (w e) -> p e w", e=2)
                        for i, (q, op) in enumerate(((s2, ALU.add), (d2, ALU.add), (s2, ALU.subtract), (d2, ALU.subtract))):
                            last = nc.vector.tensor_tensor(low[:, u, i], q[:, 0], q[:, 1], op)
                        chain(last)
                        nc.vector.tensor_scalar(low[:, u].rearrange("p i w -> p (i w)"), low[:, u].rearrange("p i w -> p (i w)"), 0.5, None, ALU.mult).then_inc(made, 1)
                    dve.wait_ge(ld, 80)
                    dve.wait_ge(made, U)
                    for u in range(U):
                        dve.wait_ge(last_made, u + 1)
                        nc.vector.tensor_tensor(nl[:, u % 2], bank[0:P, 4 + u % 2, 0:W2], b2s[:], ALU.add).then_inc(moved, 1)
                        dve.wait_ge(moved, u + 1)
                        nc.vector.tensor_tensor(o[:, 0], nl[:, u % 2], low[:, u, 1], ALU.add)
                        nc.vector.tensor_tensor(o[:, 1], nl[:, u % 2], low[:, u, 1], ALU.subtract)
                        nc.vector.tensor_tensor(o[:, 2], low[:, u, 2], low[:, u, 3], ALU.add)
                        chain(nc.vector.tensor_tensor(o[:, 3], low[:, u, 2], low[:, u, 3], ALU.subtract))
                        for r in range(2):
                            nc.vector.tensor_tensor(o[:, 4], o[:, r], o[:, 2 + r], ALU.add)
                            chain(nc.vector.tensor_tensor(o[:, 5], o[:, r], o[:, 2 + r], ALU.subtract))
                            for e in range(2):
                                to = xp[:, u, r].rearrange("p (w e) -> p e w", e=2)[:, e]
                                last = nc.vector.scalar_tensor_tensor(to, o[:, 4 + e], 0.5, to, ALU.mult, ALU.add)
                            chain(last)

        def scale_rows(pmax):
            s = sem("scaled")
            with nc.Block() as block:
                @block.vector
                def _(dve):
                    for t in range(T):
                        nc.vector.tensor_scalar(xn[:, t], xn[:, t], pmax[:, t:t + 1], None, ALU.mult).then_inc(s, 1)
                    nc.vector.memset(y_out[:], 0.0)

        def reorder(oh):
            f = sb("f", [P, 8, T, NX], F32, c)
            pos = sb("pos", [P, T], F32, c)
            pos_i = sb("pos_i", [P, T], I32, c)
            got = sb("got", [P, T, D], F32, c)
            counted, step, ready, put, back, added, stored = (sem(n) for n in ("counted", "step", "pos_ready", "rows_put", "rows_back", "added", "stored"))
            put = dma_sem("rows_put")
            with nc.Block() as block:
                @block.tensor
                def _(pe):
                    v = oh[:].rearrange("p t e -> p (t e)")
                    nc.tensor.matmul(bank[0:P, 0, 0:T * NX], above[0:P, 0:P], v, start=True, stop=True)
                    nc.tensor.matmul(bank[0:P, 1, 0:T * NX], ones[0:P, 0:P], v, start=True, stop=True).then_inc(counted, 1)

                @block.vector
                def _(dve):
                    v = [0]

                    def chain(ins):
                        v[0] += 1
                        ins.then_inc(step, 1)
                        dve.wait_ge(step, v[0])

                    dve.wait_ge(counted, 1)
                    nc.vector.tensor_copy(f[:, 0].rearrange("p t e -> p (t e)"), bank[0:P, 0, 0:T * NX])
                    chain(nc.vector.tensor_copy(f[:, 1].rearrange("p t e -> p (t e)"), bank[0:P, 1, 0:T * NX]))
                    for e in range(NX):
                        last = nc.vector.tensor_tensor_scan(f[:, 2, :, e], ones[0:P, 0:T], f[:, 1, :, e], 0.0, ALU.mult, ALU.add)
                    chain(last)
                    chain(nc.vector.tensor_tensor_scan(f[:, 3, 0, :], ones[0:P, 0:NX], f[:, 2, T - 1, :], 0.0, ALU.mult, ALU.add))
                    chain(nc.vector.tensor_tensor(f[:, 3, 1, :], f[:, 3, 0, :], f[:, 2, T - 1, :], ALU.subtract))
                    chain(nc.vector.tensor_tensor(f[:, 4], f[:, 2], f[:, 1], ALU.subtract))
                    chain(nc.vector.tensor_tensor(f[:, 4], f[:, 4], f[:, 0], ALU.add))
                    chain(nc.vector.tensor_tensor(f[:, 4], f[:, 4], f[:, 3, 1, :].unsqueeze(1).to_broadcast([P, T, NX]), ALU.add))
                    chain(nc.vector.tensor_tensor(f[:, 4], f[:, 4], oh[:], ALU.mult))
                    chain(nc.vector.tensor_reduce(pos[:], f[:, 4], X, ALU.add))
                    nc.vector.tensor_copy(pos_i[:], pos[:]).then_inc(ready, 1)
                    for t in range(T):
                        dve.wait_ge(back, 16 * T)
                        nc.vector.tensor_tensor(x[:, t], x[:, t], got[:, t], ALU.add).then_inc(added, 1)

                @block.gpsimd
                def _(pool):
                    pool.wait_ge(ready, 1)
                    for t in range(T):
                        nc.gpsimd.indirect_dma_start(out=y_dram, out_offset=bass.IndirectOffsetOnAxis(ap=pos_i[:, t:t + 1], axis=0),
                                                     in_=y_out[:, t, :], in_offset=None).then_inc(put, 16)
                    pool.wait_ge(put, 16 * T)

                @block.sync
                def _(sp):
                    sp.wait_ge(put, 16 * T)
                    for t in range(T):
                        sp.dma_start(got[:, t], y_dram[t * P:(t + 1) * P, :]).then_inc(back, 16)
                    for t in range(T):
                        sp.wait_ge(added, t + 1)
                        sp.dma_start(out[t * P:(t + 1) * P, :], x[:, t]).then_inc(stored, 16)
                    sp.wait_ge(stored, 16 * T)

        def run(stage, *args, **kw):
            nonlocal c
            outer = c
            with ExitStack() as c:
                stage(*args, **kw)
            c = outer
            if not sems:
                return
            for s in cleared_sems:
                nc.release_semaphore(s)
            for s in sems:
                nc.gpsimd.sem_clear(s)
            cleared_sems[:] = sems
            sems.clear()

        c = None
        run(constants)
        run(sort_edges)
        run(count_matrix)
        if last == -1:
            return x, dict(A=A_dram, table=table)
        gate = sb("gate", [P, T, NX])
        picks = sb("picks", [P, 2, T, NX])
        pmax = sb("pmax", [P, T])
        none = dict()
        run(norm, x, xn)
        run(gcn)
        if last == 0:
            return x, none
        run(norm, x, xn)
        run(route, "L0_ffn_router_w", None, gate, "two", None, picks)
        run(experts, "L0_ffn_w1", "L0_ffn_b1", "L0_ffn_w2", "L0_ffn_b2", gate, [picks[:, 0], picks[:, 1]], ACT.Gelu, x)
        if last == 1:
            return x, none
        run(norm, x, xn)
        run(edge_attention)
        run(turn_rows, xn)
        run(project, xT, K, a["L1_gnn_Wo"], a["L1_gnn_bo"], x)
        if last == 2:
            return x, none
        run(norm, x, xn)
        run(full_attention)
        run(project, xT, K, a["L1_ffn_Wo"], a["L1_ffn_bo"], xn)
        run(norm, xn, xn, "L1_ffn_g1", "L1_ffn_beta1")
        run(route, "L1_ffn_Wg", "L1_ffn_bg", gate, "one")
        run(experts, "L1_ffn_W1", "L1_ffn_b1", "L1_ffn_W2", "L1_ffn_b2", gate, [gate[:]], ACT.Gelu, xn)
        run(norm, xn, xn, "L1_ffn_g2", "L1_ffn_beta2", False, False, x)
        if last == 3:
            return x, none
        run(norm, x, xn)
        run(mean_layer, a["L2_gnn_W"][0:D, :], a["L2_gnn_W"][D:2 * D, :], a["L2_gnn_b"], True, x)
        if last == 4:
            return x, none
        run(to_pairs)
        run(norm, x, xn, None, None, False)
        run(wavelet)
        run(from_pairs)
        if last == 5:
            return x, none
        run(norm, x, xn)
        run(mean_layer, a["L3_gnn_w_self"], a["L3_gnn_w_neigh"], a["L3_gnn_bias"], False, xn)
        run(norm, xn, xn, "L3_gnn_gamma", "L3_gnn_beta", False, True, x)
        if last == 6:
            return x, none
        run(norm, x, xn)
        run(route, "L3_ffn_Wg", "L3_ffn_bg", gate, "one", pmax)
        y_out = sb("y_out", [P, T, D])
        run(scale_rows, pmax)
        run(experts, "L3_ffn_W1", "L3_ffn_b1", "L3_ffn_W2", "L3_ffn_b2", gate, [gate[:]], ACT.Relu, y_out)
        run(reorder, gate)



def stretch_matrix():
    import numpy as np
    n, m = D // 2, D
    pos = np.linspace(0.0, 1.0, m, dtype=np.float32) * np.float32(n - 1)
    i0 = np.clip(np.floor(pos).astype(np.int32), 0, n - 2)
    w = pos - i0.astype(np.float32)
    out = np.zeros((n, m), np.float32)
    out[i0, np.arange(m)] = np.float32(1.0) - w
    out[i0 + 1, np.arange(m)] = w
    return out


def lay_out(inputs):
    import numpy as np
    arrays = {k: np.ascontiguousarray(np.asarray(v)) for k, v in inputs.items()}
    for name, axes in (("L0_ffn_router_w", (1, 0)), ("L0_ffn_w1", (0, 2, 1)), ("L0_ffn_w2", (0, 2, 1)),
                       ("L2_ffn_fc1_w", (1, 0)), ("L2_ffn_fc2_w", (1, 0)), ("L3_gnn_w_self", (1, 0)), ("L3_gnn_w_neigh", (1, 0))):
        arrays[name] = np.ascontiguousarray(arrays[name].transpose(axes))
    arrays["stretch"] = stretch_matrix()
    return arrays


def kernel(**inputs):
    import numpy as np
    import concourse.bacc as bacc
    from concourse.bass_utils import run_bass_kernel_spmd

    nc = bacc.Bacc("TRN2", target_bir_lowering=False, num_devices=1)
    arrays, views = {}, {}
    for name, array in lay_out(inputs).items():
        arrays[f"in_{name}_dram"] = array
        views[name] = nc.dram_tensor(f"in_{name}_dram", array.shape, mybir.dt.from_np(array.dtype), kind="ExternalInput").ap()
    out = nc.dram_tensor("out_0_dram", (N, D), F32, kind="ExternalOutput").ap()
    build(nc, views, out)
    result = run_bass_kernel_spmd(nc, [arrays], core_ids=[0])
    return np.asarray(result.results[0]["out_0_dram"])
```

```python
from contextlib import ExitStack

import concourse.bass as bass
from concourse import mybir

F32 = mybir.dt.float32
BF16 = mybir.dt.bfloat16
F16 = mybir.dt.float16
I32 = mybir.dt.int32
ALU = mybir.AluOpType
ACT = mybir.ActivationFunctionType
X = mybir.AxisListType.X

N, D = 1250, 512
P = 125
T = N // P
K = D // 128
E = 20000
EC = E // P
S = 128
S2 = 2 * S
G = 4
R = 4
PAIRS = (E + T * (S2 - 1)) // S2
SC = 2 * PAIRS
assert SC % (R * G) == 0
MAGIC = 1.5 * 2.0 ** 23
ROWS = S * SC
RW = 11
H, DH = 8, 64
NX = 8
FF = 256
SLOT_TILES = 28
NEG = -1.0e30
COLS = [(0, 500), (500, 500), (1000, 250)]


def build(nc, a, out):
    ctx = ExitStack()
    names = iter(range(10000))
    sems, cleared_sems = [], []

    def sb(name, shape, dt=F32, c=None):
        return (c or ctx).enter_context(nc.sbuf_tensor(f"{name}_{next(names)}", shape, dt))

    def dma_sem(name):
        return nc.alloc_semaphore(f"{name}_{next(names)}")

    def sem(name):
        sems.append(nc.alloc_semaphore(f"{name}_{next(names)}"))
        return sems[-1]

    def dram(name, shape, dt=F32):
        return nc.dram_tensor(name, shape, dt).ap()

    def spread(v, p=P):
        return v.partition_broadcast(p)

    with ctx:
        bank = ctx.enter_context(nc.psum_tensor("bank", [128, 8, 512], F32))
        x = sb("x", [P, T, D])
        xn = sb("xn", [P, T, D])
        xT = sb("xT", [128, K, N])
        ident = sb("ident", [128, 128])
        ones = sb("ones", [128, 128])
        below = sb("below", [128, 128])
        above = sb("above", [128, 128])
        iota = sb("iota", [128, N])
        lane = sb("lane", [128, 1])
        i8 = sb("i8", [P, NX])
        dinv = sb("dinv", [P, T])
        rdeg = sb("rdeg", [P, T])
        last_row = sb("last_row", [P, T], I32)
        bounds = sb("bounds", [1, T + 1], I32)

        x_ld = dma_sem("x_loaded")

        A_dram = dram("count_matrix", (P, T, N))
        table = dram("edge_table", (ROWS, RW))
        k_dram = dram("k_rows", (N, D))
        v_dram = dram("v_rows", (N, D))
        run_dram = dram("running_max", (ROWS, H))
        x_dram = dram("x_rows", (N, D))
        y_dram = dram("y_rows", (N, D))
        x_slots = dram("x_slots", (SLOT_TILES * 128, D))
        y_slots = dram("y_slots", (SLOT_TILES * 128, D))
        key_dram = dram("edge_keys", (2, E))

        def load_bounds(eng):
            return [eng.value_load(bounds[0:1, t:t + 1], min_val=t, max_val=PAIRS - T + t) for t in range(T + 1)]

        def constants():
            iota_i = sb("iota_i", [128, N], I32, c)
            lane_i = sb("lane_i", [128, 1], I32, c)
            made, filled, masked = sem("iotas_made"), sem("ones_filled"), sem("masks_made")
            with nc.Block() as block:
                @block.sync
                def _(sp):
                    sp.dma_start(x[:], a["x"].rearrange("(t p) d -> p t d", p=P)).then_inc(x_ld, 16)

                @block.gpsimd
                def _(pool):
                    nc.gpsimd.iota(iota_i[:], [[1, N]], base=0, channel_multiplier=0).then_inc(made, 1)
                    nc.gpsimd.iota(lane_i[:], [[0, 1]], base=0, channel_multiplier=1).then_inc(made, 1)
                    nc.gpsimd.memset(ones[:], 1.0).then_inc(filled, 1)
                    pool.wait_ge(filled, 1)
                    for m, op, sign in ((ident, ALU.is_equal, 1), (below, ALU.is_gt, 1), (above, ALU.is_gt, -1)):
                        nc.gpsimd.affine_select(out=m[:], in_=ones[:], compare_op=op, fill=0.0, base=0,
                                                pattern=[[-sign, 128]], channel_multiplier=sign).then_inc(masked, 1)
                    pool.wait_ge(masked, 3)

                @block.vector
                def _(dve):
                    dve.wait_ge(made, 2)
                    nc.vector.tensor_copy(iota[:], iota_i[:]).then_inc(made, 1)
                    nc.vector.tensor_copy(lane[:], lane_i[:]).then_inc(made, 1)
                    dve.wait_ge(made, 4)
                    nc.vector.tensor_scalar(i8[:], iota[:P, 0:NX], float(NX), None, ALU.subtract).then_inc(made, 1)
                    dve.wait_ge(made, 5)

        def scatter_records(pool, rec, pos_i, chunks, put, ready=None):
            for n in chunks:
                if ready is not None and n % 8 == 0:
                    pool.wait_ge(ready, n // 8 + 1)
                nc.gpsimd.indirect_dma_start(
                    out=table, out_offset=bass.IndirectOffsetOnAxis(ap=pos_i[:, n:n + 1], axis=0),
                    in_=rec[:, n, :], in_offset=None).then_inc(put, 16)

        def sort_edges(rec, pos_i, put, chunks):
            G = 8
            NB = EC // G
            start = sb("start", [P, T], F32, c)
            cnt = sb("cnt", [P, T], F32, c)
            cols_i = sb("cols_i", [128, 2, 2 * P], I32, c)
            cols_f = sb("cols_f", [128, 2, 2 * P], F32, c)
            edge_j = sb("edge_j", [P, EC], F32, c)
            edge_t = sb("edge_t", [P, EC], F32, c)
            oht = sb("oht", [P, EC, T], F32, c)
            oht16 = sb("oht16", [P, EC, T], F16, c)
            edge_j16 = sb("edge_j16", [P, EC], F16, c)
            iota16 = sb("iota16", [P, P], F16, c)
            ohj = sb("ohj", [P, 2, G, P], F16, c)
            tiles = sb("tiles", [P, T], F32, c)
            hist = sb("hist", [P, EC, T], F32, c)
            cum = sb("cum", [P, T, EC], F32, c)
            one_row = sb("one_row", [P, EC], F32, c)
            tot = sb("tot", [P, 5, T], F32, c)
            fill = sb("fill", [S, SC, RW], F32, c)
            blank = sb("blank", [128, 2, D], F32, c)
            cols_j = sb("cols_j", [128, 2, 2 * P], F32, c)
            row = sb("row", [P, 2, 2, G * P], F32, c)
            ohjT = sb("ohjT", [P, 2, G, P], F32, c)
            same = sb("same", [P, G, P], F32, c)
            earlier = sb("earlier", [P, G, P], F32, c)
            part = sb("part", [P, G, T], F32, c)
            pos = sb("pos", [P, 5, EC], F32, c)
            lo = sb("lo", [P, EC], F32, c)
            ld, ld_attr, turned, step = sem("edges_loaded"), sem("attr_loaded"), sem("edges_turned"), sem("dve_step")
            ohj_made, hist_made, hist_kept = sem("ohj_made"), sem("hist_made"), sem("hist_kept")
            base_made, row_free = sem("base_made"), sem("row_free")
            row_ld = [sem(f"row_loaded{h}") for h in range(2)]
            ohjT_made, looked, taken = sem("ohjT_made"), sem("looked_up"), sem("lookup_taken")
            null_made, null_put, ready = sem("null_made"), sem("null_put"), sem("pos_ready")
            keys_made, keys_put = sem("keys_made"), sem("keys_put")
            blank_made, blank_put = sem("blank_made"), sem("blank_put")
            with nc.Block() as block:
                @block.sync
                def _(sp):
                    for i, name in enumerate(("src", "dst")):
                        v = a[name].rearrange("(c p) -> c p", p=P)
                        sp.dma_start(cols_i[:, i, 0:P], v[0:128, :]).then_inc(ld, 16)
                        sp.dma_start(cols_i[0:EC - 128, i, P:2 * P], v[128:EC, :]).then_inc(ld, 16)
                    sp.dma_start(rec[:, :, 2:2 + H], a["edge_attr_8"].rearrange("(c p) h -> p c h", p=P)).then_inc(ld_attr, 16)
                    sp.wait_ge(null_made, 2)
                    sp.dma_start(table.rearrange("(p c) w -> p c w", p=S), fill[:]).then_inc(null_put, 16)
                    sp.wait_ge(keys_made, 1)
                    for i, keys in enumerate((cols_f[:, 0], cols_j[:, 1])):
                        v = key_dram[i, :].rearrange("(c p) -> c p", p=P)
                        sp.dma_start(v[0:128, :], keys[:, 0:P]).then_inc(keys_put, 16)
                        sp.dma_start(v[128:EC, :], keys[0:EC - 128, P:2 * P]).then_inc(keys_put, 16)
                    sp.wait_ge(keys_put, 64)
                    v = key_dram.rearrange("k (a n) -> k a n", n=G * P)
                    with sp.Fori(0, NB // 2) as b:
                        for h in range(2):
                            sp.wait_ge(row_free, b * 2 + (h + 1))
                            sp.dma_start(row[:, h], v[:, bass.ds(b * 2 + h, 1), :].rearrange("k a n -> k (a n)").partition_broadcast(P)).then_inc(row_ld[h], 16)
                    sp.wait_ge(blank_made, 1)
                    v = x_slots.rearrange("(n u p) d -> n p u d", u=2, p=128)
                    for n in range(SLOT_TILES // 2):
                        sp.dma_start(v[n], blank[:]).then_inc(blank_put, 16)
                    v = y_slots.rearrange("(n u p) d -> n p u d", u=2, p=128)
                    reached = 2 * N // 256
                    for n in range(reached, SLOT_TILES // 2):
                        sp.dma_start(v[n], blank[:]).then_inc(blank_put, 16)
                    sp.wait_ge(blank_put, 16 * (SLOT_TILES - reached))
                    sp.wait_ge(x_ld, 16)

                @block.gpsimd
                def _(pool):
                    nc.gpsimd.memset(blank[:], 0.0).then_inc(blank_made, 1)
                    nc.gpsimd.memset(fill[:], 0.0).then_inc(null_made, 1)
                    pool.wait_ge(null_made, 1)
                    nc.gpsimd.memset(fill[:, :, RW - 1:RW], -1.0)
                    nc.gpsimd.memset(fill[:, :, 0:1], -1.0).then_inc(null_made, 1)
                    pool.wait_ge(null_put, 16)
                    pool.wait_ge(ld_attr, 16)
                    scatter_records(pool, rec, pos_i, chunks, put, ready)

                @block.tensor
                def _(pe):
                    pe.wait_ge(step, 2)
                    for i in range(2):
                        nc.tensor.transpose(bank[0:P, i, 0:128], cols_f[:, i, 0:P], ident[:])
                        last = nc.tensor.transpose(bank[0:P, i, 128:EC], cols_f[0:EC - 128, i, P:2 * P], ident[0:EC - 128, 0:EC - 128])
                    last.then_inc(turned, 1)
                    for n in range(NB):
                        pe.wait_ge(ohj_made, n + 1)
                        if n >= 2:
                            pe.wait_ge(hist_kept, n - 1)
                        for g in range(G):
                            last = nc.tensor.matmul(bank[0:P, 4 + n % 2, g * T:(g + 1) * T], ohj[:, n % 2, g, :], oht16[:, n * G + g, :], start=True, stop=True)
                        last.then_inc(hist_made, 1)
                    pe.wait_ge(base_made, 1)
                    nc.tensor.matmul(bank[0:P, 0, 0:T], above[0:P, 0:P], cnt[:], start=True, stop=True)
                    nc.tensor.matmul(bank[0:P, 0, T:2 * T], ones[0:P, 0:P], cnt[:], start=True, stop=True).then_inc(base_made, 1)
                    with pe.Fori(0, NB // 2) as b:
                        for h in range(2):
                            pe.wait_ge(ohjT_made, b * 2 + h + 1)
                            pe.wait_ge(taken, b * 2 + (h + 1))
                            for g in range(G):
                                last = nc.tensor.matmul(bank[0:P, 3, g * T:(g + 1) * T], ohjT[:, h, g, :],
                                                        hist[:, bass.ds(b * (2 * G) + (h * G + g), 1), :].rearrange("p a t -> p (a t)"), start=True, stop=True)
                            last.then_inc(looked, 1)

                @block.scalar
                def _(act):
                    for n in range(NB):
                        act.wait_ge(hist_made, n + 1)
                        nc.scalar.copy(hist[:, n * G:(n + 1) * G, :].rearrange("p c t -> p (c t)"), bank[0:P, 4 + n % 2, 0:G * T]).then_inc(hist_kept, 1)

                @block.vector
                def _(dve):
                    v = [0]

                    def chain(ins):
                        v[0] += 1
                        ins.then_inc(step, 1)
                        dve.wait_ge(step, v[0])

                    for s in (row_free, row_free, taken):
                        dve.sem_inc(s, 1)
                    dve.wait_ge(ld, 64)
                    nc.vector.memset(one_row[:], 1.0)
                    nc.vector.tensor_scalar(tiles[:], iota[0:P, 0:T], float(P), None, ALU.mult)
                    chain(nc.vector.memset(cols_f[:], 0.0))
                    nc.vector.tensor_copy(cols_f[:, :, 0:P], cols_i[:, :, 0:P])
                    chain(nc.vector.tensor_copy(cols_f[0:EC - 128, :, P:2 * P], cols_i[0:EC - 128, :, P:2 * P]))
                    def within(out, q, v, n):
                        chain(nc.vector.tensor_scalar(q, v, -(n - 1) / 2, 1.0 / n, ALU.add, ALU.mult))
                        chain(nc.vector.tensor_scalar(q, q, MAGIC, MAGIC, ALU.add, ALU.subtract))
                        chain(nc.vector.scalar_tensor_tensor(out, q, -float(n), v, ALU.mult, ALU.add))

                    within(cols_j[:, 1], cols_j[:, 0], cols_f[:, 0], P)
                    nc.vector.tensor_copy(lo[:, 0:1], lane[0:P]).then_inc(keys_made, 1)
                    dve.wait_ge(turned, 1)
                    nc.vector.tensor_copy(rec[:, :, RW - 1:RW].rearrange("p c a -> p (c a)"), bank[0:P, 0, 0:EC])
                    chain(nc.vector.tensor_copy(rec[:, :, 1:2].rearrange("p c a -> p (c a)"), bank[0:P, 1, 0:EC]))
                    srcf = rec[:, :, RW - 1:RW].rearrange("p c a -> p (c a)")
                    within(edge_j[:], edge_t[:], srcf, P)
                    nc.vector.tensor_copy(rec[:, :, 0:1].rearrange("p c a -> p (c a)"), edge_j[:])
                    chain(nc.vector.tensor_tensor(edge_t[:], srcf, edge_j[:], ALU.subtract))
                    chain(nc.vector.tensor_tensor(oht[:], edge_t[:].unsqueeze(2).to_broadcast([P, EC, T]),
                                                  tiles[:].unsqueeze(1).to_broadcast([P, EC, T]), ALU.is_equal))
                    nc.vector.tensor_copy(oht16[:], oht[:])
                    nc.vector.tensor_copy(edge_j16[:], edge_j[:])
                    chain(nc.vector.tensor_copy(iota16[:], iota[0:P, 0:P]))
                    for n in range(NB):
                        if n >= 2:
                            dve.wait_ge(hist_made, n - 1)
                        nc.vector.tensor_tensor(ohj[:, n % 2], iota16[:].unsqueeze(1).to_broadcast([P, G, P]),
                                                edge_j16[:, n * G:(n + 1) * G].unsqueeze(2).to_broadcast([P, G, P]),
                                                ALU.is_equal).then_inc(ohj_made, 1)
                    dve.wait_ge(hist_kept, NB)
                    for t in range(T):
                        last = nc.vector.tensor_tensor_scan(cum[:, t, :], one_row[:], hist[:, :, t], 0.0, ALU.mult, ALU.add)
                    chain(last)
                    chain(nc.vector.tensor_copy(cnt[:], cum[:, :, EC - 1]))
                    nc.vector.tensor_copy(tot[:, 4], cnt[:]).then_inc(base_made, 1)
                    dve.wait_ge(base_made, 2)
                    chain(nc.vector.tensor_scalar(tot[:, 0], bank[0:P, 0, T:2 * T], 1.0, float(S2 - 1), ALU.max, ALU.add))
                    within(tot[:, 2], tot[:, 1], tot[:, 0], S2)
                    chain(nc.vector.tensor_tensor(tot[:, 0], tot[:, 0], tot[:, 2], ALU.subtract))
                    chain(nc.vector.tensor_tensor_scan(tot[:, 1], one_row[:, 0:T], tot[:, 0], 0.0, ALU.mult, ALU.add))
                    chain(nc.vector.tensor_tensor(tot[:, 2], tot[:, 1], tot[:, 0], ALU.subtract))
                    chain(nc.vector.tensor_tensor(start[:], tot[:, 2], bank[0:P, 0, 0:T], ALU.add))
                    chain(nc.vector.tensor_scalar(tot[:, 3], tot[:, 1], 1.0 / S2, None, ALU.mult))
                    chain(nc.vector.memset(tot[:, 3, T - 1:T], float(PAIRS)))
                    chain(nc.vector.memset(bounds[:], 0))
                    chain(nc.vector.tensor_copy(bounds[0:1, 1:T + 1], tot[0:1, 3, :]))
                    chain(nc.vector.tensor_tensor(tot[:, 0], start[:], cnt[:], ALU.add))
                    chain(nc.vector.tensor_scalar(tot[:, 0], tot[:, 0], -1.0, 0.0, ALU.add, ALU.max))
                    within(tot[:, 2], tot[:, 1], tot[:, 0], S)
                    chain(nc.vector.scalar_tensor_tensor(tot[:, 0], tot[:, 2], float(SC), tot[:, 1], ALU.mult, ALU.add))
                    chain(nc.vector.tensor_copy(last_row[:], tot[:, 0]))
                    cumv = cum[:].rearrange("p t c -> p c t")
                    chain(nc.vector.tensor_tensor(hist[:], cumv, hist[:], ALU.subtract))
                    chain(nc.vector.tensor_tensor(hist[:], hist[:], start[:].unsqueeze(1).to_broadcast([P, EC, T]), ALU.add))
                    first = v[0]
                    with dve.Fori(0, NB // 2) as b:
                        for h in range(2):
                            n = b * 2 + h
                            dve.wait_ge(row_ld[h], b * 16 + 16)
                            nc.vector.tensor_scalar(ohjT[:, h].rearrange("p g e -> p (g e)"), row[:, h, 1], lane[0:P], None, ALU.is_equal).then_inc(ohjT_made, 1)
                            nc.vector.tensor_tensor(same[:], row[:, h, 0].rearrange("p (g e) -> p g e", g=G),
                                                    rec[:, bass.ds(n * G, G), RW - 1:RW].to_broadcast([P, G, P]), ALU.is_equal).then_inc(row_free, 1)
                            dve.wait_ge(row_free, n + 3)
                            nc.vector.tensor_tensor(earlier[:], same[:], below[0:P, 0:P].unsqueeze(1).to_broadcast([P, G, P]), ALU.mult).then_inc(step, 1)
                            dve.wait_ge(step, n * 8 + (first + 1))
                            nc.vector.tensor_reduce(pos[:, 0, bass.ds(n * G, G)], earlier[:], X, ALU.add).then_inc(step, 1)
                            dve.wait_ge(looked, n + 1)
                            nc.vector.tensor_tensor(part[:], bank[0:P, 3, 0:G * T].rearrange("p (g t) -> p g t", g=G),
                                                    oht[:, bass.ds(n * G, G), :], ALU.mult).then_inc(taken, 1)
                            dve.wait_ge(taken, n + 2)
                            here = bass.ds(n * G, G)
                            nc.vector.tensor_reduce(pos[:, 1, here], part[:], X, ALU.add).then_inc(step, 1)
                            dve.wait_ge(step, n * 8 + (first + 3))
                            nc.vector.tensor_tensor(pos[:, 2, here], pos[:, 0, here], pos[:, 1, here], ALU.add).then_inc(step, 1)
                            dve.wait_ge(step, n * 8 + (first + 4))
                            nc.vector.tensor_scalar(pos[:, 3, here], pos[:, 2, here], -(S - 1) / 2, 1.0 / S, ALU.add, ALU.mult).then_inc(step, 1)
                            dve.wait_ge(step, n * 8 + (first + 5))
                            nc.vector.tensor_scalar(pos[:, 3, here], pos[:, 3, here], MAGIC, MAGIC, ALU.add, ALU.subtract).then_inc(step, 1)
                            dve.wait_ge(step, n * 8 + (first + 6))
                            nc.vector.tensor_scalar(pos[:, 4, here], pos[:, 2, here], float(SC), None, ALU.mult).then_inc(step, 1)
                            dve.wait_ge(step, n * 8 + (first + 7))
                            nc.vector.scalar_tensor_tensor(pos[:, 4, here], pos[:, 3, here], float(1 - S * SC), pos[:, 4, here], ALU.mult, ALU.add).then_inc(step, 1)
                            dve.wait_ge(step, n * 8 + (first + 8))
                            nc.vector.tensor_copy(pos_i[:, here], pos[:, 4, here]).then_inc(ready, 1)
                    dve.wait_ge(ready, NB)

        def count_matrix(Asb):
            recs = sb("recs", [S, SC, RW], F32, c)
            w = sb("w", [S, 2, P], F16, c)
            hot = sb("hot", [S, 2, N], F16, c)
            iota16 = sb("iota16", [S, N], F16, c)
            zero = sb("zero", [S, 512], F16, c)
            one = sb("one", [P, 2], F32, c)
            Asum = sb("Asum", [P, N], F32, c)
            added = sem("tiles_added")
            deg = sb("deg", [P, 3, T], F32, c)
            ld, zeroed, w_made, hot_made = (sem(n) for n in ("recs_loaded", "zeroed", "w_made", "hot_made"))
            used = [sem(f"hot_used{h}") for h in range(2)]
            tile_done, tile_kept, stored, degs, step = (sem(n) for n in ("tile_done", "tile_kept", "A_stored", "deg_made", "deg_step"))
            with nc.Block() as block:
                @block.sync
                def _(sp):
                    sp.dma_start(recs[:], table.rearrange("(p c) w -> p c w", p=S)).then_inc(ld, 16)
                    for t in range(T):
                        sp.wait_ge(tile_kept, t + 1)
                        sp.dma_start(A_dram[:, t, :], Asb[:, t, :]).then_inc(stored, 16)
                    sp.wait_ge(stored, 16 * T)

                @block.gpsimd
                def _(pool):
                    for t in range(1, T):
                        pool.wait_ge(tile_kept, t + 1)
                        if t > 1:
                            pool.wait_ge(added, t - 1)
                        nc.gpsimd.tensor_tensor(Asum[:], Asb[:, 0] if t == 1 else Asum[:], Asb[:, t], ALU.add).then_inc(added, 1)

                @block.vector
                def _(dve):
                    nc.vector.memset(one[:], 1.0)
                    nc.vector.memset(zero[:], 0.0).then_inc(zeroed, 1)
                    nc.vector.tensor_copy(iota16[:], iota[:]).then_inc(zeroed, 1)
                    dve.wait_ge(zeroed, 2)
                    dve.wait_ge(ld, 16)
                    for n in range(PAIRS):
                        for h in range(2):
                            dve.wait_ge(used[h], n + 1)
                            nc.vector.tensor_scalar(w[:, h], iota16[:, 0:P], recs[:, bass.ds(n * 2 + h, 1), 0:1].rearrange("p a b -> p (a b)"), None, ALU.is_equal).then_inc(w_made, 1)
                            nc.vector.tensor_scalar(hot[:, h], iota16[:], recs[:, bass.ds(n * 2 + h, 1), 1:2].rearrange("p a b -> p (a b)"), None, ALU.is_equal).then_inc(hot_made, 1)
                    dve.wait_ge(degs, 1)
                    nc.vector.tensor_scalar(deg[:, 0], bank[0:P, 6, 0:T], 1.0, None, ALU.max).then_inc(step, 1)
                    nc.vector.tensor_scalar(deg[:, 1], bank[0:P, 6, 0:T], 1.0, None, ALU.add).then_inc(step, 1)
                    dve.wait_ge(step, 3)
                    nc.vector.reciprocal(rdeg[:], deg[:, 0]).then_inc(step, 1)
                    nc.vector.reciprocal(dinv[:], deg[:, 2]).then_inc(step, 1)
                    dve.wait_ge(step, 5)

                @block.tensor
                def _(pe):
                    edge_pairs = load_bounds(pe)
                    for s in used:
                        pe.sem_inc(s, 1)
                    pe.wait_ge(zeroed, 1)
                    for t in range(T):
                        if t >= 2:
                            pe.wait_ge(tile_kept, t - 1)
                        for j, (c0, cn) in enumerate(COLS):
                            nc.tensor.matmul(bank[0:P, 3 * (t % 2) + j, 0:cn], zero[:, 0:P], zero[:, 0:cn], start=True, stop=False, skip_group_check=True)
                        with pe.Fori(edge_pairs[t], edge_pairs[t + 1]) as n:
                            for h in range(2):
                                pe.wait_ge(w_made, n * 2 + (h + 1))
                                pe.wait_ge(hot_made, n * 2 + (h + 1))
                                for j, (c0, cn) in enumerate(COLS):
                                    last = nc.tensor.matmul(bank[0:P, 3 * (t % 2) + j, 0:cn], w[:, h], hot[:, h, c0:c0 + cn], start=False, stop=False, skip_group_check=True)
                                last.then_inc(used[h], 1)
                        nc.tensor.matmul(bank[0:P, 7, 0:2], zero[:, 0:P], zero[:, 0:2], start=True, stop=True).then_inc(tile_done, 1)
                    pe.wait_ge(tile_kept, T)
                    pe.wait_ge(added, T - 1)
                    for d in range(T):
                        last = nc.tensor.matmul(bank[0:P, 6, d:d + 1], Asum[:, d * P:(d + 1) * P], one[:, 0:1], start=True, stop=True)
                    last.then_inc(degs, 1)

                @block.scalar
                def _(act):
                    for t in range(T):
                        act.wait_ge(tile_done, t + 1)
                        for j, (c0, cn) in enumerate(COLS):
                            last = nc.scalar.copy(Asb[:, t, c0:c0 + cn], bank[0:P, 3 * (t % 2) + j, 0:cn])
                        last.then_inc(tile_kept, 1)
                    act.wait_ge(step, 2)
                    nc.scalar.activation(deg[:, 2], deg[:, 1], ACT.Sqrt).then_inc(step, 1)

        def norm(src, dst, scale=None, shift=None, turn=True, relu=False, add_to=None, also=None, scatter=None):
            stats = sb("stats", [P, T, 6], F32, c)
            mv = sb("mv", [P, T, 2], F32, c)
            std = sb("std", [P, 3, T], F32, c)
            gb = sb("gb", [P, 2, D], F32, c)
            counted, merged, var_made, std_made, rstd_made = (sem(n) for n in ("counted", "merged", "var_made", "std_made", "rstd_made"))
            normed, scaled, shifted, turned, kept, ld = (sem(n) for n in ("normed", "scaled", "shifted", "turned", "kept", "affine_loaded"))
            done = normed if scale is None else shifted
            with nc.Block() as block:
                @block.sync
                def _(sp):
                    if scale is not None:
                        sp.dma_start(gb[:, 0], spread(a[scale])).then_inc(ld, 16)
                        sp.dma_start(gb[:, 1], spread(a[shift])).then_inc(ld, 16)
                    if also is not None:
                        also(sp)

                if scatter is not None:
                    @block.gpsimd
                    def _(pool):
                        scatter(pool)

                @block.vector
                def _(dve):
                    for t in range(T):
                        nc.vector.bn_stats(stats[:, t], src[:, t]).then_inc(counted, 1)
                    for t in range(T):
                        dve.wait_ge(counted, t + 1)
                        nc.vector.bn_aggr(mv[:, t], stats[:, t]).then_inc(merged, 1)
                    dve.wait_ge(merged, T)
                    nc.vector.tensor_scalar(std[:, 0], mv[:, :, 1], 1e-5, None, ALU.add).then_inc(var_made, 1)
                    if scale is not None:
                        dve.wait_ge(ld, 32)
                        for t in range(T):
                            nc.vector.scalar_tensor_tensor(dst[:, t], src[:, t], mv[:, t, 0:1], gb[:, 0], ALU.subtract, ALU.mult).then_inc(scaled, 1)
                    dve.wait_ge(std_made, 1)
                    nc.vector.reciprocal(std[:, 2], std[:, 1]).then_inc(rstd_made, 1)
                    dve.wait_ge(rstd_made, 1)
                    if scale is None:
                        for t in range(T):
                            nc.vector.tensor_scalar(dst[:, t], src[:, t], mv[:, t, 0:1], std[:, 2, t:t + 1], ALU.subtract, ALU.mult).then_inc(normed, 1)
                    else:
                        for t in range(T):
                            dve.wait_ge(scaled, t + 1)
                            nc.vector.scalar_tensor_tensor(dst[:, t], dst[:, t], std[:, 2, t:t + 1], gb[:, 1], ALU.mult, ALU.add).then_inc(shifted, 1)
                    if add_to is not None:
                        for t in range(T):
                            dve.wait_ge(done, t + 1)
                            if relu:
                                nc.vector.scalar_tensor_tensor(add_to[:, t], dst[:, t], 0.0, add_to[:, t], ALU.max, ALU.add)
                            else:
                                nc.vector.tensor_tensor(add_to[:, t], dst[:, t], add_to[:, t], ALU.add)

                @block.scalar
                def _(act):
                    act.wait_ge(var_made, 1)
                    nc.scalar.activation(std[:, 1], std[:, 0], ACT.Sqrt).then_inc(std_made, 1)
                    if turn:
                        for t in range(T):
                            act.wait_ge(turned, t + 1)
                            nc.scalar.copy(xT[:, :, t * P:(t + 1) * P], bank[:, t % 2, 0:K * P].rearrange("p (k n) -> p k n", k=K)).then_inc(kept, 1)

                if turn:
                    @block.tensor
                    def _(pe):
                        for t in range(T):
                            pe.wait_ge(done, t + 1)
                            if t >= 2:
                                pe.wait_ge(kept, t - 1)
                            for k in range(K):
                                last = nc.tensor.transpose(bank[:, t % 2, k * P:(k + 1) * P], dst[:, t, k * 128:(k + 1) * 128], ident[0:P, 0:P])
                            last.then_inc(turned, 1)

        def turn_rows(src, also):
            turned, kept = sem("turned"), sem("kept")
            with nc.Block() as block:
                @block.sync
                def _(sp):
                    also(sp)

                @block.tensor
                def _(pe):
                    for t in range(T):
                        if t >= 2:
                            pe.wait_ge(kept, t - 1)
                        for k in range(K):
                            last = nc.tensor.transpose(bank[:, t % 2, k * P:(k + 1) * P], src[:, t, k * 128:(k + 1) * 128], ident[0:P, 0:P])
                        last.then_inc(turned, 1)

                @block.scalar
                def _(act):
                    for t in range(T):
                        act.wait_ge(turned, t + 1)
                        nc.scalar.copy(xT[:, :, t * P:(t + 1) * P], bank[:, t % 2, 0:K * P].rearrange("p (k n) -> p k n", k=K)).then_inc(kept, 1)

        def project_weights(w, bias):
            ws = sb("ws", [128, K, D], F32, c)
            bs = sb("bs", [P, D], F32, c)
            ld = dma_sem("weights_loaded")

            def loads(sp):
                sp.dma_start(ws[:], w.rearrange("(k p) n -> p k n", p=128)).then_inc(ld, 16)
                sp.dma_start(bs[:], spread(bias)).then_inc(ld, 16)

            return (ws, bs, ld), loads

        def project(lhs, weights, to):
            ws, bs, ld = weights
            tmp = sb("tmp", [P, 2, D], F32, c)
            made, moved, summed = (sem(n) for n in ("made", "moved", "summed"))
            with nc.Block() as block:
                @block.tensor
                def _(pe):
                    pe.wait_ge(ld, 32)
                    for t in range(T):
                        if t >= 4:
                            pe.wait_ge(moved, t - 3)
                        for k in range(K):
                            last = nc.tensor.matmul(bank[0:P, t % 4, :], lhs[:, k, t * P:(t + 1) * P], ws[:, k, :], start=(k == 0), stop=(k == K - 1))
                        last.then_inc(made, 1)

                @block.vector
                def _(dve):
                    dve.wait_ge(ld, 32)
                    for t in range(T):
                        dve.wait_ge(made, t + 1)
                        nc.vector.tensor_tensor(tmp[:, t % 2], bank[0:P, t % 4, :], bs[:], ALU.add).then_inc(moved, 1)
                        dve.wait_ge(moved, t + 1)
                        nc.vector.tensor_tensor(to[:, t], to[:, t], tmp[:, t % 2], ALU.add).then_inc(summed, 1)

        def route(w, bias, gate, mode, pmax=None, picks=None):
            wr = sb("wr", [128, K, NX], F32, c)
            br = sb("br", [P, NX], F32, c)
            lg = sb("lg", [P, T, NX], F32, c)
            p = sb("p", [P, T, NX], F32, c)
            q = sb("q", [P, T, NX], F32, c)
            oh = sb("oh", [P, T, NX], F32, c)
            m = sb("m", [P, 6, T], F32, c)
            ld, made, step, shifted, exped = (sem(n) for n in ("router_loaded", "logits_made", "step", "logits_shifted", "exped"))
            with nc.Block() as block:
                @block.sync
                def _(sp):
                    sp.dma_start(wr[:], a[w].rearrange("(k p) n -> p k n", p=128)).then_inc(ld, 16)
                    if bias is not None:
                        sp.dma_start(br[:], spread(a[bias])).then_inc(ld, 16)

                @block.tensor
                def _(pe):
                    pe.wait_ge(ld, 16 if bias is None else 32)
                    for t in range(T):
                        for k in range(K):
                            last = nc.tensor.matmul(bank[0:P, 0, t * NX:(t + 1) * NX], xT[:, k, t * P:(t + 1) * P], wr[:, k, :], start=(k == 0), stop=(k == K - 1))
                    last.then_inc(made, 1)

                if mode == "two" or pmax is not None:
                    @block.scalar
                    def _(act):
                        act.wait_ge(shifted, 1)
                        nc.scalar.activation(p[:], q[:], ACT.Exp).then_inc(exped, 1)

                @block.vector
                def _(dve):
                    v = [0]

                    def chain(ins):
                        v[0] += 1
                        ins.then_inc(step, 1)
                        dve.wait_ge(step, v[0])

                    def wide(col):
                        return col.unsqueeze(2).to_broadcast([P, T, NX])

                    def first_best(oh_, vals, i):
                        chain(nc.vector.tensor_reduce(m[:, i], vals, X, ALU.max))
                        chain(nc.vector.tensor_tensor(oh_, vals, wide(m[:, i]), ALU.is_ge))
                        chain(nc.vector.tensor_tensor(oh_, oh_, i8[:].unsqueeze(1).to_broadcast([P, T, NX]), ALU.mult))
                        chain(nc.vector.tensor_reduce(m[:, 5], oh_, X, ALU.min))
                        chain(nc.vector.tensor_tensor(oh_, i8[:].unsqueeze(1).to_broadcast([P, T, NX]), wide(m[:, 5]), ALU.is_equal))

                    dve.wait_ge(ld, 16 if bias is None else 32)
                    dve.wait_ge(made, 1)
                    raw = bank[0:P, 0, 0:T * NX].rearrange("p (t e) -> p t e", t=T)
                    if bias is None:
                        chain(nc.vector.tensor_copy(lg[:], raw))
                    else:
                        chain(nc.vector.tensor_tensor(lg[:], raw, br[:].unsqueeze(1).to_broadcast([P, T, NX]), ALU.add))
                    if mode == "one" and pmax is None:
                        first_best(gate[:], lg[:], 0)
                        return
                    chain(nc.vector.tensor_reduce(m[:, 1], lg[:], X, ALU.max))
                    nc.vector.tensor_tensor(q[:], lg[:], wide(m[:, 1]), ALU.subtract).then_inc(shifted, 1)
                    dve.wait_ge(exped, 1)
                    chain(nc.vector.tensor_reduce(m[:, 2], p[:], X, ALU.add))
                    chain(nc.vector.reciprocal(m[:, 3], m[:, 2]))
                    chain(nc.vector.tensor_tensor(p[:], p[:], wide(m[:, 3]), ALU.mult))
                    if mode == "one":
                        first_best(gate[:], p[:], 0)
                        chain(nc.vector.tensor_copy(pmax[:], m[:, 0]))
                        return
                    first_best(picks[:, 0], p[:], 0)
                    chain(nc.vector.scalar_tensor_tensor(q[:], picks[:, 0], -4.0, p[:], ALU.mult, ALU.add))
                    first_best(picks[:, 1], q[:], 4)
                    chain(nc.vector.tensor_tensor(oh[:], picks[:, 0], picks[:, 1], ALU.add))
                    chain(nc.vector.tensor_tensor(p[:], p[:], oh[:], ALU.mult))
                    chain(nc.vector.tensor_reduce(m[:, 2], p[:], X, ALU.add))
                    chain(nc.vector.tensor_scalar(m[:, 2], m[:, 2], 1e-9, None, ALU.add))
                    chain(nc.vector.reciprocal(m[:, 3], m[:, 2]))
                    chain(nc.vector.tensor_tensor(gate[:], p[:], wide(m[:, 3]), ALU.mult))

        def experts(w1, b1, w2, b2, gate, picks, func, acc):
            top = len(picks)
            MT = -(-((top * N + NX * 128 - 1) // 128) // 2) * 2
            MTL = -(-MT // 4) * 4
            assert MTL <= SLOT_TILES
            F2 = FF // 128
            w1s = sb("w1s", [128, 2, K, FF], F32, c)
            w2s = sb("w2s", [128, 2, F2, D], F32, c)
            b1r = sb("b1r", [NX * F2, 128], F32, c)
            b1T = sb("b1T", [128, NX * F2], F32, c)
            b2s = sb("b2s", [NX, D], F32, c)
            gT = sb("gT", [NX, T, P], F32, c)
            picked = sb("picked", [P, T, NX], F32, c)
            f = sb("f", [P, 5, T, NX], F32, c)
            g8 = sb("g8", [P, 6, NX], F32, c)
            pairs = sb("pairs", [P, 2], F32, c)
            pos = sb("pos", [P, top, T], F32, c)
            pos_i = sb("pos_i", [P, top, T], I32, c)
            wgt = sb("wgt", [P, top, T], F32, c)
            tiles = sb("expert_tiles", [1, NX + 2], I32, c)
            xs = sb("xs", [128, 2, 2, D], F32, c)
            turned_ = sb("xs_turned", [128, K * MTL * 128], F32, c)
            xsT = turned_[:].rearrange("p (k n) -> p k n", k=K)
            got = turned_[0:P, 0:top * T * D].rearrange("p (s t d) -> p s t d", s=top, t=T)
            hid = sb("hid", [128, F2, 128], F32, c)
            ys = sb("ys", [128, 2, D], F32, c)
            ld0, w_used, picked_made, counted, step, ready = (sem(n) for n in ("bias_loaded", "w_used", "picked", "counted", "step", "positions_ready"))
            w_ld = [sem(f"w_loaded{b}") for b in range(2)]
            xs_ld = [sem(f"xs_loaded{b}") for b in range(2)]
            y_stored = [sem(f"y_stored{b}") for b in range(2)]
            g_turned, g_kept, bias_made, bias_added, b_turned, b_kept = (sem(n) for n in (
                "gate_turned", "gate_kept", "bias_made", "bias_added", "b1_turned", "b1_kept"))
            t_made, t_kept, h_made, h_kept, y_made, y_kept, all_stored, summed = (sem(n) for n in (
                "turned", "turned_kept", "hidden_made", "hidden_kept", "y_made", "y_kept", "all_stored", "summed"))
            rows_put = dma_sem("rows_put")
            fetched = [[dma_sem("fetched") for half in range(2)] for s in range(top)]
            halves = (range(0, T // 2), range(T // 2, T))

            def load_tiles(eng):
                return [eng.value_load(tiles[0:1, e:e + 1], min_val=e, max_val=MT - NX + e) for e in range(NX + 1)]

            def load_pairs(eng):
                return eng.value_load(tiles[0:1, NX + 1:NX + 2], min_val=NX // 2, max_val=MT // 2)

            def load_weights(eng, e):
                b = e % 2
                eng.dma_start(w1s[:, b], a[w1][e:e + 1].rearrange("e (k p) n -> p (e k) n", p=128)).then_inc(w_ld[b], 16)
                eng.dma_start(w2s[:, b], a[w2][e:e + 1].rearrange("e (k p) n -> p (e k) n", p=128)).then_inc(w_ld[b], 16)

            with nc.Block() as block:
                @block.sync
                def _(sp):
                    sp.dma_start(b1r[:], a[b1].rearrange("e (f p) -> (e f) p", p=128)).then_inc(ld0, 16)
                    sp.dma_start(b2s[:], a[b2]).then_inc(ld0, 16)
                    for e in range(2):
                        load_weights(sp, e)
                    sp.wait_ge(rows_put, 16 * top * T)
                    v = x_slots.rearrange("(n u p) d -> p n u d", u=2, p=128)
                    with sp.Fori(0, MTL // 4) as j:
                        for b in range(2):
                            sp.wait_ge(t_kept, j * 4 + (b * 2 + 2))
                            sp.dma_start(xs[:, b], v[:, bass.ds(j * 2 + b, 1)].rearrange("p n u d -> p (n u) d")).then_inc(xs_ld[b], 16)
                    v = y_slots.rearrange("(n p) d -> p n d", p=128)
                    used_pairs = load_pairs(sp)
                    with sp.Fori(0, used_pairs) as j:
                        for b in range(2):
                            sp.wait_ge(y_kept, j * 2 + (b + 2))
                            sp.dma_start(v[:, bass.ds(j * 2 + b, 1), :].rearrange("p n d -> p (n d)"), ys[:, b]).then_inc(y_stored[b], 16)
                    for b in range(2):
                        sp.wait_ge(y_stored[b], used_pairs * 16 + 16)
                        sp.sem_inc(all_stored, 1)

                @block.gpsimd
                def _(pool):
                    pool.wait_ge(ready, 1)
                    for s in range(top):
                        for t in range(T):
                            nc.gpsimd.indirect_dma_start(out=x_slots, out_offset=bass.IndirectOffsetOnAxis(ap=pos_i[:, s, t:t + 1], axis=0),
                                                         in_=xn[:, t, :], in_offset=None).then_inc(rows_put, 16)
                    pool.wait_ge(rows_put, 16 * top * T)
                    pool.wait_ge(all_stored, 2)
                    for s in range(top):
                        for half, ts in enumerate(halves):
                            for t in ts:
                                nc.gpsimd.indirect_dma_start(out=got[:, s, t, :], out_offset=None, in_=y_slots,
                                                             in_offset=bass.IndirectOffsetOnAxis(ap=pos_i[:, s, t:t + 1], axis=0)).then_inc(fetched[s][half], 16)

                @block.tensor
                def _(pe):
                    pe.wait_ge(picked_made, 1)
                    v = picked[:].rearrange("p t e -> p (t e)")
                    nc.tensor.matmul(bank[0:P, 0, 0:T * NX], above[0:P, 0:P], v, start=True, stop=True)
                    nc.tensor.matmul(bank[0:P, 1, 0:T * NX], ones[0:P, 0:P], v, start=True, stop=True).then_inc(counted, 1)
                    pe.wait_ge(ld0, 32)
                    nc.tensor.transpose(bank[:, 7, 0:NX * F2], b1r[:], ident[0:NX * F2, 0:NX * F2]).then_inc(b_turned, 1)
                    for t in range(T):
                        last = nc.tensor.transpose(bank[0:NX, 4 + t // 4, (t % 4) * P:(t % 4 + 1) * P], gate[:, t, :], ident[0:P, 0:P])
                    last.then_inc(g_turned, 1)
                    pe.wait_ge(g_kept, 1)
                    for t in range(T):
                        if t >= 2:
                            pe.wait_ge(bias_added, t - 1)
                        nc.tensor.matmul(bank[0:P, 2 + t % 2, :], gT[:, t, :], b2s[:], start=True, stop=True).then_inc(bias_made, 1)
                    with pe.Fori(0, MTL // 4) as j:
                        for b in range(2):
                            pe.wait_ge(xs_ld[b], j * 16 + 16)
                            for u in range(2):
                                pe.wait_ge(t_kept, j * 4 + (b * 2 + u + 3))
                                for k in range(K):
                                    last = nc.tensor.transpose(bank[:, 4 + u, k * 128:(k + 1) * 128], xs[:, b, u, k * 128:(k + 1) * 128], ident[:])
                                last.then_inc(t_made, 1)
                    expert_tiles = load_tiles(pe)
                    pe.wait_ge(t_kept, MTL + 4)
                    pe.wait_ge(bias_added, T)
                    for e in range(NX):
                        b = e % 2
                        pe.wait_ge(w_ld[b], 32 * (e // 2 + 1))
                        with pe.Fori(expert_tiles[e], expert_tiles[e + 1]) as n:
                            for g in range(F2):
                                for k in range(K):
                                    last = nc.tensor.matmul(bank[:, g, 0:128], w1s[:, b, k, g * 128:(g + 1) * 128], xsT[:, k, bass.ds(n * 128, 128)], start=(k == 0), stop=(k == K - 1))
                                last.then_inc(h_made, 1)
                            pe.wait_ge(y_kept, n + 1)
                            for g in range(F2):
                                pe.wait_ge(h_kept, n * F2 + (g + 1))
                                last = nc.tensor.matmul(bank[:, 2, :], hid[:, g, :], w2s[:, b, g, :], start=(g == 0), stop=(g == F2 - 1))
                            last.then_inc(y_made, 1)
                        nc.tensor.matmul(bank[0:1, 7, 511:512], ident[:, 0:1], ident[:, 0:1], start=True, stop=True).then_inc(w_used, 1)

                @block.scalar
                def _(act):
                    act.sem_inc(t_kept, 4)
                    act.wait_ge(b_turned, 1)
                    nc.scalar.copy(b1T[:], bank[:, 7, 0:NX * F2]).then_inc(b_kept, 1)
                    with act.Fori(0, MTL // 2) as j:
                        for u in range(2):
                            act.wait_ge(t_made, j * 2 + (u + 1))
                            nc.scalar.copy(xsT[:, :, bass.ds(j * 256 + u * 128, 128)], bank[:, 4 + u, :].rearrange("p (k n) -> p k n", k=K)).then_inc(t_kept, 1)
                    act.wait_ge(b_kept, 1)
                    act.wait_ge(ready, 1)
                    expert_tiles = load_tiles(act)
                    for e in range(NX):
                        if e >= 1 and e + 1 < NX:
                            act.wait_ge(w_used, e)
                            load_weights(act, e + 1)
                        with act.Fori(expert_tiles[e], expert_tiles[e + 1]) as n:
                            for g in range(F2):
                                act.wait_ge(h_made, n * F2 + (g + 1))
                                nc.scalar.activation(hid[:, g, :], bank[:, g, 0:128], func, bias=b1T[:, e * F2 + g:e * F2 + g + 1]).then_inc(h_kept, 1)

                @block.vector
                def _(dve):
                    v = [0]

                    def chain(ins):
                        v[0] += 1
                        ins.then_inc(step, 1)
                        dve.wait_ge(step, v[0])

                    dve.sem_inc(y_kept, 1)
                    for s in y_stored:
                        dve.sem_inc(s, 16)
                    if top == 2:
                        nc.vector.tensor_tensor(picked[:], picks[0], picks[1], ALU.add).then_inc(picked_made, 1)
                        for s in range(2):
                            chain(nc.vector.tensor_tensor(f[:, s], gate[:], picks[s], ALU.mult))
                            chain(nc.vector.tensor_reduce(wgt[:, s], f[:, s], X, ALU.add))
                    else:
                        nc.vector.tensor_copy(picked[:], picks[0]).then_inc(picked_made, 1)
                    dve.wait_ge(counted, 1)
                    nc.vector.tensor_copy(f[:, 0].rearrange("p t e -> p (t e)"), bank[0:P, 0, 0:T * NX])
                    chain(nc.vector.tensor_copy(f[:, 1].rearrange("p t e -> p (t e)"), bank[0:P, 1, 0:T * NX]))
                    for e in range(NX):
                        last = nc.vector.tensor_tensor_scan(f[:, 2, :, e], ones[0:P, 0:T], f[:, 1, :, e], 0.0, ALU.mult, ALU.add)
                    chain(last)
                    chain(nc.vector.tensor_scalar(g8[:, 0], f[:, 2, T - 1, :], 1.0, 127.0, ALU.max, ALU.add))
                    chain(nc.vector.tensor_scalar(g8[:, 1], g8[:, 0], -63.5, 1.0 / 128, ALU.add, ALU.mult))
                    chain(nc.vector.tensor_scalar(g8[:, 1], g8[:, 1], MAGIC, MAGIC, ALU.add, ALU.subtract))
                    chain(nc.vector.tensor_tensor_scan(g8[:, 2], ones[0:P, 0:NX], g8[:, 1], 0.0, ALU.mult, ALU.add))
                    chain(nc.vector.tensor_tensor(g8[:, 3], g8[:, 2], g8[:, 1], ALU.subtract))
                    chain(nc.vector.tensor_scalar(g8[:, 4], g8[:, 3], 128.0, None, ALU.mult))
                    chain(nc.vector.tensor_copy(tiles[0:1, 0:NX], g8[0:1, 3]))
                    chain(nc.vector.tensor_scalar(pairs[:, 0:1], g8[:, 2, NX - 1:NX], 0.5, 0.25, ALU.mult, ALU.add))
                    chain(nc.vector.tensor_scalar(pairs[:, 0:1], pairs[:, 0:1], MAGIC, MAGIC, ALU.add, ALU.subtract))
                    chain(nc.vector.tensor_copy(tiles[0:1, NX + 1:NX + 2], pairs[0:1, 0:1]))
                    chain(nc.vector.tensor_scalar(pairs[:, 1:2], pairs[:, 0:1], 2.0, None, ALU.mult))
                    chain(nc.vector.tensor_copy(tiles[0:1, NX:NX + 1], pairs[0:1, 1:2]))
                    chain(nc.vector.tensor_tensor(f[:, 3], f[:, 2], f[:, 1], ALU.subtract))
                    chain(nc.vector.tensor_tensor(f[:, 3], f[:, 3], f[:, 0], ALU.add))
                    chain(nc.vector.tensor_tensor(f[:, 3], f[:, 3], g8[:, 4].unsqueeze(1).to_broadcast([P, T, NX]), ALU.add))
                    for s in range(top):
                        chain(nc.vector.tensor_tensor(f[:, 4], f[:, 3], picks[s], ALU.mult))
                        chain(nc.vector.tensor_reduce(pos[:, s], f[:, 4], X, ALU.add))
                    nc.vector.tensor_copy(pos_i[:], pos[:]).then_inc(ready, 1)
                    dve.wait_ge(g_turned, 1)
                    for j, n in enumerate((4, 4, 2)):
                        last = nc.vector.tensor_copy(gT[:, 4 * j:4 * j + n, :].rearrange("p t n -> p (t n)"), bank[0:NX, 4 + j, 0:n * P])
                    last.then_inc(g_kept, 1)
                    dve.wait_ge(rows_put, 16 * top * T)
                    for t in range(T):
                        dve.wait_ge(bias_made, t + 1)
                        nc.vector.tensor_tensor(acc[:, t], bank[0:P, 2 + t % 2, :], acc[:, t], ALU.add).then_inc(bias_added, 1)
                    with dve.Fori(0, load_pairs(dve)) as j:
                        for b in range(2):
                            dve.wait_ge(y_made, j * 2 + (b + 1))
                            dve.wait_ge(y_stored[b], j * 16 + 16)
                            nc.vector.tensor_copy(ys[:, b], bank[:, 2, :]).then_inc(y_kept, 1)
                    for s in range(top):
                        for half, ts in enumerate(halves):
                            dve.wait_ge(fetched[s][half], 16 * len(ts))
                            for t in ts:
                                if s:
                                    dve.wait_ge(summed, t + 1)
                                w_ = wgt[:, s, t:t + 1] if top == 2 else 1.0
                                nc.vector.scalar_tensor_tensor(acc[:, t], got[:, s, t, :], w_, acc[:, t], ALU.mult, ALU.add).then_inc(summed, 1)

        def graph_and_convolutions():
            HID = 128
            w1s = sb("w1s", [128, K, HID], F32, c)
            w2s = sb("w2s", [128, D], F32, c)
            b1s = sb("b1s", [P, HID], F32, c)
            b2s = sb("b2s", [P, D], F32, c)
            ld = dma_sem("weights_loaded")

            def loads(sp):
                sp.dma_start(w1s[:], a["L0_gnn_W1"].rearrange("(k p) n -> p k n", p=128)).then_inc(ld, 16)
                sp.dma_start(w2s[:], a["L0_gnn_W2"]).then_inc(ld, 16)
                sp.dma_start(b1s[:], spread(a["L0_gnn_b1"])).then_inc(ld, 16)
                sp.dma_start(b2s[:], spread(a["L0_gnn_b2"])).then_inc(ld, 16)

            def edges_and_norm():
                rec = sb("rec", [P, EC, RW], F32, c)
                pos_i = sb("pos_i", [P, EC], I32, c)
                put = dma_sem("record_put")
                first = EC - 16

                def scatter(pool):
                    scatter_records(pool, rec, pos_i, range(first, EC), put)
                    pool.wait_ge(put, 16 * EC)

                run(sort_edges, rec, pos_i, put, range(first))
                run(norm, x, xn, also=loads, scatter=scatter)

            run(edges_and_norm)
            Asb = sb("A", [P, T, N], F32, c)
            run(count_matrix, Asb)
            run(convolutions, HID, Asb, w1s, w2s, b1s, b2s, ld)

        def convolutions(HID, Asb, w1s, w2s, b1s, b2s, ld):
            hs = sb("hs", [P, 2, T, HID], F32, c)
            u = sb("u", [P, 2, T, HID], F32, c)
            uT = sb("uT", [HID, T, P], F32, c)
            tmp = sb("tmp", [P, 2, D], F32, c)
            h_made, h_kept, agg, agg_kept, step = (sem(n) for n in ("h_made", "h_kept", "aggregated", "agg_kept", "step"))
            s2_made, uT_made, uT_kept, made, moved, u_made = (sem(n) for n in ("s2_made", "uT_made", "uT_kept", "made", "moved", "u_made"))
            with nc.Block() as block:
                @block.tensor
                def _(pe):
                    pe.wait_ge(ld, 64)
                    for t in range(T):
                        if t >= 2:
                            pe.wait_ge(h_kept, t - 1)
                        for k in range(K):
                            last = nc.tensor.matmul(bank[0:P, t % 2, 0:HID], xT[:, k, t * P:(t + 1) * P], w1s[:, k, :], start=(k == 0), stop=(k == K - 1))
                        last.then_inc(h_made, 1)
                    pe.wait_ge(h_kept, T)
                    for r in range(2):
                        if r == 1:
                            pe.wait_ge(s2_made, T)
                        for d in range(T):
                            if r * T + d >= 2:
                                pe.wait_ge(agg_kept, r * T + d - 1)
                            for s in range(T):
                                last = nc.tensor.matmul(bank[0:P, 2 + d % 2, 0:HID], Asb[:, s, d * P:(d + 1) * P], hs[:, r, s, :], start=(s == 0), stop=(s == T - 1))
                            last.then_inc(agg, 1)
                    pe.wait_ge(u_made, T)
                    for t in range(T):
                        if t >= 2:
                            pe.wait_ge(uT_kept, t - 1)
                        nc.tensor.transpose(bank[0:HID, 4 + t % 2, 0:P], u[:, 1, t, :], ident[0:P, 0:P]).then_inc(uT_made, 1)
                        pe.wait_ge(uT_kept, t + 1)
                        if t >= 2:
                            pe.wait_ge(moved, t - 1)
                        nc.tensor.matmul(bank[0:P, 6 + t % 2, :], uT[:, t, :], w2s[:], start=True, stop=True).then_inc(made, 1)

                @block.scalar
                def _(act):
                    for t in range(T):
                        act.wait_ge(h_made, t + 1)
                        nc.scalar.activation(hs[:, 0, t, :], bank[0:P, t % 2, 0:HID], ACT.Copy, scale=dinv[:, t:t + 1]).then_inc(h_kept, 1)
                    for t in range(T):
                        act.wait_ge(uT_made, t + 1)
                        nc.scalar.copy(uT[:, t, :], bank[0:HID, 4 + t % 2, 0:P]).then_inc(uT_kept, 1)

                @block.vector
                def _(dve):
                    v = [0]

                    def chain(ins):
                        v[0] += 1
                        ins.then_inc(step, 1)
                        dve.wait_ge(step, v[0])

                    dve.wait_ge(ld, 64)
                    dve.wait_ge(h_kept, T)
                    for r in range(2):
                        for d in range(T):
                            dve.wait_ge(agg, r * T + d + 1)
                            nc.vector.tensor_tensor(u[:, r, d, :], bank[0:P, 2 + d % 2, 0:HID], hs[:, r, d, :], ALU.add).then_inc(agg_kept, 1)
                            dve.wait_ge(agg_kept, r * T + d + 1)
                            if r == 1:
                                nc.vector.tensor_scalar(u[:, 1, d, :], u[:, 1, d, :], dinv[:, d:d + 1], None, ALU.mult).then_inc(u_made, 1)
                                continue
                            chain(nc.vector.scalar_tensor_tensor(u[:, 0, d, :], u[:, 0, d, :], dinv[:, d:d + 1], b1s[:], ALU.mult, ALU.add))
                            nc.vector.tensor_scalar(hs[:, 1, d, :], u[:, 0, d, :], 0.0, dinv[:, d:d + 1], ALU.max, ALU.mult).then_inc(s2_made, 1)
                        if r == 0:
                            dve.wait_ge(s2_made, T)
                    for t in range(T):
                        dve.wait_ge(made, t + 1)
                        nc.vector.tensor_tensor(tmp[:, t % 2], bank[0:P, 6 + t % 2, :], b2s[:], ALU.add).then_inc(moved, 1)
                        dve.wait_ge(moved, t + 1)
                        nc.vector.tensor_tensor(x[:, t], x[:, t], tmp[:, t % 2], ALU.add).then_inc(step, 1)

        def edge_qkv(q3, recs, wT, ws, bs, ld, recs_ld):
            kvs = sb("kvs", [P, 2, 2, D], F32, c)
            qf = sb("qf", [P, 2, D], F32, c)
            B = 8
            src16 = sb("src16", [S, SC], F16, c)
            iota16 = sb("iota16", [S, P], F16, c)
            w = sb("w", [S, 3, B, P], BF16, c)
            identb = sb("identb", [128, 128], BF16, c)
            batches = [range(t * (SC // B) // T, (t + 1) * (SC // B) // T) for t in range(T)]
            wTp = bank[:, 6:8, :].bitcast(BF16)
            copied, w_made, w_turned, wT_kept = (sem(n) for n in ("copied", "w_made", "w_turned", "wT_kept"))
            made, kept, split = (sem(n) for n in ("made", "kept", "split"))
            put = [sem(f"kv_put{b}") for b in range(2)]
            with nc.Block() as block:
                @block.sync
                def _(sp):
                    for t in range(T):
                        sp.wait_ge(kept, 3 * t + 3)
                        sp.dma_start(k_dram[t * P:(t + 1) * P, :], kvs[:, t % 2, 0]).then_inc(put[t % 2], 16)
                        sp.dma_start(v_dram[t * P:(t + 1) * P, :], kvs[:, t % 2, 1]).then_inc(put[t % 2], 16)
                    for b in range(2):
                        sp.wait_ge(put[b], 16 * T)

                @block.tensor
                def _(pe):
                    pe.wait_ge(ld, 96)
                    for t in range(T):
                        for i in range(3):
                            if t >= 2:
                                pe.wait_ge(kept, 3 * (t - 2) + i + 1)
                            for k in range(K):
                                last = nc.tensor.matmul(bank[0:P, 3 * (t % 2) + i, :], xT[:, k, t * P:(t + 1) * P], ws[:, i, k, :], start=(k == 0), stop=(k == K - 1))
                            last.then_inc(made, 1)
                        for j in batches[t]:
                            pe.wait_ge(w_made, j + 1)
                            if j >= 2:
                                pe.wait_ge(wT_kept, j - 1)
                            for g in range(B):
                                last = nc.tensor.transpose(wTp[0:P, j % 2, g * S:(g + 1) * S], w[:, j % 3, g, :], identb[:])
                            last.then_inc(w_turned, 1)

                @block.scalar
                def _(act):
                    for j in range(SC // B):
                        act.wait_ge(w_turned, j + 1)
                        nc.scalar.copy(wT[:, j * B * S:(j + 1) * B * S], wTp[0:P, j % 2, :]).then_inc(wT_kept, 1)

                @block.vector
                def _(dve):
                    v = [0]

                    def chain(ins):
                        v[0] += 1
                        ins.then_inc(split, 1)
                        dve.wait_ge(split, v[0])

                    nc.vector.tensor_copy(identb[:], ident[:])
                    nc.vector.tensor_copy(iota16[:], iota[:, 0:P])
                    dve.wait_ge(recs_ld, 16)
                    nc.vector.tensor_copy(src16[:], recs[:, :, 0:1].rearrange("p c a -> p (c a)")).then_inc(copied, 1)
                    dve.wait_ge(copied, 1)
                    for t in range(T):
                        for j in batches[t]:
                            if j >= 3:
                                dve.wait_ge(w_turned, j - 2)
                            nc.vector.tensor_tensor(w[:, j % 3], iota16[:].unsqueeze(1).to_broadcast([S, B, P]),
                                                    src16[:, j * B:(j + 1) * B].unsqueeze(2).to_broadcast([S, B, P]), ALU.is_equal).then_inc(w_made, 1)
                        if t == 0:
                            dve.wait_ge(ld, 96)
                        for i in range(3):
                            dve.wait_ge(made, 3 * t + i + 1)
                            if i == 1 and t >= 2:
                                dve.wait_ge(put[t % 2], 32 * (t // 2))
                            dst = qf[:, 0] if i == 0 else kvs[:, t % 2, i - 1]
                            nc.vector.tensor_tensor(dst, bank[0:P, 3 * (t % 2) + i, :], bs[:, i], ALU.add).then_inc(kept, 1)
                        dve.wait_ge(kept, 3 * t + 1)
                        chain(nc.vector.tensor_copy(q3[:, 0, t], qf[:, 0]))
                        chain(nc.vector.tensor_tensor(qf[:, 1], qf[:, 0], q3[:, 0, t], ALU.subtract))
                        chain(nc.vector.tensor_copy(q3[:, 1, t], qf[:, 1]))
                        chain(nc.vector.tensor_tensor(qf[:, 0], qf[:, 1], q3[:, 1, t], ALU.subtract))
                        chain(nc.vector.tensor_copy(q3[:, 2, t], qf[:, 0]))

        def gather_rows(pool, source, index, into, free, loaded, gone):
            with pool.Fori(0, SC // (R * G)) as i:
                for h in range(R):
                    pool.wait_ge(free[h], i + 1)
                    pool.sem_inc(gone, 1)
                    for g in range(G):
                        nc.gpsimd.indirect_dma_start(out=into[:, h * G + g, :], out_offset=None, in_=source,
                                                     in_offset=bass.IndirectOffsetOnAxis(ap=index[:, h * G + g:h * G + g + 1], axis=0)).then_inc(loaded[h], 16)

        def edge_logits(q3, recs, lg, wT):
            kg = sb("kg", [S, R * G, D], F32, c)
            idx = sb("idx", [S, R * G], I32, c)
            prod = sb("prod", [S, 2, D], F32, c)
            HV = 4
            q_made, multiplied, reduced, summed, dot = (sem(n) for n in ("q_spread", "multiplied", "reduced", "summed", "scaled"))
            idx_made = [sem(f"index_made{h}") for h in range(R)]
            k_ld = [dma_sem(f"k_gathered{h}") for h in range(R)]
            gone = sem("pool_passed")
            with nc.Block() as block:
                @block.gpsimd
                def _(pool):
                    gather_rows(pool, k_dram, idx, kg, idx_made, k_ld, gone)

                @block.scalar
                def _(act):
                    for n in range(SC):
                        act.wait_ge(multiplied, n + 3)
                        for h in range(HV, H):
                            v = prod[:, n % 2, h * DH:(h + 1) * DH]
                            last = nc.scalar.activation(v, v, ACT.Copy, accum_out=lg[:, n, h:h + 1])
                        last.then_inc(summed, 1)

                @block.tensor
                def _(pe):
                    edge_pairs = load_bounds(pe)
                    for t in range(T):
                        with pe.Fori(edge_pairs[t], edge_pairs[t + 1]) as n:
                            for h in range(2):
                                pe.wait_ge(multiplied, n * 2 + (h + 1))
                                for i in range(3):
                                    last = nc.tensor.matmul(bank[:, h, :], wT[:, bass.ds(n * (2 * S) + h * S, S)], q3[:, i, t, :], start=(i == 0), stop=(i == 2))
                                last.then_inc(q_made, 1)

                @block.vector
                def _(dve):
                    dve.sem_inc(multiplied, 2)
                    for h in range(R):
                        nc.vector.tensor_copy(idx[:, h * G:(h + 1) * G], recs[:, h * G:(h + 1) * G, 1]).then_inc(idx_made[h], 1)
                    def unit(i, tail):
                        for h in range(R):
                            dve.wait_ge(k_ld[h], i * (16 * G) + 16 * G)
                            for g in range(G):
                                n = i * (R * G) + (h * G + g)
                                dve.wait_ge(q_made, n + 1)
                                if n >= 2:
                                    dve.wait_ge(summed, n - 1)
                                nc.vector.tensor_tensor(prod[:, g % 2], kg[:, h * G + g, :], bank[:, g % 2, :], ALU.mult).then_inc(multiplied, 1)
                                dve.wait_ge(multiplied, n + 3)
                                nc.vector.tensor_reduce(lg[:, n, 0:HV], prod[:, g % 2, 0:HV * DH].rearrange("p (h d) -> p h d", h=HV), X, ALU.add).then_inc(reduced, 1)
                            if not tail:
                                nc.vector.tensor_copy(idx[:, h * G:(h + 1) * G], recs[:, bass.ds(i * (R * G) + (h * G + R * G), G), 1:2].rearrange("p a b -> p (a b)")).then_inc(idx_made[h], 1)

                    for i in range(SC // (R * G)):
                        unit(i, i == SC // (R * G) - 1)
                    dve.wait_ge(reduced, SC)
                    dve.wait_ge(summed, SC)
                    nc.vector.scalar_tensor_tensor(lg[:], lg[:], DH ** -0.5, recs[:, :, 2:2 + H], ALU.mult, ALU.add).then_inc(dot, 1)

        def edge_max(recs, lg, m3):
            PN = SC // 4
            key = sb("key", [S, SC + 1], F32, c)
            after = sb("after", [S, S], F32, c)
            wrap = sb("wrap", [S, S], F32, c)
            brk = sb("brk", [S, SC], F32, c)
            brks = sb("brks", [S, SC, H], F32, c)
            brow = sb("brow", [H, 2, 4 * S], F32, c)
            run_ = sb("run", [H, 2, 4 * S], F32, c)
            back = sb("back", [S, SC, H], F32, c)
            mm = sb("mm", [P, 3, T, H], F32, c)
            keys_made, before_made, brk_made, spread_, rows_made, brow_kept, step, scanned, turned, kept, put, cut = (sem(n) for n in (
                "keys_made", "before_made", "brk_made", "brk_spread", "rows_made", "brow_kept", "step", "scanned", "turned_back", "kept", "run_put", "first_key"))
            got = dma_sem("max_gathered")
            with nc.Block() as block:
                @block.gpsimd
                def _(pool):
                    nc.gpsimd.memset(key[:, 0:1], -2.0).then_inc(cut, 1)
                    pool.wait_ge(put, 16)
                    for t in range(T):
                        nc.gpsimd.indirect_dma_start(out=mm[:, 0, t, :], out_offset=None, in_=run_dram,
                                                     in_offset=bass.IndirectOffsetOnAxis(ap=last_row[:, t:t + 1], axis=0)).then_inc(got, 16)

                @block.sync
                def _(sp):
                    sp.wait_ge(kept, PN)
                    sp.dma_start(run_dram.rearrange("(p c) h -> p c h", p=S), back[:]).then_inc(put, 16)

                @block.tensor
                def _(pe):
                    pe.wait_ge(cut, 1)
                    pe.wait_ge(keys_made, 1)
                    nc.tensor.matmul(bank[:, 7, 0:SC], after[:], key[:, 1:], start=True, stop=False)
                    nc.tensor.matmul(bank[:, 7, 0:SC], wrap[:], key[:, 0:SC], start=False, stop=True).then_inc(before_made, 1)
                    pe.wait_ge(spread_, 1)
                    for j in range(PN + 1):
                        if j < PN:
                            if j >= 2:
                                pe.wait_ge(scanned, j - 1)
                                pe.wait_ge(brow_kept, j - 1)
                            for g in range(4):
                                nc.tensor.transpose(bank[0:H, j % 2, g * S:(g + 1) * S], lg[:, 4 * j + g, :], ident[:])
                            for g in range(4):
                                last = nc.tensor.transpose(bank[0:H, 2 + j % 2, g * S:(g + 1) * S], brks[:, 4 * j + g, :], ident[:])
                            last.then_inc(rows_made, 1)
                        if j >= 1:
                            i = j - 1
                            pe.wait_ge(scanned, i + 1)
                            if i >= 2:
                                pe.wait_ge(kept, i - 1)
                            for g in range(4):
                                last = nc.tensor.transpose(bank[:, 4 + i % 2, g * H:(g + 1) * H], run_[:, i % 2, g * S:(g + 1) * S], ident[0:H, 0:H])
                            last.then_inc(turned, 1)

                @block.scalar
                def _(act):
                    act.wait_ge(brk_made, 1)
                    nc.scalar.copy(brks[:], brk[:].unsqueeze(2).to_broadcast([S, SC, H])).then_inc(spread_, 1)
                    for j in range(PN + 1):
                        if j < PN:
                            act.wait_ge(rows_made, j + 1)
                            if j >= 2:
                                act.wait_ge(scanned, j - 1)
                            nc.scalar.copy(brow[:, j % 2], bank[0:H, 2 + j % 2, :]).then_inc(brow_kept, 1)
                        if j >= 1:
                            act.wait_ge(turned, j)
                            nc.scalar.copy(back[:, 4 * (j - 1):4 * j, :].rearrange("p c h -> p (c h)"), bank[:, 4 + (j - 1) % 2, 0:4 * H]).then_inc(kept, 1)

                @block.vector
                def _(dve):
                    nc.vector.memset(after[:, 0:1], 0.0)
                    nc.vector.tensor_copy(after[:, 1:S], ident[:, 0:S - 1])
                    nc.vector.memset(wrap[:, 1:S], 0.0)
                    nc.vector.tensor_copy(wrap[:, 0:1], ident[:, S - 1:S])
                    nc.vector.tensor_copy(key[:, 1:], recs[:, :, RW - 1:RW].rearrange("p c a -> p (c a)")).then_inc(keys_made, 1)
                    dve.wait_ge(before_made, 1)
                    nc.vector.tensor_tensor(brk[:], bank[:, 7, 0:SC], key[:, 1:], ALU.not_equal).then_inc(step, 1)
                    dve.wait_ge(step, 1)
                    nc.vector.tensor_scalar(brk[:], brk[:], NEG, None, ALU.mult).then_inc(brk_made, 1)
                    for j in range(PN):
                        dve.wait_ge(brow_kept, j + 1)
                        if j >= 2:
                            dve.wait_ge(turned, j - 1)
                        if j >= 1:
                            dve.wait_ge(scanned, j)
                        first = NEG if j == 0 else run_[:, (j - 1) % 2, 4 * S - 1:4 * S]
                        nc.vector.tensor_tensor_scan(run_[:, j % 2], brow[:, j % 2], bank[0:H, j % 2, :], first, ALU.add, ALU.max).then_inc(scanned, 1)
                    dve.wait_ge(got, 16 * T)

                    v = [1]

                    def chain(ins):
                        v[0] += 1
                        ins.then_inc(cut, 1)
                        dve.wait_ge(cut, v[0])

                    chain(nc.vector.tensor_copy(m3[:, :, 0, :], mm[:, 0]))
                    chain(nc.vector.tensor_tensor(mm[:, 1], mm[:, 0], m3[:, :, 0, :], ALU.subtract))
                    chain(nc.vector.tensor_copy(m3[:, :, 1, :], mm[:, 1]))
                    chain(nc.vector.tensor_tensor(mm[:, 2], mm[:, 1], m3[:, :, 1, :], ALU.subtract))
                    chain(nc.vector.tensor_copy(m3[:, :, 2, :], mm[:, 2]))

        def edge_exp(recs, lg, wT, m3, p3):
            r = sb("r", [S, 2, SC, H], F32, c)
            made, taken, exped, step = (sem(n) for n in ("max_spread", "max_taken", "exped", "step"))
            with nc.Block() as block:
                @block.tensor
                def _(pe):
                    edge_pairs = load_bounds(pe)
                    for t in range(T):
                        with pe.Fori(edge_pairs[t], edge_pairs[t + 1]) as n:
                            pe.wait_ge(taken, n + 1)
                            for h in range(2):
                                for i in range(3):
                                    last = nc.tensor.matmul(bank[:, h, 0:H], wT[:, bass.ds(n * (2 * S) + h * S, S)], m3[:, t, i, :], start=(i == 0), stop=(i == 2))
                            last.then_inc(made, 1)

                @block.vector
                def _(dve):
                    v = [0]

                    def chain(ins):
                        v[0] += 1
                        ins.then_inc(step, 1)
                        dve.wait_ge(step, v[0])

                    dve.sem_inc(taken, 1)
                    for n in range(PAIRS):
                        dve.wait_ge(made, n + 1)
                        nc.vector.tensor_tensor(lg[:, 2 * n:2 * n + 2, :], lg[:, 2 * n:2 * n + 2, :], bank[:, 0:2, 0:H], ALU.subtract).then_inc(taken, 1)
                    dve.wait_ge(taken, PAIRS + 1)
                    dve.sem_inc(exped, 1)
                    dve.wait_ge(exped, 2)
                    chain(nc.vector.tensor_copy(p3[:, :, 0, :], lg[:]))
                    chain(nc.vector.tensor_tensor(r[:, 0], lg[:], p3[:, :, 0, :], ALU.subtract))
                    chain(nc.vector.tensor_copy(p3[:, :, 1, :], r[:, 0]))
                    chain(nc.vector.tensor_tensor(r[:, 1], r[:, 0], p3[:, :, 1, :], ALU.subtract))
                    chain(nc.vector.tensor_copy(p3[:, :, 2, :], r[:, 1]))

                @block.scalar
                def _(act):
                    act.wait_ge(exped, 1)
                    nc.scalar.activation(lg[:], lg[:], ACT.Exp).then_inc(exped, 1)

        def edge_sum(recs, lg, p3):
            vg = sb("vg", [S, R * G, D], F32, c)
            idx = sb("idx", [S, R * G], I32, c)
            w = sb("w", [S, 2, P], F32, c)
            wb = sb("wb", [S, 2, P], BF16, c)
            pv = sb("pv", [S, 2, D], F32, c)
            zero = sb("zero", [S, 512], BF16, c)
            den = sb("den", [P, 2, T, H], F32, c)
            dparts = sb("dparts", [P, T, 3 * H], F32, c)
            zeroed, w_made, wb_made, pv_made, tile_done, tile_kept, step = (sem(n) for n in ("zeroed", "w_made", "wb_made", "pv_made", "tile_done", "tile_kept", "step"))
            idx_made = [sem(f"index_made{h}") for h in range(R)]
            used = [sem(f"pv_used{h}") for h in range(2)]
            v_ld = [dma_sem(f"v_gathered{h}") for h in range(R)]
            gone = sem("pool_passed")
            with nc.Block() as block:
                @block.gpsimd
                def _(pool):
                    gather_rows(pool, v_dram, idx, vg, idx_made, v_ld, gone)

                @block.tensor
                def _(pe):
                    edge_pairs = load_bounds(pe)
                    for s in used:
                        pe.sem_inc(s, 1)
                    pe.wait_ge(zeroed, 1)
                    for t in range(T):
                        if t >= 2:
                            pe.wait_ge(tile_kept, t - 1)
                        y, d = bank[0:P, 2 * (t % 2), :], bank[0:P, 2 * (t % 2) + 1, 0:3 * H]
                        for o, cn in ((y, D), (d, 3 * H)):
                            nc.tensor.matmul(o, zero[:, 0:P], zero[:, 0:cn], start=True, stop=False, skip_group_check=True)
                        with pe.Fori(edge_pairs[t], edge_pairs[t + 1]) as n:
                            for h in range(2):
                                pe.wait_ge(wb_made, n * 2 + (h + 1))
                                nc.tensor.matmul(d, wb[:, h], p3[:, bass.ds(n * 2 + h, 1), :, :].rearrange("p a i h -> p (a i h)"), start=False, stop=False, skip_group_check=True)
                                pe.wait_ge(pv_made, n * 2 + (h + 1))
                                nc.tensor.matmul(y, w[:, h], pv[:, h], start=False, stop=False, skip_group_check=True).then_inc(used[h], 1)
                        nc.tensor.matmul(bank[0:P, 7, 0:2], zero[:, 0:P], zero[:, 0:2], start=True, stop=True).then_inc(tile_done, 1)

                @block.scalar
                def _(act):
                    edge_pairs = load_bounds(act)
                    for t in range(T):
                        with act.Fori(edge_pairs[t], edge_pairs[t + 1]) as n:
                            for h in range(2):
                                act.wait_ge(w_made, n * 2 + (h + 1))
                                nc.scalar.copy(wb[:, h], w[:, h]).then_inc(wb_made, 1)
                        act.wait_ge(tile_done, t + 1)
                        nc.scalar.copy(xn[:, t], bank[0:P, 2 * (t % 2), :])
                        nc.scalar.copy(dparts[:, t], bank[0:P, 2 * (t % 2) + 1, 0:3 * H]).then_inc(tile_kept, 1)

                @block.vector
                def _(dve):
                    nc.vector.memset(zero[:], 0.0).then_inc(zeroed, 1)
                    for h in range(R):
                        nc.vector.tensor_copy(idx[:, h * G:(h + 1) * G], recs[:, h * G:(h + 1) * G, 1]).then_inc(idx_made[h], 1)

                    def unit(i, tail):
                        for h in range(R):
                            for g in range(G):
                                n = i * (R * G) + (h * G + g)
                                b = g % 2
                                dve.wait_ge(used[b], n // 2 + 1)
                                nc.vector.tensor_scalar(w[:, b], iota[:, 0:P], recs[:, bass.ds(n, 1), 0:1].rearrange("p a b -> p (a b)"), None, ALU.is_equal).then_inc(w_made, 1)
                                if g == 0:
                                    dve.wait_ge(v_ld[h], i * (16 * G) + 16 * G)
                                nc.vector.tensor_tensor(pv[:, b].rearrange("p (h d) -> p h d", h=H), vg[:, h * G + g, :].rearrange("p (h d) -> p h d", h=H),
                                                        lg[:, bass.ds(n, 1), :].rearrange("p a h -> p (a h)").unsqueeze(2).to_broadcast([S, H, DH]), ALU.mult).then_inc(pv_made, 1)
                                if g == G - 1:
                                    dve.wait_ge(pv_made, n + 1)
                            if not tail:
                                nc.vector.tensor_copy(idx[:, h * G:(h + 1) * G], recs[:, bass.ds(i * (R * G) + (h * G + R * G), G), 1:2].rearrange("p a b -> p (a b)")).then_inc(idx_made[h], 1)

                    for i in range(SC // (R * G)):
                        unit(i, i == SC // (R * G) - 1)

                    v = [0]

                    def chain(ins):
                        v[0] += 1
                        ins.then_inc(step, 1)
                        dve.wait_ge(step, v[0])

                    dve.wait_ge(tile_kept, T)
                    chain(nc.vector.tensor_reduce(den[:, 0], dparts[:].rearrange("p t (i h) -> p t h i", i=3), X, ALU.add))
                    chain(nc.vector.tensor_scalar(den[:, 0], den[:, 0], 1e-30, None, ALU.max))
                    chain(nc.vector.reciprocal(den[:, 1], den[:, 0]))
                    for t in range(T):
                        y3 = xn[:, t].rearrange("p (h d) -> p h d", h=H)
                        chain(nc.vector.tensor_tensor(y3, y3, den[:, 1, t].unsqueeze(2).to_broadcast([P, H, DH]), ALU.mult))

        def edge_inputs(q3, recs, wT):
            ws = sb("ws", [128, 3, K, D], F32, c)
            bs = sb("bs", [P, 3, D], F32, c)
            ld, recs_ld = dma_sem("weights_loaded"), dma_sem("recs_loaded")

            def loads(sp):
                sp.dma_start(recs[:], table.rearrange("(p c) w -> p c w", p=S)).then_inc(recs_ld, 16)
                for i, n in enumerate("qkv"):
                    sp.dma_start(ws[:, i], a[f"L1_gnn_W{n}"].rearrange("(k p) n -> p k n", p=128)).then_inc(ld, 16)
                    sp.dma_start(bs[:, i], spread(a[f"L1_gnn_b{n}"])).then_inc(ld, 16)

            run(norm, x, xn, also=loads)
            run(edge_qkv, q3, recs, wT, ws, bs, ld, recs_ld)

        def edge_attention():
            q3 = sb("q3", [P, 3, T, D], BF16, c)
            recs = sb("recs", [S, SC, RW], F32, c)
            wT = sb("wT", [P, SC * S], BF16, c)
            run(edge_inputs, q3, recs, wT)
            lg = sb("lg", [S, SC, H], F32, c)
            m3 = sb("m3", [P, T, 3, H], BF16, c)
            p3 = sb("p3", [S, SC, 3, H], BF16, c)
            run(edge_logits, q3, recs, lg, wT)
            run(edge_max, recs, lg, m3)
            run(edge_exp, recs, lg, wT, m3, p3)
            run(edge_sum, recs, lg, p3)

        def full_attention(oT, also):
            wq = sb("wq", [128, 3, K, 128], F32, c)
            bqk = sb("bqk", [128, 2], F32, c)
            bv = sb("bv", [P, D], F32, c)
            qz = sb("qz", [128, 2, N], F32, c)
            kz = sb("kz", [128, 2, N], F32, c)
            EXTRA = (DH, 0)
            vs = sb("vs", [P, T, 128], F32, c)
            mxp = sb("mxp", [P, 2, T, 3], F32, c)
            nm = sb("nm", [P, 2, 2, T], F32, c)
            pT = sb("pT", [P, T, N], F32, c)
            psum_k = sb("psum_k", [P, N], F32, c)
            rden = sb("rden", [128, N], F32, c)
            bias_ld, w_ld, w_used = sem("bias_loaded"), sem("w_loaded"), sem("w_used")
            zeroed, ones_set, row_zeroed, turns = (sem(n) for n in ("zeroed", "ones_set", "row_zeroed", "turns"))
            made, folded, negated, added, o_made, o_free, divided = (sem(n) for n in (
                "group_made", "max_folded", "max_negated", "p_added", "outputs_made", "outputs_moved", "outputs_divided"))
            RING = 6
            free = [sem(f"bank_free{i}") for i in range(RING)]
            V_T = [(0, 2), (2, 2), (4, 2), (6, 2), (8, 1), (9, 1)]
            R_T = [(0, 4), (4, 4), (8, 2)]
            groups = [("q", j) for j in range(3)] + [("k", j) for j in range(3)] + [("v", j) for j in range(6)]
            for h in range(2):
                groups += [("s", h, t, j) for t in range(T) for j in range(3)]
            for h in range(2):
                groups += [("row", h, j) for j in range(3)]
                for t in range(T):
                    groups += [("p", h, t, j) for j in range(3)]
                    if h == 1 and t == 1:
                        groups += [("den", 0, j) for j in range(3)]
            groups += [("den", 1, j) for j in range(3)]
            NG = len(groups)
            assert NG % RING == 0
            at = {g: i for i, g in enumerate(groups)}
            O_COLS = [(0, 313, 0, 6), (313, 312, 64, 6), (625, 313, 0, 7), (938, 312, 64, 7)]
            NO = len(O_COLS)
            SCALE = DH ** -0.5

            def bank_of(*g):
                return at[g] % RING

            def wait_made(eng, m, *g):
                eng.wait_ge(made, m * NG + (at[g] + 1))

            def wait_copied(eng, m, *g):
                eng.wait_ge(free[at[g] % RING], m * (NG // RING) + (at[g] // RING + 2))

            with nc.Block() as block:
                @block.sync
                def _(sp):
                    sp.dma_start(bv[:], spread(a["L1_ffn_bv"])).then_inc(bias_ld, 16)
                    also(sp)
                    with sp.Fori(0, K) as m:
                        sp.wait_ge(w_used, m + 1)
                        for i, n in enumerate("qk"):
                            sp.dma_start(bqk[:, i:i + 1], a[f"L1_ffn_b{n}"].rearrange("(m p a) -> m p a", p=128, a=1)[bass.ds(m, 1)].rearrange("m p a -> (m p) a"), allow_slow_non_contiguous=True).then_inc(w_ld, 16)
                        for i, n in enumerate("qkv"):
                            sp.dma_start(wq[:, i], a[f"L1_ffn_W{n}"].rearrange("(k p) (m n) -> p k m n", p=128, n=128)[:, :, bass.ds(m, 1), :].rearrange("p k m n -> p k (m n)")).then_inc(w_ld, 16)

                @block.gpsimd
                def _(pool):
                    for b in (qz, kz):
                        nc.gpsimd.memset(b[DH:128, 0, :], 0.0).then_inc(zeroed, 1)
                        nc.gpsimd.memset(b[0:DH, 1, :], 0.0).then_inc(zeroed, 1)
                    pool.wait_ge(zeroed, 4)
                    for h in range(2):
                        nc.gpsimd.memset(kz[EXTRA[h]:EXTRA[h] + 1, h, :], 1.0).then_inc(ones_set, 1)
                    with pool.Fori(0, K) as m:
                        wait_made(pool, m, "q", 0)
                        pool.sem_inc(turns, 1)
                        for h in range(2):
                            nc.gpsimd.memset(qz[EXTRA[h]:EXTRA[h] + 1, h, :], 0.0).then_inc(row_zeroed, 1)

                @block.tensor
                def _(pe):
                    def wait_free(m, g):
                        pe.wait_ge(free[at[g] % RING], m * (NG // RING) + (at[g] // RING + 1))

                    def den(m, h):
                        pe.wait_ge(added, m * (2 * (T - 1)) + (h + 2) * (T - 1))
                        for j, (c0, cn) in enumerate(COLS):
                            wait_free(m, ("den", h, j))
                            nc.tensor.matmul(bank[:, bank_of("den", h, j), 0:cn], ones[0:P, :], psum_k[:, c0:c0 + cn], start=True, stop=True).then_inc(made, 1)

                    def outputs(m, h, t):
                        if t == 0:
                            pe.wait_ge(o_free, m * (2 * NO) + (h + 1) * NO)
                        for j in range(3):
                            wait_copied(pe, m, "p", h, t, j)
                        for c0, cn, p0, b in O_COLS:
                            last = nc.tensor.matmul(bank[p0:p0 + DH, b, 0:cn], vs[:, t, h * DH:(h + 1) * DH], pT[:, t, c0:c0 + cn], start=(t == 0), stop=(t == T - 1))
                        if t == T - 1:
                            last.then_inc(o_made, 1)

                    pe.sem_inc(w_used, 1)
                    pe.wait_ge(zeroed, 4)
                    pe.wait_ge(ones_set, 2)
                    with pe.Fori(0, K) as m:
                        pe.wait_ge(w_ld, m * 80 + 80)
                        for i, n in enumerate("qk"):
                            for j, (c0, cn) in enumerate(COLS):
                                wait_free(m, (n, j))
                                for k in range(K):
                                    last = nc.tensor.matmul(bank[:, bank_of(n, j), 0:cn], wq[:, i, k, :], xT[:, k, c0:c0 + cn], start=(k == 0), stop=(k == K - 1))
                                last.then_inc(made, 1)
                        for j, (t0, tn) in enumerate(V_T):
                            wait_free(m, ("v", j))
                            for t in range(t0, t0 + tn):
                                for k in range(K):
                                    last = nc.tensor.matmul(bank[0:P, bank_of("v", j), (t - t0) * 128:(t - t0 + 1) * 128], xT[:, k, t * P:(t + 1) * P], wq[:, 2, k, :], start=(k == 0), stop=(k == K - 1))
                            last.then_inc(made, 1)
                        pe.wait_ge(row_zeroed, m * 2 + 2)
                        for j in range(3):
                            wait_copied(pe, m, "q", j)
                            wait_copied(pe, m, "k", j)
                        for h in range(2):
                            for t in range(T):
                                for j, (c0, cn) in enumerate(COLS):
                                    wait_free(m, ("s", h, t, j))
                                    ins = nc.tensor.matmul(bank[0:P, bank_of("s", h, t, j), 0:cn], qz[:, h, t * P:(t + 1) * P], kz[:, h, c0:c0 + cn], start=True, stop=True)
                                    ins.then_inc(made, 1)
                                    if (h, t, j) == (0, 0, 0):
                                        pe.wait_ge(made, m * NG + (at[("v", 5)] + 1))
                                        pe.sem_inc(w_used, 1)
                        for h in range(2):
                            pe.wait_ge(negated, m * 2 + (h + 1))
                            for j, (t0, tn) in enumerate(R_T):
                                wait_free(m, ("row", h, j))
                                for t in range(t0, t0 + tn):
                                    last = nc.tensor.matmul(bank[EXTRA[h]:EXTRA[h] + 1, bank_of("row", h, j), (t - t0) * P:(t - t0 + 1) * P], nm[:, h, 1, t:t + 1], ident[0:P, 0:P], start=True, stop=True)
                                last.then_inc(made, 1)
                            for j in range(3):
                                wait_copied(pe, m, "row", h, j)
                            if h == 0:
                                for j in range(6):
                                    wait_copied(pe, m, "v", j)
                            for t in range(T):
                                for j, (c0, cn) in enumerate(COLS):
                                    wait_free(m, ("p", h, t, j))
                                    nc.tensor.matmul(bank[0:P, bank_of("p", h, t, j), 0:cn], kz[:, h, t * P:(t + 1) * P], qz[:, h, c0:c0 + cn], start=True, stop=True).then_inc(made, 1)
                                if h == 1 and t == 1:
                                    den(m, 0)
                                if t >= 1:
                                    outputs(m, h, t - 1)
                            outputs(m, h, T - 1)
                        den(m, 1)

                @block.scalar
                def _(act):
                    act.wait_ge(zeroed, 4)
                    with act.Fori(0, K) as m:
                        for i, (n, z) in enumerate((("q", qz), ("k", kz))):
                            for j, (c0, cn) in enumerate(COLS):
                                wait_made(act, m, n, j)
                                for h in range(2):
                                    r = slice(h * DH, (h + 1) * DH)
                                    last = nc.scalar.activation(z[r, h, c0:c0 + cn], bank[r, bank_of(n, j), 0:cn], ACT.Identity, bias=bqk[r, i:i + 1])
                                last.then_inc(free[bank_of(n, j)], 1)
                        for h in range(2):
                            e = slice(EXTRA[h], EXTRA[h] + 1)
                            for j, (t0, tn) in enumerate(R_T):
                                wait_made(act, m, "row", h, j)
                                nc.scalar.copy(qz[e, h, t0 * P:(t0 + tn) * P], bank[e, bank_of("row", h, j), 0:tn * P]).then_inc(free[bank_of("row", h, j)], 1)
                            act.wait_ge(added, m * (2 * (T - 1)) + (h + 1) * (T - 1))
                            for t in range(T):
                                for j, (c0, cn) in enumerate(COLS):
                                    wait_made(act, m, "p", h, t, j)
                                    nc.scalar.activation(pT[:, t, c0:c0 + cn], bank[0:P, bank_of("p", h, t, j), 0:cn], ACT.Exp, scale=SCALE).then_inc(free[bank_of("p", h, t, j)], 1)

                @block.vector
                def _(dve):
                    for s in free:
                        dve.sem_inc(s, 1)
                    dve.sem_inc(o_free, NO)
                    dve.sem_inc(added, T - 1)
                    dve.wait_ge(bias_ld, 16)
                    with dve.Fori(0, K) as m:
                        def head_rows(h, c0, cn):
                            return oT[h * DH:(h + 1) * DH, bass.ds(m, 1), c0:c0 + cn].rearrange("p a n -> p (a n)")

                        def move(h):
                            dve.wait_ge(o_made, m * 2 + (h + 1))
                            for c0, cn, p0, b in O_COLS:
                                nc.vector.tensor_copy(head_rows(h, c0, cn), bank[p0:p0 + DH, b, 0:cn]).then_inc(o_free, 1)

                        def finish(h):
                            for j, (c0, cn) in enumerate(COLS):
                                wait_made(dve, m, "den", h, j)
                                b = bank_of("den", h, j)
                                nc.vector.reciprocal(rden[:, c0:c0 + cn], bank[:, b, 0:cn]).then_inc(free[b], 1)
                            for j in range(3):
                                wait_copied(dve, m, "den", h, j)
                            dve.wait_ge(o_free, m * (2 * NO) + (h + 2) * NO)
                            nc.vector.tensor_tensor(head_rows(h, 0, N), head_rows(h, 0, N), rden[h * DH:(h + 1) * DH, :], ALU.mult).then_inc(divided, 1)

                        for j, (t0, tn) in enumerate(V_T):
                            wait_made(dve, m, "v", j)
                            b = bank_of("v", j)
                            nc.vector.tensor_tensor(vs[:, t0:t0 + tn, :], bank[0:P, b, 0:tn * 128].rearrange("p (t n) -> p t n", t=tn),
                                                    bv[:, bass.ds(m * 128, 128)].unsqueeze(1).to_broadcast([P, tn, 128]), ALU.add).then_inc(free[b], 1)
                        for h in range(2):
                            for t in range(T):
                                for j, (c0, cn) in enumerate(COLS):
                                    wait_made(dve, m, "s", h, t, j)
                                    b = bank_of("s", h, t, j)
                                    nc.vector.tensor_reduce(mxp[:, h, t, j:j + 1], bank[0:P, b, 0:cn], X, ALU.max).then_inc(free[b], 1)
                            for t in (T - 2, T - 1):
                                for j in range(3):
                                    wait_copied(dve, m, "s", h, t, j)
                            nc.vector.tensor_reduce(nm[:, h, 0, :], mxp[:, h], X, ALU.max).then_inc(folded, 1)
                            dve.wait_ge(folded, m * 2 + (h + 1))
                            nc.vector.tensor_scalar(nm[:, h, 1, :], nm[:, h, 0, :], -1.0, None, ALU.mult).then_inc(negated, 1)
                        for h in range(2):
                            if h == 1:
                                move(0)
                                finish(0)
                            for t in range(1, T):
                                if t == 1:
                                    for j in range(3):
                                        wait_copied(dve, m, "p", h, 0, j)
                                else:
                                    dve.wait_ge(added, m * (2 * (T - 1)) + ((h + 1) * (T - 1) + t - 1))
                                for j in range(3):
                                    wait_copied(dve, m, "p", h, t, j)
                                nc.vector.tensor_tensor(psum_k[:], pT[:, 0, :] if t == 1 else psum_k[:], pT[:, t, :], ALU.add).then_inc(added, 1)
                        move(1)
                        finish(1)

        def turn_and_project():
            weights, loads = project_weights(a["L1_gnn_Wo"], a["L1_gnn_bo"])
            run(turn_rows, xn, loads)
            run(project, xT, weights, x)

        def attention_and_project():
            oT = sb("oT", [128, K, N], F32, c)
            weights, loads = project_weights(a["L1_ffn_Wo"], a["L1_ffn_bo"])
            run(full_attention, oT, loads)
            run(project, oT, weights, xn)

        def mean_layer(w_self, w_neigh, bias, relu, to, to_dram=None):
            Asb = sb("A", [P, T, N], F32, c)
            ws = sb("ws", [128, 2, K, D], F32, c)
            bs = sb("bs", [P, D], F32, c)
            A_ld, ld = dma_sem("A_loaded"), dma_sem("weights_loaded")

            def loads(sp):
                for t in range(T):
                    sp.dma_start(Asb[:, t], A_dram[:, t]).then_inc(A_ld, 16)
                for i, w in enumerate((w_self, w_neigh)):
                    sp.dma_start(ws[:, i], w.rearrange("(k p) n -> p k n", p=128)).then_inc(ld, 16)
                sp.dma_start(bs[:], spread(bias)).then_inc(ld, 16)

            run(norm, x, xn, also=loads)
            run(mean, Asb, ws, bs, A_ld, ld, relu, to, to_dram)

        def mean(Asb, ws, bs, A_ld, ld, relu, to, to_dram):
            aT = sb("aT", [128, K, N], F32, c)
            tmp = sb("tmp", [P, 2, D], F32, c)
            agg, agg_kept, made, moved, step, put = (sem(n) for n in ("aggregated", "agg_kept", "made", "moved", "step", "put"))
            with nc.Block() as block:
                if to_dram is not None:
                    @block.sync
                    def _(sp):
                        for t in range(T):
                            sp.wait_ge(step, 2 * (t + 1))
                            sp.dma_start(to_dram[t * P:(t + 1) * P, :], to[:, t]).then_inc(put, 16)
                        sp.wait_ge(put, 16 * T)

                @block.tensor
                def _(pe):
                    pe.wait_ge(A_ld, 16 * T)
                    g = 0
                    for c0, cn in COLS:
                        for k in range(K):
                            if g >= 4:
                                pe.wait_ge(agg_kept, g - 3)
                            for s in range(T):
                                last = nc.tensor.matmul(bank[:, g % 4, 0:cn], xn[:, s, k * 128:(k + 1) * 128], Asb[:, s, c0:c0 + cn], start=(s == 0), stop=(s == T - 1))
                            last.then_inc(agg, 1)
                            g += 1
                    pe.wait_ge(agg_kept, g)
                    pe.wait_ge(ld, 48)
                    for t in range(T):
                        if t >= 2:
                            pe.wait_ge(moved, t - 1)
                        for i, lhs in enumerate((xT, aT)):
                            for k in range(K):
                                last = nc.tensor.matmul(bank[0:P, 4 + 2 * (t % 2) + i, :], lhs[:, k, t * P:(t + 1) * P], ws[:, i, k, :], start=(k == 0), stop=(k == K - 1))
                        last.then_inc(made, 1)

                @block.scalar
                def _(act):
                    g = 0
                    for c0, cn in COLS:
                        for k in range(K):
                            act.wait_ge(agg, g + 1)
                            nc.scalar.copy(aT[:, k, c0:c0 + cn], bank[:, g % 4, 0:cn]).then_inc(agg_kept, 1)
                            g += 1

                @block.vector
                def _(dve):
                    v = [0]

                    def chain(ins):
                        v[0] += 1
                        ins.then_inc(step, 1)
                        dve.wait_ge(step, v[0])

                    dve.wait_ge(ld, 48)
                    for t in range(T):
                        dve.wait_ge(made, t + 1)
                        o = tmp[:, t % 2]
                        chain(nc.vector.tensor_tensor(o, bank[0:P, 4 + 2 * (t % 2), :], bs[:], ALU.add))
                        nc.vector.scalar_tensor_tensor(o, bank[0:P, 5 + 2 * (t % 2), :], rdeg[:, t:t + 1], o, ALU.mult, ALU.add).then_inc(moved, 1)
                        dve.wait_ge(moved, t + 1)
                        if relu:
                            chain(nc.vector.scalar_tensor_tensor(to[:, t], o, 0.0, to[:, t], ALU.max, ALU.add))
                        else:
                            chain(nc.vector.tensor_copy(to[:, t], o))

        U = N // 2 // P
        PC = N // 2
        W2 = D // 2

        def to_pairs():
            got = sem("x_got")
            with nc.Block() as block:
                @block.sync
                def _(sp):
                    sp.dma_start(x[:].rearrange("p (u r) d -> p u (r d)", r=2), x_dram.rearrange("(u p r) d -> p u (r d)", p=P, r=2)).then_inc(got, 16)
                    sp.wait_ge(got, 16)

        def from_pairs():
            got = sem("x_got")
            with nc.Block() as block:
                @block.sync
                def _(sp):
                    sp.dma_start(x[:], x_dram.rearrange("(t p) d -> p t d", p=P)).then_inc(got, 16)
                    sp.wait_ge(got, 16)

        def wavelet():
            F = FF // 128
            C2 = [(0, 375), (375, 250)]
            wi = sb("wi", [128, 2, D], F32, c)
            w1s = sb("w1s", [128, K, FF], F32, c)
            w2s = sb("w2s", [128, F, W2], F32, c)
            b1s = sb("b1s", [128, F], F32, c)
            b2s = sb("b2s", [P, W2], F32, c)
            sums = sb("sums", [P, U, D], F32, c)
            difs = sb("difs", [P, U, D], F32, c)
            low = sb("low", [P, U, 4, W2], F32, c)
            llT = sb("llT", [128, 2, PC], F32, c)
            upT = sb("upT", [128, K, PC], F32, c)
            hT = sb("hT", [128, F, PC], F32, c)
            nl = sb("nl", [P, 2, W2], F32, c)
            o = sb("o", [P, 6, W2], F32, c)
            ld, made, step, turned, kept, mm, mm_kept, last_made, moved = (sem(n) for n in (
                "loaded", "parts_made", "step", "ll_turned", "ll_kept", "product_made", "product_kept", "new_made", "new_moved"))
            x_made, put = sem("x_made"), sem("x_put")
            pairs = xn[:].rearrange("p (u r) d -> p u r d", r=2)
            xp = x[:].rearrange("p (u r) d -> p u r d", r=2)
            with nc.Block() as block:
                @block.sync
                def _(sp):
                    sp.dma_start(wi[:], a["stretch"].rearrange("(k p) n -> p k n", p=128)).then_inc(ld, 16)
                    sp.dma_start(w1s[:], a["L2_ffn_fc1_w"].rearrange("(k p) n -> p k n", p=128)).then_inc(ld, 16)
                    sp.dma_start(w2s[:], a["L2_ffn_fc2_w"].rearrange("(k p) n -> p k n", p=128)).then_inc(ld, 16)
                    sp.dma_start(b1s[:], a["L2_ffn_fc1_b"].rearrange("(f p) -> p f", p=128), allow_slow_non_contiguous=True).then_inc(ld, 16)
                    sp.dma_start(b2s[:], spread(a["L2_ffn_fc2_b"])).then_inc(ld, 16)
                    for u in range(U):
                        sp.wait_ge(x_made, u + 1)
                        sp.dma_start(x_dram[2 * u * P:2 * (u + 1) * P, :].rearrange("(p r) d -> p r d", r=2), xp[:, u]).then_inc(put, 16)
                    sp.wait_ge(put, 16 * U)

                @block.tensor
                def _(pe):
                    for u in range(U):
                        pe.wait_ge(made, u + 1)
                        if u >= 2:
                            pe.wait_ge(kept, u - 1)
                        for k in range(2):
                            last = nc.tensor.transpose(bank[:, u % 2, k * P:(k + 1) * P], low[:, u, 0, k * 128:(k + 1) * 128], ident[0:P, 0:P])
                        last.then_inc(turned, 1)
                    pe.wait_ge(kept, U)
                    pe.wait_ge(ld, 80)
                    g = 0
                    for lhs, rhs, k_n, m_n in ((wi, llT, 2, K), (w1s, upT, K, F)):
                        if m_n == F:
                            pe.wait_ge(mm_kept, g)
                        for c0, cn in C2:
                            for m in range(m_n):
                                if g >= 2:
                                    pe.wait_ge(mm_kept, g - 1)
                                for k in range(k_n):
                                    last = nc.tensor.matmul(bank[:, 2 + g % 2, 0:cn], lhs[:, k, m * 128:(m + 1) * 128], rhs[:, k, c0:c0 + cn], start=(k == 0), stop=(k == k_n - 1))
                                last.then_inc(mm, 1)
                                g += 1
                    pe.wait_ge(mm_kept, g)
                    for u in range(U):
                        if u >= 2:
                            pe.wait_ge(moved, u - 1)
                        for k in range(F):
                            last = nc.tensor.matmul(bank[0:P, 4 + u % 2, 0:W2], hT[:, k, u * P:(u + 1) * P], w2s[:, k, :], start=(k == 0), stop=(k == F - 1))
                        last.then_inc(last_made, 1)

                @block.scalar
                def _(act):
                    act.wait_ge(ld, 80)
                    for u in range(U):
                        act.wait_ge(turned, u + 1)
                        nc.scalar.copy(llT[:, :, u * P:(u + 1) * P], bank[:, u % 2, 0:2 * P].rearrange("p (k n) -> p k n", k=2)).then_inc(kept, 1)
                    g = 0
                    for dst, m_n in ((upT, K), (hT, F)):
                        for c0, cn in C2:
                            for m in range(m_n):
                                act.wait_ge(mm, g + 1)
                                if dst is upT:
                                    nc.scalar.copy(dst[:, m, c0:c0 + cn], bank[:, 2 + g % 2, 0:cn]).then_inc(mm_kept, 1)
                                else:
                                    nc.scalar.activation(dst[:, m, c0:c0 + cn], bank[:, 2 + g % 2, 0:cn], ACT.Gelu, bias=b1s[:, m:m + 1]).then_inc(mm_kept, 1)
                                g += 1

                @block.vector
                def _(dve):
                    v = [0]

                    def chain(ins):
                        v[0] += 1
                        ins.then_inc(step, 1)
                        dve.wait_ge(step, v[0])

                    for u in range(U):
                        nc.vector.tensor_tensor(sums[:, u], pairs[:, u, 0], pairs[:, u, 1], ALU.add).then_inc(step, 1)
                        nc.vector.tensor_tensor(difs[:, u], pairs[:, u, 0], pairs[:, u, 1], ALU.subtract).then_inc(step, 1)
                        v[0] += 2
                        dve.wait_ge(step, v[0])
                        s2 = sums[:, u].rearrange("p (w e) -> p e w", e=2)
                        d2 = difs[:, u].rearrange("p (w e) -> p e w", e=2)
                        for i, (q, op) in enumerate(((s2, ALU.add), (d2, ALU.add), (s2, ALU.subtract), (d2, ALU.subtract))):
                            last = nc.vector.tensor_tensor(low[:, u, i], q[:, 0], q[:, 1], op)
                        chain(last)
                        nc.vector.tensor_scalar(low[:, u].rearrange("p i w -> p (i w)"), low[:, u].rearrange("p i w -> p (i w)"), 0.5, None, ALU.mult).then_inc(made, 1)
                    dve.wait_ge(ld, 80)
                    dve.wait_ge(made, U)
                    for u in range(U):
                        dve.wait_ge(last_made, u + 1)
                        nc.vector.tensor_tensor(nl[:, u % 2], bank[0:P, 4 + u % 2, 0:W2], b2s[:], ALU.add).then_inc(moved, 1)
                        dve.wait_ge(moved, u + 1)
                        nc.vector.tensor_tensor(o[:, 0], nl[:, u % 2], low[:, u, 1], ALU.add)
                        nc.vector.tensor_tensor(o[:, 1], nl[:, u % 2], low[:, u, 1], ALU.subtract)
                        nc.vector.tensor_tensor(o[:, 2], low[:, u, 2], low[:, u, 3], ALU.add)
                        chain(nc.vector.tensor_tensor(o[:, 3], low[:, u, 2], low[:, u, 3], ALU.subtract))
                        for r in range(2):
                            nc.vector.tensor_tensor(o[:, 4], o[:, r], o[:, 2 + r], ALU.add)
                            chain(nc.vector.tensor_tensor(o[:, 5], o[:, r], o[:, 2 + r], ALU.subtract))
                            for e in range(2):
                                to = xp[:, u, r].rearrange("p (w e) -> p e w", e=2)[:, e]
                                last = nc.vector.scalar_tensor_tensor(to, o[:, 4 + e], 0.5, to, ALU.mult, ALU.add)
                            chain(last)
                        dve.sem_inc(x_made, 1)

        def scale_rows(pmax):
            s = sem("scaled")
            with nc.Block() as block:
                @block.vector
                def _(dve):
                    for t in range(T):
                        nc.vector.tensor_scalar(xn[:, t], xn[:, t], pmax[:, t:t + 1], None, ALU.mult).then_inc(s, 1)
                    nc.vector.memset(y_out[:], 0.0)

        def reorder(oh):
            f = sb("f", [P, 8, T, NX], F32, c)
            pos = sb("pos", [P, T], F32, c)
            pos_i = sb("pos_i", [P, T], I32, c)
            got = sb("got", [P, T, D], F32, c)
            counted, step, ready, back, added, stored = (sem(n) for n in ("counted", "step", "pos_ready", "rows_back", "added", "stored"))
            put = dma_sem("rows_put")
            with nc.Block() as block:
                @block.tensor
                def _(pe):
                    v = oh[:].rearrange("p t e -> p (t e)")
                    nc.tensor.matmul(bank[0:P, 0, 0:T * NX], above[0:P, 0:P], v, start=True, stop=True)
                    nc.tensor.matmul(bank[0:P, 1, 0:T * NX], ones[0:P, 0:P], v, start=True, stop=True).then_inc(counted, 1)

                @block.vector
                def _(dve):
                    v = [0]

                    def chain(ins):
                        v[0] += 1
                        ins.then_inc(step, 1)
                        dve.wait_ge(step, v[0])

                    dve.wait_ge(counted, 1)
                    nc.vector.tensor_copy(f[:, 0].rearrange("p t e -> p (t e)"), bank[0:P, 0, 0:T * NX])
                    chain(nc.vector.tensor_copy(f[:, 1].rearrange("p t e -> p (t e)"), bank[0:P, 1, 0:T * NX]))
                    for e in range(NX):
                        last = nc.vector.tensor_tensor_scan(f[:, 2, :, e], ones[0:P, 0:T], f[:, 1, :, e], 0.0, ALU.mult, ALU.add)
                    chain(last)
                    chain(nc.vector.tensor_tensor_scan(f[:, 3, 0, :], ones[0:P, 0:NX], f[:, 2, T - 1, :], 0.0, ALU.mult, ALU.add))
                    chain(nc.vector.tensor_tensor(f[:, 3, 1, :], f[:, 3, 0, :], f[:, 2, T - 1, :], ALU.subtract))
                    chain(nc.vector.tensor_tensor(f[:, 4], f[:, 2], f[:, 1], ALU.subtract))
                    chain(nc.vector.tensor_tensor(f[:, 4], f[:, 4], f[:, 0], ALU.add))
                    chain(nc.vector.tensor_tensor(f[:, 4], f[:, 4], f[:, 3, 1, :].unsqueeze(1).to_broadcast([P, T, NX]), ALU.add))
                    chain(nc.vector.tensor_tensor(f[:, 4], f[:, 4], oh[:], ALU.mult))
                    chain(nc.vector.tensor_reduce(pos[:], f[:, 4], X, ALU.add))
                    nc.vector.tensor_copy(pos_i[:], pos[:]).then_inc(ready, 1)
                    for t in range(T):
                        dve.wait_ge(back, 16 * T)
                        nc.vector.tensor_tensor(x[:, t], x[:, t], got[:, t], ALU.add).then_inc(added, 1)

                @block.gpsimd
                def _(pool):
                    pool.wait_ge(ready, 1)
                    for t in range(T):
                        nc.gpsimd.indirect_dma_start(out=y_dram, out_offset=bass.IndirectOffsetOnAxis(ap=pos_i[:, t:t + 1], axis=0),
                                                     in_=y_out[:, t, :], in_offset=None).then_inc(put, 16)
                    pool.wait_ge(put, 16 * T)

                @block.sync
                def _(sp):
                    sp.wait_ge(put, 16 * T)
                    for t in range(T):
                        sp.dma_start(got[:, t], y_dram[t * P:(t + 1) * P, :]).then_inc(back, 16)
                    for t in range(T):
                        sp.wait_ge(added, t + 1)
                        sp.dma_start(out[t * P:(t + 1) * P, :], x[:, t]).then_inc(stored, 16)
                    sp.wait_ge(stored, 16 * T)

        def run(stage, *args, **kw):
            nonlocal c
            outer = c
            with ExitStack() as c:
                stage(*args, **kw)
            c = outer
            if not sems:
                return
            for s in cleared_sems:
                nc.release_semaphore(s)
            for s in sems:
                nc.gpsimd.sem_clear(s)
            cleared_sems[:] = sems
            sems.clear()

        c = None
        run(constants)
        gate = sb("gate", [P, T, NX])
        picks = sb("picks", [P, 2, T, NX])
        pmax = sb("pmax", [P, T])
        run(graph_and_convolutions)
        run(norm, x, xn)
        run(route, "L0_ffn_router_w", None, gate, "two", None, picks)
        run(experts, "L0_ffn_w1", "L0_ffn_b1", "L0_ffn_w2", "L0_ffn_b2", gate, [picks[:, 0], picks[:, 1]], ACT.Gelu, x)
        run(edge_attention)
        run(turn_and_project)
        run(norm, x, xn)
        run(attention_and_project)
        run(norm, xn, xn, "L1_ffn_g1", "L1_ffn_beta1")
        run(route, "L1_ffn_Wg", "L1_ffn_bg", gate, "one")
        run(experts, "L1_ffn_W1", "L1_ffn_b1", "L1_ffn_W2", "L1_ffn_b2", gate, [gate[:]], ACT.Gelu, xn)
        run(norm, xn, xn, "L1_ffn_g2", "L1_ffn_beta2", False, False, x)
        run(mean_layer, a["L2_gnn_W"][0:D, :], a["L2_gnn_W"][D:2 * D, :], a["L2_gnn_b"], True, x, x_dram)
        run(to_pairs)
        run(norm, x, xn, None, None, False)
        run(wavelet)
        run(from_pairs)
        run(mean_layer, a["L3_gnn_w_self"], a["L3_gnn_w_neigh"], a["L3_gnn_bias"], False, xn)
        run(norm, xn, xn, "L3_gnn_gamma", "L3_gnn_beta", False, True, x)
        run(norm, x, xn)
        run(route, "L3_ffn_Wg", "L3_ffn_bg", gate, "one", pmax)
        y_out = sb("y_out", [P, T, D])
        run(scale_rows, pmax)
        run(experts, "L3_ffn_W1", "L3_ffn_b1", "L3_ffn_W2", "L3_ffn_b2", gate, [gate[:]], ACT.Relu, y_out)
        run(reorder, gate)


def stretch_matrix():
    import numpy as np
    n, m = D // 2, D
    pos = np.linspace(0.0, 1.0, m, dtype=np.float32) * np.float32(n - 1)
    i0 = np.clip(np.floor(pos).astype(np.int32), 0, n - 2)
    w = pos - i0.astype(np.float32)
    out = np.zeros((n, m), np.float32)
    out[i0, np.arange(m)] = np.float32(1.0) - w
    out[i0 + 1, np.arange(m)] = w
    return out


def lay_out(inputs):
    import numpy as np
    arrays = {k: np.ascontiguousarray(np.asarray(v)) for k, v in inputs.items()}
    for name, axes in (("L0_ffn_router_w", (1, 0)), ("L0_ffn_w1", (0, 2, 1)), ("L0_ffn_w2", (0, 2, 1)),
                       ("L2_ffn_fc1_w", (1, 0)), ("L2_ffn_fc2_w", (1, 0)), ("L3_gnn_w_self", (1, 0)), ("L3_gnn_w_neigh", (1, 0))):
        arrays[name] = np.ascontiguousarray(arrays[name].transpose(axes))
    arrays["stretch"] = stretch_matrix()
    return arrays


def kernel(**inputs):
    import numpy as np
    import concourse.bacc as bacc
    from concourse.bass_utils import run_bass_kernel_spmd

    nc = bacc.Bacc("TRN2", target_bir_lowering=False, num_devices=1)
    arrays, views = {}, {}
    for name, array in lay_out(inputs).items():
        arrays[f"in_{name}_dram"] = array
        views[name] = nc.dram_tensor(f"in_{name}_dram", array.shape, mybir.dt.from_np(array.dtype), kind="ExternalInput").ap()
    out = nc.dram_tensor("out_0_dram", (N, D), F32, kind="ExternalOutput").ap()
    build(nc, views, out)
    result = run_bass_kernel_spmd(nc, [arrays], core_ids=[0])
    return np.asarray(result.results[0]["out_0_dram"])
```
